# Optimizing a Trainium2 kernel written in Bass

```python
import numpy as np
import jax
import jax.numpy as jnp

def _softmax(x, axis=-1):
    return jax.nn.softmax(x, axis=axis)

def _gelu(x):
    return jax.nn.gelu(x, approximate=True)

def _silu(x):
    return jax.nn.silu(x)

def _sigmoid(x):
    return jax.nn.sigmoid(x)

def _layernorm(x, axis=-1, eps=1e-05):
    m = jnp.mean(x, axis=axis, keepdims=True)
    v = jnp.var(x, axis=axis, keepdims=True)
    return (x - m) / jnp.sqrt(v + eps)

def _scatter_add(tgt, idx, src, axis=0):
    return tgt.at[idx].add(src)

def _segment_sum(src, seg, n):
    return jax.ops.segment_sum(src, seg, n)
kernel_name = 'mk_conv_attn_hybrid_d2_conv_nchw256_r2_3d7b80'

def setup_inputs(seed: int=0):
    np.random.seed(seed)
    _w = jnp.asarray

    def _rec_inputs():
        import jax
        import jax.numpy as jnp
        _gk = jax.random.key(seed)
        x = -0.0002928 + 1 * jax.random.normal(jax.random.fold_in(_gk, 1), (4, 128, 32, 32), jnp.float32)
        return x
    x = _rec_inputs()

    def _L0_conv_setup():
        import jax, jax.numpy as jnp
        import numpy as np
        NUM_GROUPS = 32
        EPS = 1e-06

        def group_norm(x, scale, bias):
            B, C, H, W = x.shape
            g = x.reshape(B, NUM_GROUPS, C // NUM_GROUPS, H, W)
            mu = g.mean(axis=(2, 3, 4), keepdims=True)
            var = g.var(axis=(2, 3, 4), keepdims=True)
            g = (g - mu) * jax.lax.rsqrt(var + EPS)
            x = g.reshape(B, C, H, W)
            return x * scale[None, :, None, None] + bias[None, :, None, None]

        def nin(x, W, b):
            return jnp.einsum('bchw,cd->bdhw', x, W) + b[None, :, None, None]
        key = jax.random.key(seed)
        ks = jax.random.split(key, 5)
        B, C, H, W = (4, 128, 32, 32)
        s = 1.0 / np.sqrt(C)
        return {'x': jax.random.normal(ks[0], (B, C, H, W), jnp.float32), 'gn_scale': jnp.ones((C,), jnp.float32), 'gn_bias': jnp.zeros((C,), jnp.float32), 'Wq': jax.random.normal(ks[1], (C, C), jnp.float32) * s, 'bq': jnp.zeros((C,), jnp.float32), 'Wk': jax.random.normal(ks[2], (C, C), jnp.float32) * s, 'bk': jnp.zeros((C,), jnp.float32), 'Wv': jax.random.normal(ks[3], (C, C), jnp.float32) * s, 'bv': jnp.zeros((C,), jnp.float32), 'Wp': jax.random.normal(ks[4], (C, C), jnp.float32) * s, 'bp': jnp.zeros((C,), jnp.float32)}
    _L0_conv_all = _L0_conv_setup()
    _L0_conv_in = {k: v for k, v in _L0_conv_all.items() if k in ('gn_scale', 'gn_bias', 'Wq', 'bq', 'Wk', 'bk', 'Wv', 'bv', 'Wp', 'bp')}
    del _L0_conv_all

    def _L1_attn_setup():
        import jax, jax.numpy as jnp
        import numpy as np
        HEADS = 4
        DIM_HEAD = 32
        key = jax.random.key(seed)
        k1, k2, k3 = jax.random.split(key, 3)
        B, L, D = (16, 4096, 128)
        hidden = HEADS * DIM_HEAD
        x = jax.random.normal(k1, (B, L, D), dtype=jnp.float32)
        W_qkv = jax.random.normal(k2, (D, 3 * hidden), dtype=jnp.float32) * D ** (-0.5)
        W_out = jax.random.normal(k3, (hidden, D), dtype=jnp.float32) * hidden ** (-0.5)
        b_out = jnp.zeros((D,), dtype=jnp.float32)
        return {'x': x, 'W_qkv': W_qkv, 'W_out': W_out, 'b_out': b_out}
    _L1_attn_all = _L1_attn_setup()
    _L1_attn_in = {k: v for k, v in _L1_attn_all.items() if k in ('W_qkv', 'W_out', 'b_out')}
    del _L1_attn_all

    def _L1_ffn_setup():
        import jax, jax.numpy as jnp
        import numpy as np
        NUM_EXPERTS = 8
        TOP_K = 2
        B, S, D = (8, 4096, 128)

        def _moe(tokens, router_w, w1, b1, w2, b2):
            N = tokens.shape[0]
            E = router_w.shape[0]
            logits = tokens.astype(jnp.float32) @ router_w.astype(jnp.float32).T
            probs = jax.nn.softmax(logits, axis=-1)
            rw, re = jax.lax.top_k(probs, TOP_K)
            if TOP_K > 1:
                rw = rw / jnp.maximum(rw.sum(-1, keepdims=True), 1e-12)
            rw = rw.astype(tokens.dtype)
            combine = jnp.zeros((N, E), tokens.dtype).at[jnp.arange(N)[:, None], re].set(rw)
            out = tokens
            for e in range(E):
                h = jax.nn.gelu(tokens @ w1[e] + b1[e], approximate=False)
                y = h @ w2[e] + b2[e]
                out = out + combine[:, e:e + 1] * y
            return out
        key = jax.random.key(seed)
        ks = jax.random.split(key, 4)
        scale = 1.0 / np.sqrt(D).astype(np.float32)
        return {'input_embeddings': jax.random.normal(ks[0], (B, S, D), jnp.float32), 'router_w': jax.random.normal(ks[1], (NUM_EXPERTS, D), jnp.float32) * scale, 'w1': jax.random.normal(ks[2], (NUM_EXPERTS, D, D), jnp.float32) * scale, 'b1': jnp.zeros((NUM_EXPERTS, D), jnp.float32), 'w2': jax.random.normal(ks[3], (NUM_EXPERTS, D, D), jnp.float32) * scale, 'b2': jnp.zeros((NUM_EXPERTS, D), jnp.float32)}
    _L1_ffn_all = _L1_ffn_setup()
    _L1_ffn_in = {k: v for k, v in _L1_ffn_all.items() if k in ('router_w', 'w1', 'b1', 'w2', 'b2')}
    del _L1_ffn_all
    return {'x': x, 'L0_conv_gn_scale': _L0_conv_in['gn_scale'], 'L0_conv_gn_bias': _L0_conv_in['gn_bias'], 'L0_conv_Wq': _L0_conv_in['Wq'], 'L0_conv_bq': _L0_conv_in['bq'], 'L0_conv_Wk': _L0_conv_in['Wk'], 'L0_conv_bk': _L0_conv_in['bk'], 'L0_conv_Wv': _L0_conv_in['Wv'], 'L0_conv_bv': _L0_conv_in['bv'], 'L0_conv_Wp': _L0_conv_in['Wp'], 'L0_conv_bp': _L0_conv_in['bp'], 'L1_attn_W_qkv': _L1_attn_in['W_qkv'], 'L1_attn_W_out': _L1_attn_in['W_out'], 'L1_attn_b_out': _L1_attn_in['b_out'], 'L1_ffn_router_w': _L1_ffn_in['router_w'], 'L1_ffn_w1': _L1_ffn_in['w1'], 'L1_ffn_b1': _L1_ffn_in['b1'], 'L1_ffn_w2': _L1_ffn_in['w2'], 'L1_ffn_b2': _L1_ffn_in['b2']}

def reference(x, L0_conv_gn_scale, L0_conv_gn_bias, L0_conv_Wq, L0_conv_bq, L0_conv_Wk, L0_conv_bk, L0_conv_Wv, L0_conv_bv, L0_conv_Wp, L0_conv_bp, L1_attn_W_qkv, L1_attn_W_out, L1_attn_b_out, L1_ffn_router_w, L1_ffn_w1, L1_ffn_b1, L1_ffn_w2, L1_ffn_b2):
    import jax
    import jax.numpy as jnp

    def _L0_conv_ref(x, gn_scale, gn_bias, Wq, bq, Wk, bk, Wv, bv, Wp, bp):
        import jax, jax.numpy as jnp
        import numpy as np
        NUM_GROUPS = 32
        EPS = 1e-06

        def group_norm(x, scale, bias):
            B, C, H, W = x.shape
            g = x.reshape(B, NUM_GROUPS, C // NUM_GROUPS, H, W)
            mu = g.mean(axis=(2, 3, 4), keepdims=True)
            var = g.var(axis=(2, 3, 4), keepdims=True)
            g = (g - mu) * jax.lax.rsqrt(var + EPS)
            x = g.reshape(B, C, H, W)
            return x * scale[None, :, None, None] + bias[None, :, None, None]

        def nin(x, W, b):
            return jnp.einsum('bchw,cd->bdhw', x, W) + b[None, :, None, None]
        B, C, H, W = x.shape
        h = group_norm(x, gn_scale, gn_bias)
        q = nin(h, Wq, bq)
        k = nin(h, Wk, bk)
        v = nin(h, Wv, bv)
        w = jnp.einsum('bchw,bcHW->bhwHW', q, k) * C ** (-0.5)
        w = jax.nn.softmax(w.reshape(B, H, W, H * W), axis=-1).reshape(B, H, W, H, W)
        h = jnp.einsum('bhwHW,bcHW->bchw', w, v)
        h = nin(h, Wp, bp)
        return x + h

    def _L1_attn_ref(x, W_qkv, W_out, b_out):
        import jax, jax.numpy as jnp
        import numpy as np
        HEADS = 4
        DIM_HEAD = 32
        B, L, D = x.shape
        scale = DIM_HEAD ** (-0.5)
        qkv = jnp.einsum('bld,df->blf', x, W_qkv)
        qkv = qkv.reshape(B, L, 3, HEADS, DIM_HEAD)
        q = jnp.transpose(qkv[:, :, 0], (0, 2, 1, 3)) * scale
        k = jax.nn.softmax(jnp.transpose(qkv[:, :, 1], (0, 2, 1, 3)), axis=2)
        v = jnp.transpose(qkv[:, :, 2], (0, 2, 1, 3))
        context = jnp.einsum('bhld,bhle->bhde', k, v)
        out = jnp.einsum('bhde,bhld->bhle', context, q)
        out = jnp.transpose(out, (0, 2, 1, 3)).reshape(B, L, HEADS * DIM_HEAD)
        return jnp.einsum('blf,fd->bld', out, W_out) + b_out

    def _L1_ffn_ref(input_embeddings, router_w, w1, b1, w2, b2):
        import jax, jax.numpy as jnp
        import numpy as np
        NUM_EXPERTS = 8
        TOP_K = 2
        B, S, D = (8, 4096, 128)

        def _moe(tokens, router_w, w1, b1, w2, b2):
            N = tokens.shape[0]
            E = router_w.shape[0]
            logits = tokens.astype(jnp.float32) @ router_w.astype(jnp.float32).T
            probs = jax.nn.softmax(logits, axis=-1)
            rw, re = jax.lax.top_k(probs, TOP_K)
            if TOP_K > 1:
                rw = rw / jnp.maximum(rw.sum(-1, keepdims=True), 1e-12)
            rw = rw.astype(tokens.dtype)
            combine = jnp.zeros((N, E), tokens.dtype).at[jnp.arange(N)[:, None], re].set(rw)
            out = tokens
            for e in range(E):
                h = jax.nn.gelu(tokens @ w1[e] + b1[e], approximate=False)
                y = h @ w2[e] + b2[e]
                out = out + combine[:, e:e + 1] * y
            return out
        b, s, d = input_embeddings.shape
        tokens = input_embeddings.reshape(b * s, d)
        return _moe(tokens, router_w, w1, b1, w2, b2).reshape(b, s, d)

    def _gn(v, G=32, eps=1e-05):
        B_, C_, H_, W_ = v.shape
        g = v.reshape(B_, G, C_ // G, H_, W_)
        m = jnp.mean(g, axis=(2, 3, 4), keepdims=True)
        s = jnp.var(g, axis=(2, 3, 4), keepdims=True)
        return ((g - m) / jnp.sqrt(s + eps)).reshape(v.shape)

    def _ln_c(v, eps=1e-06):
        m = jnp.mean(v, axis=1, keepdims=True)
        s = jnp.var(v, axis=1, keepdims=True)
        return (v - m) / jnp.sqrt(s + eps)

    def _ln_t(v, eps=1e-05):
        m = jnp.mean(v, axis=-1, keepdims=True)
        s = jnp.var(v, axis=-1, keepdims=True)
        return (v - m) / jnp.sqrt(s + eps)

    def _to_tokens(v):
        B_, C_, H_, W_ = v.shape
        return v.reshape(B_, C_, H_ * W_).transpose(0, 2, 1)

    def _from_tokens(t, like):
        B_, C_, H_, W_ = like.shape
        return t.transpose(0, 2, 1).reshape(B_, C_, H_, W_)
    x = _L0_conv_ref(x, L0_conv_gn_scale, L0_conv_gn_bias, L0_conv_Wq, L0_conv_bq, L0_conv_Wk, L0_conv_bk, L0_conv_Wv, L0_conv_bv, L0_conv_Wp, L0_conv_bp)
    t = _to_tokens(x)
    t = t + _L1_attn_ref(_ln_t(t), L1_attn_W_qkv, L1_attn_W_out, L1_attn_b_out)
    t = t + _L1_ffn_ref(_ln_t(t), L1_ffn_router_w, L1_ffn_w1, L1_ffn_b1, L1_ffn_w2, L1_ffn_b2)
    x = _from_tokens(t, x)
    return x

_drawn_inputs = setup_inputs


def setup_inputs(seed=0):
    import zlib

    import numpy as np

    out = dict(_drawn_inputs(seed))
    spreads = {'L0_conv_gn_scale': (1.0, 0.2),
     'L0_conv_gn_bias': (0.0, 0.1),
     'L0_conv_bq': (0.0, 0.354),
     'L0_conv_bk': (0.0, 0.8),
     'L0_conv_bv': (0.0, 0.1),
     'L0_conv_bp': (0.0, 0.1),
     'L1_attn_b_out': (0.0, 0.1),
     'L1_ffn_b1': (0.0, 0.324),
     'L1_ffn_b2': (0.0, 0.1)}
    factors = {}
    for name, (base, spread) in spreads.items():
        noise = np.random.default_rng([zlib.crc32(name.encode()), seed]).standard_normal(out[name].shape)
        drawn = base * np.exp(spread * noise) if base else spread * noise
        out[name] = jnp.asarray(drawn.astype(out[name].dtype))
    for name, factor in factors.items():
        out[name] = (out[name] * factor).astype(out[name].dtype)
    return out
```

```python
from contextlib import ExitStack

import concourse.bass as bass
from concourse import mybir

FP32 = mybir.dt.float32
FP32R = mybir.dt.float32r
ALU = mybir.AluOpType
ACT = mybir.ActivationFunctionType
AX = mybir.AxisListType

B, C, T = 4, 128, 1024
GROUP = C // 32
HEADS, HEAD = 4, 32
E = 8
P = 128
BANK = 512
TILES = T // P
QUAD = BANK // P
HALVES = T // BANK
SCALE = float(C) ** -0.5
GN_EPS, LN_EPS = 1e-6, 1e-5

SETUP_UNITS = ["gn_mean", "gn_var", "wvT", "wpv", "bias_o"]
ATTENTION = dict(
    qk=["q0", "q1", "k0", "k1"], v=["v0", "v1"], xT=["xT0", "xT1"],
    T=[[f"T{i}a", f"T{i}b"] for i in range(TILES)],
)
FIRST_UNITS = (
    ATTENTION["qk"] + ["gn_mean", "gn_var"] + ATTENTION["v"]
    + ["l1qT", "routerT", "b1T"] + ATTENTION["T"][0]
    + ATTENTION["T"][1] + ATTENTION["xT"] + ATTENTION["T"][2] + ATTENTION["T"][3]
    + ["PV0"] + ATTENTION["T"][4] + ATTENTION["T"][5] + ["OT0"] + ATTENTION["T"][6]
)
LOOP_UNITS = (
    ATTENTION["T"][7] + ["PV1"] + ATTENTION["qk"] + ["OT1"] + ATTENTION["v"]
    + ATTENTION["T"][0] + ATTENTION["T"][1] + ATTENTION["xT"] + ["u0", "u1"]
    + ATTENTION["T"][2] + ["kT0", "kT1"] + ["p0", "p1"] + ATTENTION["T"][3] + ["g"]
    + ["ctx", "PV0", "m2", "m3"] + ATTENTION["T"][4] + ["o0", "o1"]
    + ATTENTION["T"][5] + ["OT0"]
    + ["w0", "w1", "lg0", "lg1"] + ATTENTION["T"][6] + ["lT", "z0", "z1", "c0", "c1"]
)
TAIL_UNITS = (
    ATTENTION["T"][7] + ["PV1", "OT1", "u0", "u1", "kT0", "kT1", "p0", "p1", "g", "ctx", "m2",
                         "m3", "o0", "o1", "w0", "w1", "lg0", "lg1", "lT", "z0", "z1", "c0", "c1"]
)
TAIL_AT = dict(OT=0, u=2, kT=3, p=4, g=5, ctx=6, m2=7, m3=8, o=9, w=11, lT=12, z=13, c=14)
CHAIN = 25


class Place:

    def __init__(self, banks, before):
        self.banks, self.before = banks, before

    def bank(self, unit):
        return self.banks[unit][0]

    def earlier(self, unit):
        bank, n = self.banks[unit]
        return self.before[bank] + n


def banks_of(units, banks):
    count, found = [0] * 4, {}
    for n, unit in enumerate(units):
        bank = banks[n % len(banks)]
        found[unit] = (bank, count[bank])
        count[bank] += 1
    return found, count


def conv_attention_moe(nc, x, gn_scale, gn_bias, wq, bq, wk, bk, wv, bv, wp, bp,
                       w_qkv, w_out, b_out, router, w1, b1, w2, b2, out):
    setup_at, setup_n = banks_of(SETUP_UNITS, range(4))
    first_at, first_n = banks_of(FIRST_UNITS, range(4))
    loop_at, loop_n = banks_of(LOOP_UNITS, range(4))
    tail_at, tail_n = banks_of(TAIL_UNITS, range(2))
    SETUP = Place(setup_at, [0] * 4)
    FIRST = Place(first_at, setup_n)

    def loop_place(b):
        return Place(loop_at, [s + f + (b - 1) * n for s, f, n in zip(setup_n, first_n, loop_n)])

    TAIL = Place(tail_at, [s + f + (B - 1) * n for s, f, n in zip(setup_n, first_n, loop_n)])

    def y_place(m):
        return Place({"y0": (2, 0), "y1": (3, 0)}, [TAIL.before[k] + m for k in range(4)])

    scratch_z = nc.dram_tensor("scratch_z", (B * HALVES, C, BANK), FP32).ap()
    scratch_c = nc.dram_tensor("scratch_c", (B * HALVES, 2 * E, BANK), FP32).ap()
    x_v = x.rearrange("b c h w -> b c (h w)")
    out_v = out.rearrange("b c h w -> b c (h w)")

    ctx = ExitStack()
    with ctx:
        def sb(name, shape, dt=FP32):
            return ctx.enter_context(nc.sbuf_tensor(name, shape, dt))

        def sem(name):
            return ctx.enter_context(nc.semaphore(name))

        ident = sb("ident", [P, P])
        group_mean = sb("group_mean", [C, C])
        head_mask = sb("head_mask", [C, C])
        minus_half = sb("minus_half", [P, TILES])
        falling = sb("falling", [P, E])
        wout_s = sb("wout_s", [C, C])
        wqkv_s = sb("wqkv_s", [C, 3 * C])
        l1qT = sb("l1qT", [C, C])
        wq_hi, wq_lo, wk_hi, wk_lo, wpv_hi, wpv_lo, l1k_hi, l1k_lo, rt_hi, rt_lo = (
            sb(n, [C, C], FP32R) for n in ("wq_hi", "wq_lo", "wk_hi", "wk_lo", "wpv_hi", "wpv_lo",
                                           "l1k_hi", "l1k_lo", "rt_hi", "rt_lo"))
        bout_row = sb("bout_row", [P, C])
        cols = sb("cols", [C, 8])
        bq_c, bk_c, bv_c, bp_c, gs_c, gb_c, bias_o = (cols[:, i:i + 1] for i in range(7))
        b1_c = sb("b1_c", [C, E])
        b2_s = sb("b2_s", [2 * E, C])
        b2_hi, b2_lo = sb("b2_hi", [2 * E, C], FP32R), sb("b2_lo", [2 * E, C], FP32R)
        pick = sb("pick", [2 * E, E, P], FP32R)
        w1_hi, w1_lo, w2_hi, w2_lo = (sb(n, [C, E * C], FP32R) for n in
                                      ("w1_hi", "w1_lo", "w2_hi", "w2_lo"))
        x_s = sb("x_s", [C, B, T])
        h_f = sb("h_f", [C, T])
        h_hi, h_lo = sb("h_hi", [C, T], FP32R), sb("h_lo", [C, T], FP32R)
        xb = sb("xb", [C, T])
        q_hi, q_lo, k_hi, k_lo = (sb(n, [C, T], FP32R) for n in ("q_hi", "q_lo", "k_hi", "k_lo"))
        v_hi, v_lo = sb("v_hi", [P, TILES * C], FP32R), sb("v_lo", [P, TILES * C], FP32R)
        prob = sb("prob", [P, 2, T])
        pT_hi = sb("pT_hi", [P, TILES, BANK], FP32R)
        pT_lo = sb("pT_lo", [P, TILES, BANK], FP32R)
        o_s = sb("o_s", [C, BANK])
        xT = sb("xT", [P, TILES, C])
        t1 = sb("t1", [P, TILES, C])
        t2 = sb("t2", [P, TILES, C])
        u = sb("u", [P, TILES, C])
        uT_hi, uT_lo = sb("uT_hi", [C, T], FP32R), sb("uT_lo", [C, T], FP32R)
        p1 = sb("p1", [C, T])
        p1T = sb("p1T", [P, TILES, C])
        w_n = sb("w_n", [P, TILES, C])
        gT_s, ctx_s, m2T_s = (sb(n, [C, C]) for n in ("gT_s", "ctx_s", "m2T_s"))
        m3_hi, m3_lo = sb("m3_hi", [C, C], FP32R), sb("m3_lo", [C, C], FP32R)
        wT_hi, wT_lo = sb("wT_hi", [C, B * T], FP32R), sb("wT_lo", [C, B * T], FP32R)
        gst = sb("gst", [C, B, HALVES, 6])
        gmv = sb("gmv", [C, B, 2])
        gsum = sb("gsum", [C, 4, B])
        gmul, gadd = sb("gmul", [C, B]), sb("gadd", [C, B])
        affine = sb("affine", [C, 2])
        mx = sb("mx", [P, 2, TILES])
        psum_row = sb("psum_row", [P, 2, TILES])
        lst = sb("lst", [P, TILES, 6])
        lmv = sb("lmv", [P, TILES, 2])
        rstd = sb("rstd", [P, 2, TILES])
        kst = sb("kst", [C, 8])
        lg = sb("lg", [P, TILES, E])
        rt = sb("rt", [P, 6, TILES, E])
        rr = sb("rr", [P, 8, TILES])
        comb = sb("comb", [P, TILES, 2 * E])
        cb_in = sb("cb_in", [2 * E, HALVES, BANK], FP32R)
        wq_raw, wk_raw, wq_sc = (p1T[:, i, :] for i in range(3))
        rows8 = p1T[0:E, 3:5, :]
        wv_s, wp_s, wvT = gT_s, ctx_s, m2T_s
        w1_raw, w2_raw = t1[:, :, :].rearrange("p a b -> p (a b)"), u[:, :, :].rearrange("p a b -> p (a b)")
        pick_raw = w_n[0:2 * E, :, :].rearrange("p a b -> p (a b)")
        zT = u[:, :, :].rearrange("p a b -> p (a b)")
        lgT = p1[0:E, :]
        cT = p1T[0:2 * E, :, :].rearrange("p a b -> p (a b)")
        gel, hs, out_s, z_in = (x_s[:, i, :] for i in range(4))
        hs_hi, hs_lo = h_hi, h_lo

        scores = ctx.enter_context(nc.psum_tensor("scores", [P, 4, BANK], FP32))
        ring = ctx.enter_context(nc.psum_tensor("ring", [P, 4, BANK], FP32))

        filled = [sem(f"filled{k}") for k in range(4)]
        drained = [sem(f"drained{k}") for k in range(4)]
        ld_x = [sem(f"ld_x{b}") for b in range(B)]
        ld_w = {n: sem(f"ld_{n}") for n in ("wq", "wk", "wv", "wp", "cols", "qkv", "wout", "bout",
                                            "rows8", "b2", "w1", "w2")}
        const_made = sem("const_made")
        mask_made = sem("mask_made")
        experts_split = sem("experts_split")
        setup_made = sem("setup_made")
        pool_chain = sem("pool_chain")
        dve_chain = sem("dve_chain")
        gn_mv = sem("gn_mv")
        gn_rstd = sem("gn_rstd")
        gn_made = sem("gn_made")
        h_made, xb_made = sem("h_made"), sem("xb_made")
        h_hi_made, h_lo_made = sem("h_hi_made"), sem("h_lo_made")
        x_copied = sem("x_copied")
        passed_dve, passed_pe, passed_pool, passed_sp = (
            sem(f"passed_{e}") for e in ("dve", "pe", "pool", "sp"))
        xb_read = sem("xb_read")
        s_made, s_max, s_exp = sem("s_made"), sem("s_max"), sem("s_exp")
        qk_hi_made, v_hi_made, p_hi_made = sem("qk_hi_made"), sem("v_hi_made"), sem("p_hi_made")
        u_hi_made, m3_hi_made, w_hi_made = sem("u_hi_made"), sem("m3_hi_made"), sem("w_hi_made")
        r_made = sem("r_made")
        chain = sem("chain")
        ln_stats, ln_rstd, eps_added = sem("ln_stats"), sem("ln_rstd"), sem("eps_added")
        u_made, w_made, z_made, t1b_made = sem("u_made"), sem("w_made"), sem("z_made"), sem("t1b_made")
        k_max, r_exp, c_made = sem("k_max"), sem("r_exp"), sem("c_made")
        z_stored, c_stored = sem("z_stored"), sem("c_stored")
        z_loaded = [sem(f"z_loaded{h}") for h in range(HALVES)]
        c_loaded = [sem(f"c_loaded{h}") for h in range(HALVES)]
        e_h, e_gelu, e_mul, e_hi, e_lo, e_y = (sem(n) for n in
                                               ("e_h", "e_gelu", "e_mul", "e_hi", "e_lo", "e_y"))
        stored = [sem(f"stored{h}") for h in range(HALVES)]

        row_max, row_sum = mx[:, 0, :], psum_row
        bqs_c = cols[:, 7:8]
        block = ctx.enter_context(nc.Block())
        passed = {}

        def first_batch(m):
            return isinstance(m, int) and m == 0

        def as_tiles(m):
            return m.rearrange("p (j t) -> p j t", j=QUAD)

        def tile_group(m, n, i):
            return m[:, n * QUAD:(n + 1) * QUAD, (i % QUAD) * P:(i % QUAD + 1) * P]

        def ps(place, unit):
            return ring[:, place.bank(unit), :]

        def wait_filled(eng, place, unit):
            eng.wait_ge(filled[place.bank(unit)], place.earlier(unit) + 1)

        def wait_drained(eng, place, unit):
            eng.wait_ge(drained[place.bank(unit)], place.earlier(unit) + 1)

        def apart(eng):
            eng.sem_inc(passed[eng], 1)

        def tile(m, j):
            return m[:, j * P:(j + 1) * P]

        def half(m, n):
            return m[:, n * BANK:(n + 1) * BANK]

        @block.sync
        def _(sp):
            passed[sp] = passed_sp
            sp.dma_start(x_s[:, 0, :], x_v[0]).then_inc(ld_x[0], 16)
            sp.dma_start(wp_s[:, :], wp).then_inc(ld_w["wp"], 16)
            sp.dma_start(rows8[:, 0, :], router).then_inc(ld_w["rows8"], 16)
            sp.dma_start(rows8[:, 1, :], b1).then_inc(ld_w["rows8"], 16)
            for n in range(2):
                sp.dma_start(b2_s[n * E:(n + 1) * E, :], b2).then_inc(ld_w["b2"], 16)
            for b in range(1, B):
                sp.dma_start(x_s[:, b, :], x_v[b]).then_inc(ld_x[b], 16)
            sp.dma_start(w1_raw.rearrange("p (e f) -> p e f", e=E),
                         w1.rearrange("e c f -> c e f")).then_inc(ld_w["w1"], 16)
            sp.dma_start(w2_raw.rearrange("p (e f) -> p e f", e=E),
                         w2.rearrange("e c f -> c e f")).then_inc(ld_w["w2"], 16)

            def store_routed(place, lb):
                for unit in ("z0", "z1"):
                    wait_drained(sp, place, unit)
                    apart(sp)
                sp.dma_start(scratch_z[bass.ds(lb * HALVES, HALVES)].rearrange("h c t -> c h t"),
                             zT.rearrange("c (h t) -> c h t", h=HALVES)).then_inc(z_stored, 16)
                for unit in ("c0", "c1"):
                    wait_drained(sp, place, unit)
                    apart(sp)
                sp.dma_start(scratch_c[bass.ds(lb * HALVES, HALVES)].rearrange("h c t -> c h t"),
                             cT.rearrange("c (h t) -> c h t", h=HALVES)).then_inc(c_stored, 16)

            def load_routed(m, h):
                sp.wait_ge(z_stored, 16 * (m + 2))
                apart(sp)
                sp.wait_ge(c_stored, 16 * (m + 2))
                apart(sp)
                sp.dma_start(half(z_in, h), scratch_z[m * HALVES + h]).then_inc(z_loaded[h], 16)
                sp.dma_start(cb_in[:, h, :].bitcast(FP32), scratch_c[m * HALVES + h]).then_inc(c_loaded[h], 16)

            sp.sem_inc(z_stored, 16)
            sp.sem_inc(c_stored, 16)
            with sp.Fori(1, B) as b:
                store_routed(loop_place(b), b - 1)
            sp.wait_ge(xb_made, B)
            for h in range(HALVES):
                load_routed(0, h)
            def result(m, h, more):
                wait_drained(sp, y_place(m), f"y{h}")
                apart(sp)
                sp.dma_start(out_v[m, :, h * BANK:(h + 1) * BANK], half(out_s, h)).then_inc(stored[h], 16)
                if more:
                    load_routed(m + 1, h)

            result(0, 0, True)
            store_routed(TAIL, B - 1)
            result(0, 1, True)
            with sp.Fori(1, B - 1) as m:
                for h in range(HALVES):
                    result(m, h, True)
            for h in range(HALVES):
                result(B - 1, h, False)
            for h in range(HALVES):
                sp.wait_ge(stored[h], 16 * B)

        @block.gpsimd
        def _(pool):
            passed[pool] = passed_pool
            made = [0]

            def after(ins):
                made[0] += 1
                ins.then_inc(pool_chain, 1)
                pool.wait_ge(pool_chain, made[0])

            bout_b = bout_row[:, :].unsqueeze(1).to_broadcast([P, TILES, C])
            pool.dma_start(wqkv_s[:, :], w_qkv).then_inc(ld_w["qkv"], 16)
            pool.dma_start(wout_s[:, :], w_out).then_inc(ld_w["wout"], 16)
            pool.dma_start(bout_row[:, :], b_out.rearrange("(a c) -> a c", a=1).to_broadcast([P, C])
                           ).then_inc(ld_w["bout"], 16)
            pool.memset(group_mean[:, :], 1.0 / GROUP)
            pool.memset(minus_half[:, :], -0.5)
            after(pool.memset(ident[:, :], 0.0))
            after(pool.affine_select(out=ident[:, :], in_=ident[:, :], compare_op=ALU.not_equal, fill=1.0,
                                     base=0, pattern=[[-1, P]], channel_multiplier=1))
            g_v = group_mean[:, :].rearrange("p (g c) -> p g c", c=GROUP)
            after(pool.affine_select(out=g_v, in_=g_v, compare_op=ALU.is_ge, fill=0.0, base=0,
                                     pattern=[[-GROUP, C // GROUP], [0, GROUP]], channel_multiplier=1))
            pool.affine_select(out=g_v, in_=g_v, compare_op=ALU.is_ge, fill=0.0, base=GROUP - 1,
                               pattern=[[GROUP, C // GROUP], [0, GROUP]],
                               channel_multiplier=-1).then_inc(const_made, 1)

            def group_rstd(place, b0, nb):
                wait_drained(pool, place, "gn_var")
                after(pool.tensor_scalar(gsum[:, 3, b0:b0 + nb], gsum[:, 2, b0:b0 + nb],
                                         1.0, GN_EPS, ALU.mult, ALU.add))
                pool.tensor_tensor(gsum[:, 3, b0:b0 + nb], gsum[:, 3, b0:b0 + nb],
                                   minus_half[:, 0:nb], ALU.pow).then_inc(gn_rstd, 1)

            def norm_x(b):
                pool.tensor_copy(affine[:, 0:1], gmul[:, bass.ds(b, 1)])
                pool.tensor_copy(affine[:, 1:2], gadd[:, bass.ds(b, 1)])
                pool.tensor_copy(xb[:, :], x_s[:, bass.ds(b, 1), :].rearrange("p a t -> p (a t)")
                                 ).then_inc(x_copied, 1)
                pool.wait_ge(x_copied, b + 1)
                apart(pool)
                pool.tensor_scalar(h_f[:, :], xb[:, :], affine[:, 0:1], affine[:, 1:2],
                                   ALU.mult, ALU.add).then_inc(h_made, 1)

            def add_bias(b):
                pool.tensor_scalar(xb[:, :], xb[:, :], 1.0, bias_o, ALU.mult, ALU.add).then_inc(xb_made, 1)

            def token_rstd(n):
                pool.wait_ge(ln_stats, n + 1)
                apart(pool)
                pool.tensor_scalar(rstd[:, 0, :], lmv[:, :, 1], 1.0, LN_EPS, ALU.mult, ALU.add
                                   ).then_inc(eps_added, 1)
                pool.wait_ge(eps_added, n + 1)
                pool.tensor_tensor(rstd[:, 1, :], rstd[:, 0, :], minus_half[:, :], ALU.pow
                                   ).then_inc(ln_rstd, 1)

            def linear(lb):
                token_rstd(2 * lb)
                pool.wait_ge(u_made, lb + 1)
                pool.tensor_tensor(t2[:, :, :], t1[:, :, :], bout_b, ALU.add).then_inc(t1b_made, 1)
                token_rstd(2 * lb + 1)
                pool.wait_ge(w_made, lb + 1)
                pool.tensor_tensor(t2[:, :, :], t2[:, :, :], w_n[:, :, :], ALU.add).then_inc(z_made, 1)

            group_rstd(SETUP, 0, 1)
            pool.wait_ge(gn_made, 1)
            norm_x(0)
            after(pool.memset(head_mask[:, :], float(HEAD) ** -0.5))
            m_v = head_mask[:, :].rearrange("p (g c) -> p g c", c=HEAD)
            after(pool.affine_select(out=m_v, in_=m_v, compare_op=ALU.is_ge, fill=0.0, base=0,
                                     pattern=[[-HEAD, HEADS], [0, HEAD]], channel_multiplier=1))
            after(pool.affine_select(out=m_v, in_=m_v, compare_op=ALU.is_ge, fill=0.0, base=HEAD - 1,
                                     pattern=[[HEAD, HEADS], [0, HEAD]], channel_multiplier=-1))
            for e in range(E):
                pool.memset(falling[:, e:e + 1], float(E - e))
            p_v = pick_raw.rearrange("p (e t) -> p e t", e=E)
            after(pool.memset(pick_raw, 0.0))
            for base in (0, -E):
                after(pool.affine_select(out=p_v, in_=p_v, compare_op=ALU.not_equal, fill=1.0, base=base,
                                         pattern=[[-1, E], [0, P]], channel_multiplier=1))
            pool.tensor_copy(pick[:, :, :], p_v).then_inc(mask_made, 1)
            wait_drained(pool, SETUP, "bias_o")
            pool.wait_ge(ld_x[0], 16)
            add_bias(0)
            group_rstd(FIRST, 1, B - 1)
            pool.wait_ge(gn_made, 2)
            for n, (name, raw, hi, lo) in enumerate((("w1", w1_raw, w1_hi, w1_lo),
                                                    ("w2", w2_raw, w2_hi, w2_lo),
                                                    ("b2", b2_s[:, :], b2_hi, b2_lo))):
                pool.wait_ge(ld_w[name], 32 if name == "b2" else 16)
                after(pool.tensor_copy(hi[:, :], raw))
                pool.tensor_tensor(lo[:, :], raw, hi[:, :].bitcast(FP32), ALU.subtract
                                   ).then_inc(experts_split, 1)
            pool.wait_ge(ld_w["bout"], 16)
            with pool.Fori(1, B) as b:
                pool.wait_ge(h_hi_made, b * HALVES)
                pool.wait_ge(h_lo_made, b * HALVES)
                pool.wait_ge(xb_read, b)
                norm_x(b)
                add_bias(b)
                linear(b - 1)
            linear(B - 1)

        @block.scalar
        def _(act):
            act.dma_start(wq_raw, wq).then_inc(ld_w["wq"], 16)
            for i, v in enumerate((bq, bk, bv, bp, gn_scale, gn_bias)):
                act.dma_start(cols[:, i:i + 1], v.rearrange("(c a) -> c a", a=1)).then_inc(ld_w["cols"], 16)
            act.dma_start(wk_raw, wk).then_inc(ld_w["wk"], 16)
            act.dma_start(wv_s[:, :], wv).then_inc(ld_w["wv"], 16)

            def split_h(b):
                act.wait_ge(h_made, b + 1)
                for n in range(HALVES):
                    act.activation(half(h_hi, n), half(h_f, n), ACT.Copy).then_inc(h_hi_made, 1)

            def project_qk(place):
                for unit, hi, bias, n in (("q0", q_hi, bqs_c, 0), ("q1", q_hi, bqs_c, 1),
                                          ("k0", k_hi, bk_c, 0), ("k1", k_hi, bk_c, 1)):
                    wait_filled(act, place, unit)
                    act.activation(half(hi, n), ps(place, unit), ACT.Identity, bias=bias).then_inc(qk_hi_made, 1)

            def project_v(place):
                for n in range(HALVES):
                    wait_filled(act, place, f"v{n}")
                    act.activation(half(v_hi, n), ps(place, f"v{n}"), ACT.Copy).then_inc(v_hi_made, 1)

            def softmax(b, i):
                act.wait_ge(s_max, b * TILES + i + 1)
                act.activation(prob[:, i % 2, :], scores[:, 2 * (i % 2):2 * (i % 2) + 2, :].rearrange("p a t -> p (a t)"),
                               ACT.Exp, bias=row_max[:, i:i + 1], accum_out=row_sum[:, 0, i:i + 1]).then_inc(s_exp, 1)

            def turn_probs(place, i):
                for n, unit in enumerate((f"T{i}a", f"T{i}b")):
                    wait_filled(act, place, unit)
                    act.activation(tile_group(pT_hi, n, i), as_tiles(ps(place, unit)), ACT.Copy).then_inc(p_hi_made, 1)

            def take_o(place, g):
                wait_filled(act, place, f"PV{g}")
                act.activation(o_s[:, :], ps(place, f"PV{g}"), ACT.Copy).then_inc(drained[place.bank(f"PV{g}")], 1)

            def turn_x(place):
                for n in range(HALVES):
                    unit = f"xT{n}"
                    wait_filled(act, place, unit)
                    act.activation(xT[:, n * QUAD:(n + 1) * QUAD, :], as_tiles(ps(place, unit)), ACT.Copy
                                   ).then_inc(drained[place.bank(unit)], 1)

            def turn_normed(place, kind, hi, made):
                for n in range(HALVES):
                    wait_filled(act, place, f"{kind}{n}")
                    act.activation(hi[n], ps(place, f"{kind}{n}"), ACT.Copy).then_inc(made, 1)

            def key_softmax(place, lb):
                act.wait_ge(k_max, lb + 1)
                for n in range(HALVES):
                    act.activation(half(p1, n), ps(place, f"kT{n}"), ACT.Exp, bias=kst[:, 2:3],
                                   accum_out=kst[:, 4 + n:5 + n]).then_inc(drained[place.bank(f"kT{n}")], 1)

            def turn_keys(place, lb):
                act.wait_ge(c_stored, lb * 16 + 16)
                for n in range(HALVES):
                    unit = f"p{n}"
                    wait_filled(act, place, unit)
                    act.activation(p1T[:, n * QUAD:(n + 1) * QUAD, :], as_tiles(ps(place, unit)), ACT.Copy
                                   ).then_inc(drained[place.bank(unit)], 1)

            def take_m3(place):
                wait_filled(act, place, "m3")
                act.activation(m3_hi[:, :], tile(ps(place, "m3"), 0), ACT.Copy).then_inc(m3_hi_made, 1)

            def take_logits(place):
                for n in range(HALVES):
                    unit = f"lg{n}"
                    wait_filled(act, place, unit)
                    act.activation(half(lgT, n), ps(place, unit)[0:E, :], ACT.Copy
                                   ).then_inc(drained[place.bank(unit)], 1)

            def route_exp(place, lb):
                wait_drained(act, place, "lT")
                act.activation(rt[:, 1, :, :], rt[:, 0, :, :], ACT.Exp).then_inc(r_exp, 1)

            def turn_z(place):
                for n in range(HALVES):
                    unit = f"z{n}"
                    wait_filled(act, place, unit)
                    act.activation(half(zT, n), ps(place, unit), ACT.Copy).then_inc(drained[place.bank(unit)], 1)

            def turn_comb(place):
                for n in range(HALVES):
                    unit = f"c{n}"
                    wait_filled(act, place, unit)
                    act.activation(half(cT, n), ps(place, unit)[0:2 * E, :], ACT.Copy
                                   ).then_inc(drained[place.bank(unit)], 1)

            def w_halves(lb):
                return [wT_hi[:, bass.ds(lb * T + n * BANK, BANK)] for n in range(HALVES)]

            uT_halves = [half(uT_hi, n) for n in range(HALVES)]

            def batch(place, b, lb):
                split_h(b)
                if lb is not None:
                    turn_probs(place, 7)
                    take_o(place, 1)
                project_qk(place)
                softmax(b, 0)
                project_v(place)
                softmax(b, 1)
                turn_probs(place, 0)
                softmax(b, 2)
                turn_probs(place, 1)
                if lb is not None:
                    wait_drained(act, place, "OT1")
                turn_x(place)
                act.sem_inc(xb_read, 1)
                if lb is not None:
                    turn_normed(place, "u", uT_halves, u_hi_made)
                softmax(b, 3)
                turn_probs(place, 2)
                if lb is not None:
                    key_softmax(place, lb)
                softmax(b, 4)
                if lb is not None:
                    turn_keys(place, lb)
                turn_probs(place, 3)
                softmax(b, 5)
                take_o(place, 0)
                if lb is not None:
                    take_m3(place)
                turn_probs(place, 4)
                softmax(b, 6)
                turn_probs(place, 5)
                softmax(b, 7)
                if lb is not None:
                    turn_normed(place, "w", w_halves(lb), w_hi_made)
                    take_logits(place)
                turn_probs(place, 6)
                if lb is not None:
                    route_exp(place, lb)
                    turn_z(place)
                    turn_comb(place)

            batch(FIRST, 0, None)
            with act.Fori(1, B) as b:
                batch(loop_place(b), b, b - 1)

            def gelu(m, s):
                act.wait_ge(e_h, m * (2 * E) + s + 1)
                if not (first_batch(m) and s < 2):
                    act.wait_ge(e_mul, m * (2 * E) + s - 1)
                act.activation(half(gel, s % 2), scores[:, s % 2, :], ACT.Gelu, bias=b1_c[:, s % E:s % E + 1]
                               ).then_inc(e_gelu, 1)

            def high(m, s):
                act.wait_ge(e_mul, m * (2 * E) + s + 1)
                if not (first_batch(m) and s < 2):
                    act.wait_ge(e_y, m * (2 * E) + s - 1)
                act.activation(half(hs_hi, s % 2), half(hs, s % 2), ACT.Copy).then_inc(e_hi, 1)

            def experts(m, between):
                gelu(m, 0)
                for s in range(2 * E):
                    if s + 1 < 2 * E:
                        gelu(m, s + 1)
                    high(m, s)
                    for step in between.get(s, ()):
                        step()

            lb = B - 1
            turn_probs(TAIL, 7)
            take_o(TAIL, 1)
            act.wait_ge(xb_made, B)
            experts(0, {
                TAIL_AT["u"]: [lambda: turn_normed(TAIL, "u", uT_halves, u_hi_made)],
                TAIL_AT["kT"]: [lambda: key_softmax(TAIL, lb)],
                TAIL_AT["p"]: [lambda: turn_keys(TAIL, lb)],
                TAIL_AT["m3"]: [lambda: take_m3(TAIL)],
                TAIL_AT["w"]: [lambda: turn_normed(TAIL, "w", w_halves(lb), w_hi_made),
                               lambda: take_logits(TAIL)],
                TAIL_AT["lT"]: [lambda: route_exp(TAIL, lb)],
                TAIL_AT["z"]: [lambda: turn_z(TAIL)],
                TAIL_AT["c"]: [lambda: turn_comb(TAIL)],
            })
            with act.Fori(1, B) as m:
                experts(m, {})

        @block.vector
        def _(dve):
            passed[dve] = passed_dve
            made = [0]

            def after(ins):
                made[0] += 1
                ins.then_inc(dve_chain, 1)
                dve.wait_ge(dve_chain, made[0])

            linked = [0]

            def link(lb, ins):
                linked[0] += 1
                ins.then_inc(chain, 1)
                dve.wait_ge(chain, lb * CHAIN + linked[0])

            def group_stats(b0, nb):
                for b in range(b0, b0 + nb):
                    dve.wait_ge(ld_x[b], 16)
                    for n in range(HALVES):
                        last = dve.bn_stats(gst[:, b, n, :], half(x_s[:, b, :], n))
                after(last)
                for b in range(b0, b0 + nb):
                    last = dve.bn_aggr(gmv[:, b, :], gst[:, b, :, :])
                last.then_inc(gn_mv, 1)

            def group_deviation(place, b0, nb):
                mean, dev = gsum[:, 0, b0:b0 + nb], gsum[:, 1, b0:b0 + nb]
                wait_filled(dve, place, "gn_mean")
                dve.tensor_copy(mean, ps(place, "gn_mean")[:, 0:nb]).then_inc(drained[place.bank("gn_mean")], 1)
                wait_drained(dve, place, "gn_mean")
                after(dve.tensor_tensor(dev, gmv[:, b0:b0 + nb, 0], mean, ALU.subtract))
                after(dve.tensor_tensor(dev, dev, dev, ALU.mult))
                dve.tensor_tensor(dev, dev, gmv[:, b0:b0 + nb, 1], ALU.add).then_inc(gn_mv, 1)
                wait_filled(dve, place, "gn_var")
                dve.tensor_copy(gsum[:, 2, b0:b0 + nb], ps(place, "gn_var")[:, 0:nb]
                                ).then_inc(drained[place.bank("gn_var")], 1)

            def group_affine(n, b0, nb):
                dve.wait_ge(gn_rstd, n)
                after(dve.tensor_scalar(gmul[:, b0:b0 + nb], gsum[:, 3, b0:b0 + nb], gs_c, None, ALU.mult))
                after(dve.tensor_tensor(gadd[:, b0:b0 + nb], gsum[:, 0, b0:b0 + nb], gmul[:, b0:b0 + nb], ALU.mult))
                dve.tensor_scalar(gadd[:, b0:b0 + nb], gadd[:, b0:b0 + nb], -1.0, gb_c, ALU.mult, ALU.add
                                  ).then_inc(gn_made, 1)

            def split(raw, hi, lo):
                after(dve.tensor_copy(hi, raw))
                dve.tensor_tensor(lo, raw, hi.bitcast(FP32), ALU.subtract).then_inc(setup_made, 1)

            dve.memset(rt_hi[:, :].bitcast(FP32), 0.0)
            dve.memset(rt_lo[:, :].bitcast(FP32), 0.0)
            group_stats(0, 1)
            dve.wait_ge(ld_w["wq"], 16)
            after(dve.tensor_scalar(wq_sc, wq_raw, SCALE, None, ALU.mult))
            split(wq_sc, wq_hi[:, :], wq_lo[:, :])
            group_deviation(SETUP, 0, 1)
            dve.wait_ge(ld_w["wk"], 16)
            split(wk_raw, wk_hi[:, :], wk_lo[:, :])
            dve.wait_ge(ld_w["cols"], 96)
            dve.tensor_scalar(bqs_c, bq_c, SCALE, None, ALU.mult).then_inc(setup_made, 1)
            group_affine(1, 0, 1)
            wait_filled(dve, SETUP, "wvT")
            dve.tensor_copy(wvT[:, :], tile(ps(SETUP, "wvT"), 0)).then_inc(drained[SETUP.bank("wvT")], 1)
            wait_filled(dve, SETUP, "wpv")
            after(dve.tensor_copy(wpv_hi[:, :], tile(ps(SETUP, "wpv"), 0)))
            dve.tensor_tensor(wpv_lo[:, :], tile(ps(SETUP, "wpv"), 0), wpv_hi[:, :].bitcast(FP32), ALU.subtract
                              ).then_inc(drained[SETUP.bank("wpv")], 1)
            wait_filled(dve, SETUP, "bias_o")
            dve.tensor_tensor(bias_o, ps(SETUP, "bias_o")[:, 0:1], bp_c, ALU.add
                              ).then_inc(drained[SETUP.bank("bias_o")], 1)

            def split_h(b):
                for n in range(HALVES):
                    dve.wait_ge(h_hi_made, b * HALVES + n + 1)
                    dve.tensor_tensor(half(h_lo, n), half(h_f, n), half(h_hi, n).bitcast(FP32), ALU.subtract
                                      ).then_inc(h_lo_made, 1)

            def setup_rest():
                wait_filled(dve, FIRST, "l1qT")
                dve.tensor_copy(l1qT[:, :], tile(ps(FIRST, "l1qT"), 0)).then_inc(drained[FIRST.bank("l1qT")], 1)
                wait_filled(dve, FIRST, "routerT")
                after(dve.tensor_copy(rt_hi[:, 0:E], ps(FIRST, "routerT")[:, 0:E]))
                dve.tensor_tensor(rt_lo[:, 0:E], ps(FIRST, "routerT")[:, 0:E], rt_hi[:, 0:E].bitcast(FP32),
                                  ALU.subtract).then_inc(drained[FIRST.bank("routerT")], 1)
                wait_filled(dve, FIRST, "b1T")
                dve.tensor_copy(b1_c[:, :], ps(FIRST, "b1T")[:, 0:E]).then_inc(drained[FIRST.bank("b1T")], 1)
                dve.wait_ge(ld_w["qkv"], 16)
                split(wqkv_s[:, C:2 * C], l1k_hi[:, :], l1k_lo[:, :])

            def low(place, unit, hi, lo, made, count):
                dve.wait_ge(made, count)
                dve.tensor_tensor(lo, ps(place, unit)[:, 0:lo.shape[-1]], hi.bitcast(FP32), ALU.subtract
                                  ).then_inc(drained[place.bank(unit)], 1)

            def project_qk(place, b):
                for n, (unit, hi, lo, bias) in enumerate((("q0", q_hi, q_lo, bqs_c), ("q1", q_hi, q_lo, bqs_c),
                                                          ("k0", k_hi, k_lo, bk_c), ("k1", k_hi, k_lo, bk_c))):
                    dve.wait_ge(qk_hi_made, b * 4 + n + 1)
                    dve.scalar_tensor_tensor(out=half(lo, n % 2), in0=ps(place, unit), scalar=bias,
                                             in1=half(hi, n % 2).bitcast(FP32), op0=ALU.add, op1=ALU.subtract
                                             ).then_inc(drained[place.bank(unit)], 1)

            def project_v(place, b):
                for n in range(HALVES):
                    low(place, f"v{n}", half(v_hi, n), half(v_lo, n), v_hi_made, b * HALVES + n + 1)

            def row_maximum(b, i):
                dve.wait_ge(s_made, b * TILES + i + 1)
                dve.tensor_reduce(row_max[:, i:i + 1], scores[:, 2 * (i % 2):2 * (i % 2) + 2, :].rearrange("p a t -> p (a t)"),
                                  AX.X, ALU.max, negate=True).then_inc(s_max, 1)

            def turn_probs(place, b, i):
                for n, unit in enumerate((f"T{i}a", f"T{i}b")):
                    dve.wait_ge(p_hi_made, b * (2 * TILES) + 2 * i + n + 1)
                    dve.tensor_tensor(tile_group(pT_lo, n, i), as_tiles(ps(place, unit)),
                                      tile_group(pT_hi, n, i).bitcast(FP32), ALU.subtract
                                      ).then_inc(drained[place.bank(unit)], 1)

            def residual(place, b, g):
                dve.wait_ge(s_exp, b * TILES + (g + 1) * QUAD)
                dve.reciprocal(row_sum[:, 1, g * QUAD:(g + 1) * QUAD], row_sum[:, 0, g * QUAD:(g + 1) * QUAD]
                               ).then_inc(r_made, 1)
                dve.wait_ge(r_made, b * 2 + g + 1)
                if g == 0:
                    wait_drained(dve, place, "xT0")
                    wait_drained(dve, place, "xT1")
                wait_filled(dve, place, f"OT{g}")
                for j in range(QUAD):
                    i = g * QUAD + j
                    last = dve.scalar_tensor_tensor(out=t1[:, i, :], in0=tile(ps(place, f"OT{g}"), j),
                                                    scalar=row_sum[:, 1, i:i + 1], in1=xT[:, i, :],
                                                    op0=ALU.mult, op1=ALU.add)
                last.then_inc(drained[place.bank(f"OT{g}")], 1)

            def norm_stats(lb, src):
                for j in range(TILES):
                    last = dve.bn_stats(lst[:, j, :], src[:, j, :])
                link(lb, last)
                apart(dve)
                for j in range(TILES):
                    last = dve.bn_aggr(lmv[:, j, :], lst[:, j, :])
                last.then_inc(ln_stats, 1)

            def norm_apply(n, src, dst, ready):
                dve.wait_ge(ln_rstd, n)
                for j in range(TILES):
                    last = dve.tensor_scalar(dst[:, j, :], src[:, j, :], lmv[:, j, 0:1], rstd[:, 1, j:j + 1],
                                             ALU.subtract, ALU.mult)
                last.then_inc(ready, 1)

            def norm1_stats(place, lb):
                linked[0] = 0
                wait_drained(dve, place, "OT1")
                norm_stats(lb, t1)

            def norm1_apply(lb):
                dve.wait_ge(z_stored, lb * 16 + 16)
                norm_apply(2 * lb + 1, t1, u, u_made)

            def turn_normed(place, kind, hi, lo, made, lb):
                for n in range(HALVES):
                    low(place, f"{kind}{n}", hi[n], lo[n], made, lb * HALVES + n + 1)

            def key_maximum(place, lb):
                for n in range(HALVES):
                    wait_filled(dve, place, f"kT{n}")
                    last = dve.tensor_reduce(kst[:, n:n + 1], ps(place, f"kT{n}"), AX.X, ALU.max, negate=True)
                link(lb, last)
                dve.tensor_tensor(kst[:, 2:3], kst[:, 0:1], kst[:, 1:2], ALU.min).then_inc(k_max, 1)

            def key_sums(place, lb):
                wait_drained(dve, place, "kT0")
                wait_drained(dve, place, "kT1")
                link(lb, dve.tensor_tensor(kst[:, 6:7], kst[:, 4:5], kst[:, 5:6], ALU.add))
                link(lb, dve.reciprocal(kst[:, 7:8], kst[:, 6:7]))

            def take(place, unit, dst):
                wait_filled(dve, place, unit)
                dve.tensor_copy(dst, tile(ps(place, unit), 0)).then_inc(drained[place.bank(unit)], 1)

            def take_ctx(place):
                wait_filled(dve, place, "ctx")
                dve.scalar_tensor_tensor(out=ctx_s[:, :], in0=tile(ps(place, "ctx"), 0), scalar=kst[:, 7:8],
                                         in1=head_mask[:, :], op0=ALU.mult, op1=ALU.mult
                                         ).then_inc(drained[place.bank("ctx")], 1)

            def take_m3(place, lb):
                low(place, "m3", m3_hi[:, :], m3_lo[:, :], m3_hi_made, lb + 1)

            def take_out(place, lb):
                dve.wait_ge(t1b_made, lb + 1)
                for n in range(HALVES):
                    unit = f"o{n}"
                    wait_filled(dve, place, unit)
                    dst = t2[:, n * QUAD:(n + 1) * QUAD, :]
                    dve.tensor_tensor(dst, as_tiles(ps(place, unit)), dst, ALU.add).then_inc(drained[place.bank(unit)], 1)
                wait_drained(dve, place, "o0")
                wait_drained(dve, place, "o1")
                norm_stats(lb, t2)

            def norm2_apply(lb):
                norm_apply(2 * lb + 2, t2, w_n, w_made)

            def over(v):
                return v.unsqueeze(2).to_broadcast([P, TILES, E])

            falling_b = falling[:, :].unsqueeze(1).to_broadcast([P, TILES, E])

            def route_in(place, lb):
                wait_filled(dve, place, "lT")
                logits = ps(place, "lT")[:, 0:TILES * E].rearrange("p (j e) -> p j e", e=E)
                link(lb, dve.tensor_reduce(rr[:, 0, :], logits, AX.X, ALU.max, negate=True))
                dve.tensor_tensor(rt[:, 0, :, :], logits, over(rr[:, 0, :]), ALU.add
                                  ).then_inc(drained[place.bank("lT")], 1)

            def route(lb):
                prob_e, ex, one, left, two = (rt[:, i, :, :] for i in range(5))
                total, first, k1, second, k2, both = (rr[:, i, :] for i in range(1, 7))
                tt, red = dve.tensor_tensor, dve.tensor_reduce
                dve.wait_ge(r_exp, lb + 1)
                link(lb, red(total, ex, AX.X, ALU.add))
                link(lb, dve.reciprocal(total, total))
                link(lb, tt(prob_e, ex, over(total), ALU.mult))
                link(lb, red(first, prob_e, AX.X, ALU.max))
                link(lb, tt(one, prob_e, over(first), ALU.is_equal))
                link(lb, tt(one, one, falling_b, ALU.mult))
                link(lb, red(k1, one, AX.X, ALU.max))
                link(lb, tt(one, one, over(k1), ALU.is_equal))
                link(lb, dve.scalar_tensor_tensor(out=left, in0=one, scalar=-2.0, in1=prob_e,
                                                  op0=ALU.mult, op1=ALU.add))
                link(lb, red(second, left, AX.X, ALU.max))
                link(lb, tt(two, left, over(second), ALU.is_equal))
                link(lb, tt(two, two, falling_b, ALU.mult))
                link(lb, red(k2, two, AX.X, ALU.max))
                link(lb, tt(two, two, over(k2), ALU.is_equal))
                dve.tensor_tensor(both, first, second, ALU.add)
                link(lb, tt(one, one, two, ALU.add))
                dve.tensor_scalar(both, both, 1e-12, None, ALU.max)
                link(lb, tt(one, one, prob_e, ALU.mult))
                link(lb, dve.reciprocal(both, both))
                link(lb, tt(one, one, over(both), ALU.mult))
                link(lb, dve.tensor_copy(comb[:, :, 0:E].bitcast(FP32R), one))
                tt(comb[:, :, E:2 * E], one, comb[:, :, 0:E], ALU.subtract).then_inc(c_made, 1)
                assert linked[0] == CHAIN, linked[0]

            def w_halves(w, lb):
                return [w[:, bass.ds(lb * T + n * BANK, BANK)] for n in range(HALVES)]

            uT_halves = [[half(m, n) for n in range(HALVES)] for m in (uT_hi, uT_lo)]

            def batch(place, b, lb):
                split_h(b)
                if lb is not None:
                    turn_probs(place, lb, 7)
                project_qk(place, b)
                row_maximum(b, 0)
                if lb is None:
                    group_stats(1, B - 1)
                    group_deviation(place, 1, B - 1)
                else:
                    residual(place, lb, 1)
                    norm1_stats(place, lb)
                project_v(place, b)
                row_maximum(b, 1)
                if lb is None:
                    setup_rest()
                else:
                    norm1_apply(lb)
                turn_probs(place, b, 0)
                row_maximum(b, 2)
                turn_probs(place, b, 1)
                if lb is None:
                    group_affine(2, 1, B - 1)
                else:
                    turn_normed(place, "u", uT_halves[0], uT_halves[1], u_hi_made, lb)
                row_maximum(b, 3)
                turn_probs(place, b, 2)
                if lb is not None:
                    key_maximum(place, lb)
                row_maximum(b, 4)
                if lb is not None:
                    key_sums(place, lb)
                turn_probs(place, b, 3)
                if lb is not None:
                    take(place, "g", gT_s[:, :])
                row_maximum(b, 5)
                if lb is not None:
                    take_ctx(place)
                    take(place, "m2", m2T_s[:, :])
                    take_m3(place, lb)
                turn_probs(place, b, 4)
                if lb is not None:
                    take_out(place, lb)
                row_maximum(b, 6)
                turn_probs(place, b, 5)
                if lb is not None:
                    norm2_apply(lb)
                    dve.wait_ge(t1b_made, lb + 1)
                else:
                    dve.wait_ge(experts_split, 3)
                residual(place, b, 0)
                row_maximum(b, 7)
                if lb is not None:
                    turn_normed(place, "w", w_halves(wT_hi, lb), w_halves(wT_lo, lb), w_hi_made, lb)
                turn_probs(place, b, 6)
                if lb is not None:
                    route_in(place, lb)
                    route(lb)

            batch(FIRST, 0, None)
            with dve.Fori(1, B) as b:
                batch(loop_place(b), b, b - 1)

            def weigh(m, s):
                dve.wait_ge(e_gelu, m * (2 * E) + s + 1)
                if not (first_batch(m) and s < 2):
                    dve.wait_ge(e_hi, m * (2 * E) + s - 1)
                    dve.wait_ge(e_lo, m * (2 * E) + s - 1)
                dve.tensor_tensor(half(hs, s % 2), half(gel, s % 2), scores[:, 2 + s % 2, :], ALU.mult
                                  ).then_inc(e_mul, 1)

            def lower(m, s):
                dve.wait_ge(e_hi, m * (2 * E) + s + 1)
                if not (first_batch(m) and s < 2):
                    dve.wait_ge(e_y, m * (2 * E) + s - 1)
                dve.tensor_tensor(half(hs_lo, s % 2), half(hs, s % 2), half(hs_hi, s % 2).bitcast(FP32),
                                  ALU.subtract).then_inc(e_lo, 1)

            def result(m, h):
                place = y_place(m)
                dve.wait_ge(e_y, m * (2 * E) + (h + 1) * E)
                dve.wait_ge(z_loaded[h], m * 16 + 16)
                if not first_batch(m):
                    dve.wait_ge(stored[h], m * 16)
                dve.tensor_tensor(half(out_s, h), ps(place, f"y{h}"), half(z_in, h), ALU.add
                                  ).then_inc(drained[place.bank(f"y{h}")], 1)

            def experts(m, between):
                weigh(m, 0)
                for s in range(2 * E):
                    if s + 1 < 2 * E:
                        weigh(m, s + 1)
                    lower(m, s)
                    if s == 1 and not first_batch(m):
                        result(m - 1, 1)
                    if s == E + 1:
                        result(m, 0)
                    for step in between.get(s, ()):
                        step()

            lb = B - 1
            turn_probs(TAIL, lb, 7)
            dve.wait_ge(xb_made, B)
            experts(0, {
                TAIL_AT["OT"]: [lambda: residual(TAIL, lb, 1), lambda: norm1_stats(TAIL, lb)],
                TAIL_AT["OT"] + 1: [lambda: norm1_apply(lb)],
                TAIL_AT["u"]: [lambda: turn_normed(TAIL, "u", uT_halves[0], uT_halves[1], u_hi_made, lb)],
                TAIL_AT["kT"]: [lambda: key_maximum(TAIL, lb)],
                TAIL_AT["p"]: [lambda: key_sums(TAIL, lb)],
                TAIL_AT["g"]: [lambda: take(TAIL, "g", gT_s[:, :])],
                TAIL_AT["ctx"]: [lambda: take_ctx(TAIL)],
                TAIL_AT["m2"]: [lambda: take(TAIL, "m2", m2T_s[:, :])],
                TAIL_AT["m3"]: [lambda: take_m3(TAIL, lb)],
                TAIL_AT["o"]: [lambda: take_out(TAIL, lb)],
                TAIL_AT["o"] + 1: [lambda: norm2_apply(lb)],
                TAIL_AT["w"]: [lambda: turn_normed(TAIL, "w", w_halves(wT_hi, lb), w_halves(wT_lo, lb), w_hi_made, lb)],
                TAIL_AT["lT"]: [lambda: route_in(TAIL, lb), ],
                TAIL_AT["z"]: [lambda: route(lb)],
            })
            with dve.Fori(1, B) as m:
                experts(m, {})
            result(B - 1, 1)

        @block.tensor
        def _(pe):
            passed[pe] = passed_pe
            def open_unit(place, unit):
                if not (isinstance(place.earlier(unit), int) and place.earlier(unit) == 0):
                    pe.wait_ge(drained[place.bank(unit)], place.earlier(unit))
                return ps(place, unit)

            def fill(place, unit, ins):
                ins.then_inc(filled[place.bank(unit)], 1)

            def product3(dst, left, right, start=True, stop=True):
                (lh, ll), (rh, rl) = left, right
                pe.matmul(dst, lh, rh, start=start, stop=False)
                pe.matmul(dst, lh, rl, start=False, stop=False)
                return pe.matmul(dst, ll, rh, start=False, stop=stop)

            def whole(place, unit, left, right):
                fill(place, unit, product3(open_unit(place, unit), left, right))

            def small(place, unit, n, left, right):
                dst = open_unit(place, unit)
                fill(place, unit, pe.matmul(dst[:, 0:n], left, right, start=True, stop=True))

            def turn(place, unit, tiles, rows=P, step=P):
                dst = open_unit(place, unit)
                for j, t in enumerate(tiles):
                    last = pe.transpose(dst[0:t.shape[-1], j * step:j * step + rows], t, ident[0:rows, 0:rows])
                fill(place, unit, last)

            def group_average(place, n, b0, nb):
                pe.wait_ge(gn_mv, n + 1)
                small(place, "gn_mean", nb, group_mean[:, :], gmv[:, b0:b0 + nb, 0])
                pe.wait_ge(gn_mv, n + 2)
                small(place, "gn_var", nb, group_mean[:, :], gsum[:, 1, b0:b0 + nb])

            pe.wait_ge(const_made, 1)
            group_average(SETUP, 0, 0, 1)
            pe.wait_ge(ld_w["wv"], 16)
            turn(SETUP, "wvT", [wv_s[:, :]])
            wait_drained(pe, SETUP, "wvT")
            pe.wait_ge(ld_w["wp"], 16)
            small(SETUP, "wpv", C, wvT[:, :], wp_s[:, :])
            pe.wait_ge(ld_w["cols"], 96)
            small(SETUP, "bias_o", 1, wp_s[:, :], bv_c)
            pe.wait_ge(setup_made, 3)

            def project_qk(place, b):
                for n, (unit, w) in enumerate((("q0", (wq_hi, wq_lo)), ("q1", (wq_hi, wq_lo)),
                                               ("k0", (wk_hi, wk_lo)), ("k1", (wk_hi, wk_lo)))):
                    pe.wait_ge(h_lo_made, b * HALVES + n % 2 + 1)
                    whole(place, unit, [m[:, :] for m in w], (half(h_hi, n % 2), half(h_lo, n % 2)))

            def project_v(place):
                for n in range(HALVES):
                    dst = open_unit(place, f"v{n}")
                    for j in range(QUAD):
                        i = n * QUAD + j
                        last = product3(tile(dst, j), (tile(h_hi, i), tile(h_lo, i)), (wpv_hi[:, :], wpv_lo[:, :]))
                    fill(place, f"v{n}", last)

            def score(b, i):
                if not (isinstance(b, int) and b == 0 and i < 2):
                    pe.wait_ge(s_exp, b * TILES + i - 1)
                for n in range(HALVES):
                    last = product3(scores[:, 2 * (i % 2) + n, :], (tile(q_hi, i), tile(q_lo, i)),
                                    (half(k_hi, n), half(k_lo, n)))
                last.then_inc(s_made, 1)

            def turn_probs(place, b, i):
                pe.wait_ge(s_exp, b * TILES + i + 1)
                for n in range(HALVES):
                    turn(place, f"T{i}" + "ab"[n], [tile(prob[:, i % 2, :], n * QUAD + j) for j in range(QUAD)])

            def attend(place, g, k0, k1):
                unit = f"PV{g}"
                if k0 == 0:
                    open_unit(place, unit)
                    wait_drained(pe, place, f"T{(g + 1) * QUAD - 1}a")
                    wait_drained(pe, place, f"T{(g + 1) * QUAD - 1}b")
                for k in range(k0, k1):
                    last = product3(ps(place, unit), (tile(v_hi, k), tile(v_lo, k)),
                                    (pT_hi[:, k, :], pT_lo[:, k, :]), start=k == 0, stop=k == TILES - 1)
                if k1 == TILES:
                    fill(place, unit, last)

            def turn_o(place, g):
                wait_drained(pe, place, f"PV{g}")
                turn(place, f"OT{g}", [tile(o_s, j) for j in range(QUAD)])

            def turn_x(place, b):
                pe.wait_ge(xb_made, b + 1)
                for n in range(HALVES):
                    turn(place, f"xT{n}", [tile(xb, n * QUAD + j) for j in range(QUAD)])

            def tiles_of(src, n):
                return [src[:, n * QUAD + j, :] for j in range(QUAD)]

            def turn_u(place, lb):
                pe.wait_ge(u_made, lb + 1)
                for n in range(HALVES):
                    turn(place, f"u{n}", tiles_of(u, n))

            def keys(place):
                for n in range(HALVES):
                    wait_drained(pe, place, f"u{n}")
                    whole(place, f"kT{n}", (l1k_hi[:, :], l1k_lo[:, :]), (half(uT_hi, n), half(uT_lo, n)))

            def turn_keys(place):
                for n in range(HALVES):
                    wait_drained(pe, place, f"kT{n}")
                    turn(place, f"p{n}", [tile(p1, n * QUAD + j) for j in range(QUAD)])

            def gather_keys(place):
                wait_drained(pe, place, "p0")
                wait_drained(pe, place, "p1")
                dst = open_unit(place, "g")
                for j in range(TILES):
                    last = pe.matmul(dst[:, 0:C], u[:, j, :], p1T[:, j, :], start=j == 0, stop=j == TILES - 1)
                fill(place, "g", last)

            def context(place):
                wait_drained(pe, place, "g")
                small(place, "ctx", C, gT_s[:, :], wqkv_s[:, 2 * C:3 * C])

            def merge2(place):
                wait_drained(pe, place, "ctx")
                small(place, "m2", C, ctx_s[:, :], l1qT[:, :])

            def merge3(place):
                wait_drained(pe, place, "m2")
                small(place, "m3", C, m2T_s[:, :], wout_s[:, :])

            def linear_out(place):
                wait_drained(pe, place, "m3")
                for n in range(HALVES):
                    dst = open_unit(place, f"o{n}")
                    for j in range(QUAD):
                        i = n * QUAD + j
                        last = product3(tile(dst, j), (tile(uT_hi, i), tile(uT_lo, i)), (m3_hi[:, :], m3_lo[:, :]))
                    fill(place, f"o{n}", last)

            def turn_w(place, lb):
                pe.wait_ge(w_made, lb + 1)
                for n in range(HALVES):
                    turn(place, f"w{n}", tiles_of(w_n, n))

            def w_of(lb, n):
                return [m[:, bass.ds(lb * T + n * BANK, BANK)] for m in (wT_hi, wT_lo)]

            def logits(place, lb):
                for n in range(HALVES):
                    wait_drained(pe, place, f"w{n}")
                    whole(place, f"lg{n}", (rt_hi[:, :], rt_lo[:, :]), w_of(lb, n))

            def turn_logits(place):
                wait_drained(pe, place, "lg0")
                wait_drained(pe, place, "lg1")
                dst = open_unit(place, "lT")
                apart(pe)
                for j in range(TILES):
                    last = pe.transpose(dst[:, j * E:(j + 1) * E], tile(lgT, j), ident[0:E, 0:E])
                fill(place, "lT", last)

            def turn_z(place, lb):
                pe.wait_ge(z_made, lb + 1)
                for n in range(HALVES):
                    turn(place, f"z{n}", tiles_of(t2, n))

            def turn_comb(place, lb):
                pe.wait_ge(c_made, lb + 1)
                for n in range(HALVES):
                    turn(place, f"c{n}", tiles_of(comb, n))

            def batch(place, b, lb):
                if lb is not None:
                    turn_probs(place, lb, 7)
                    attend(place, 1, 0, TILES)
                project_qk(place, b)
                for unit in ATTENTION["qk"]:
                    wait_drained(pe, place, unit)
                score(b, 0)
                if lb is None:
                    group_average(place, 2, 1, B - 1)
                else:
                    turn_o(place, 1)
                project_v(place)
                if lb is None:
                    pe.wait_ge(ld_w["qkv"], 16)
                    turn(place, "l1qT", [wqkv_s[:, 0:C]])
                    pe.wait_ge(ld_w["rows8"], 32)
                    turn(place, "routerT", [rows8[:, 0, :]], rows=E)
                    turn(place, "b1T", [rows8[:, 1, :]], rows=E)
                score(b, 1)
                turn_probs(place, b, 0)
                score(b, 2)
                turn_probs(place, b, 1)
                turn_x(place, b)
                if lb is not None:
                    turn_u(place, lb)
                score(b, 3)
                turn_probs(place, b, 2)
                if lb is not None:
                    keys(place)
                score(b, 4)
                if lb is not None:
                    turn_keys(place)
                turn_probs(place, b, 3)
                if lb is not None:
                    gather_keys(place)
                score(b, 5)
                for n in range(HALVES):
                    wait_drained(pe, place, f"v{n}")
                if lb is not None:
                    context(place)
                attend(place, 0, 0, 3)
                if lb is not None:
                    merge2(place)
                attend(place, 0, 3, TILES)
                if lb is not None:
                    merge3(place)
                turn_probs(place, b, 4)
                if lb is not None:
                    linear_out(place)
                score(b, 6)
                turn_probs(place, b, 5)
                turn_o(place, 0)
                score(b, 7)
                if lb is not None:
                    turn_w(place, lb)
                    logits(place, lb)
                turn_probs(place, b, 6)
                if lb is not None:
                    turn_logits(place)
                    turn_z(place, lb)
                    turn_comb(place, lb)

            batch(FIRST, 0, None)
            with pe.Fori(1, B) as b:
                batch(loop_place(b), b, b - 1)

            def hidden(m, s):
                h, e = s // E, s % E
                if first_batch(m) and s < 2:
                    pe.wait_ge(s_exp, B * TILES)
                else:
                    pe.wait_ge(e_gelu, m * (2 * E) + s - 1)
                    pe.wait_ge(e_mul, m * (2 * E) + s - 1)
                product3(scores[:, s % 2, :], (tile(w1_hi, e), tile(w1_lo, e)), w_of(m, h))
                pe.wait_ge(c_loaded[h], m * 16 + 16)
                pe.matmul(scores[:, 2 + s % 2, :], pick[:, e, :], cb_in[:, h, :], start=True, stop=True
                          ).then_inc(e_h, 1)

            def outward(m, s):
                h, e = s // E, s % E
                place = y_place(m)
                dst = ps(place, f"y{h}")
                if e == 0:
                    open_unit(place, f"y{h}")
                    pe.matmul(dst, b2_hi[:, :], cb_in[:, h, :], start=True, stop=False)
                    pe.matmul(dst, b2_lo[:, :], cb_in[:, h, :], start=False, stop=False)
                pe.wait_ge(e_lo, m * (2 * E) + s + 1)
                last = product3(dst, (tile(w2_hi, e), tile(w2_lo, e)), (half(hs_hi, s % 2), half(hs_lo, s % 2)),
                                start=False, stop=e == E - 1)
                last.then_inc(e_y, 1)

            def experts(m, last, between):
                for s in range(2 * E):
                    if s + 2 < 2 * E:
                        hidden(m, s + 2)
                    elif not last:
                        hidden(m + 1, s + 2 - 2 * E)
                    outward(m, s)
                    for step in between.get(s, ()):
                        step()

            lb = B - 1
            turn_probs(TAIL, lb, 7)
            attend(TAIL, 1, 0, TILES)
            pe.wait_ge(experts_split, 3)
            pe.wait_ge(mask_made, 1)
            hidden(0, 0)
            hidden(0, 1)
            experts(0, False, {
                TAIL_AT["OT"]: [lambda: turn_o(TAIL, 1)],
                TAIL_AT["u"]: [lambda: turn_u(TAIL, lb)],
                TAIL_AT["kT"]: [lambda: keys(TAIL)],
                TAIL_AT["p"]: [lambda: turn_keys(TAIL)],
                TAIL_AT["g"]: [lambda: gather_keys(TAIL)],
                TAIL_AT["ctx"]: [lambda: context(TAIL)],
                TAIL_AT["m2"]: [lambda: merge2(TAIL)],
                TAIL_AT["m3"]: [lambda: merge3(TAIL)],
                TAIL_AT["o"]: [lambda: linear_out(TAIL)],
                TAIL_AT["w"]: [lambda: turn_w(TAIL, lb), lambda: logits(TAIL, lb)],
                TAIL_AT["lT"]: [lambda: turn_logits(TAIL)],
                TAIL_AT["z"]: [lambda: turn_z(TAIL, lb)],
                TAIL_AT["c"]: [lambda: turn_comb(TAIL, lb)],
            })
            with pe.Fori(1, B - 1) as m:
                experts(m, False, {})
            experts(B - 1, True, {})


_INS = ['x', 'L0_conv_gn_scale', 'L0_conv_gn_bias', 'L0_conv_Wq', 'L0_conv_bq', 'L0_conv_Wk', 'L0_conv_bk',
        'L0_conv_Wv', 'L0_conv_bv', 'L0_conv_Wp', 'L0_conv_bp', 'L1_attn_W_qkv', 'L1_attn_W_out',
        'L1_attn_b_out', 'L1_ffn_router_w', 'L1_ffn_w1', 'L1_ffn_b1', 'L1_ffn_w2', 'L1_ffn_b2']


def kernel(**inputs):
    import numpy as _np
    import concourse.bacc as _bacc
    from concourse import mybir as _mybir
    from concourse.bass_utils import run_bass_kernel_spmd as _run

    nc = _bacc.Bacc("TRN2", target_bir_lowering=False, num_devices=1)
    arrays, args = {}, []
    for name in _INS:
        a = _np.ascontiguousarray(inputs[name])
        arrays[f"in_{name}_dram"] = a
        args.append(nc.dram_tensor(f"in_{name}_dram", a.shape, _mybir.dt.from_np(a.dtype), kind="ExternalInput").ap())
    o = nc.dram_tensor("out_0_dram", (4, 128, 32, 32), _mybir.dt.float32, kind="ExternalOutput").ap()
    conv_attention_moe(nc, *args, o)
    r = _run(nc, [arrays], core_ids=[0])
    return r.results[0]["out_0_dram"]
```

```python
from contextlib import ExitStack

import concourse.bass as bass
from concourse import mybir

FP32 = mybir.dt.float32
FP32R = mybir.dt.float32r
ALU = mybir.AluOpType
ACT = mybir.ActivationFunctionType
AX = mybir.AxisListType

B, C, T = 4, 128, 1024
GROUP = C // 32
HEADS, HEAD = 4, 32
E = 8
P = 128
BANK = 512
TILES = T // P
QUAD = BANK // P
HALVES = T // BANK
SCALE = float(C) ** -0.5
GN_EPS, LN_EPS = 1e-6, 1e-5

SETUP_UNITS = ["gn_mean", "gn_var", "wvT", "wpv", "bias_o"]
ATTENTION = dict(
    qk=["q0", "q1", "k0", "k1"], v=["v0", "v1"], xT=["xT0", "xT1"],
    T=[[f"T{i}a", f"T{i}b"] for i in range(TILES)],
)
LINEAR = dict(u=["u0", "u1"], kT=["kT0", "kT1"], p=["p0", "p1"])
ROUTING = dict(o=["o0", "o1"], w=["w0", "w1"], lg=["lg0", "lg1"], z=["z0", "z1"], c=["c0", "c1"])


def attention_units(linear, routing):
    T, L, R = ATTENTION["T"], linear, routing
    return (
        T[7] * L + ROUTING["o"] * R + ATTENTION["qk"] + ["PV1"] * L
        + (["OT1"] if L else ["gn_mean", "gn_var"]) + ATTENTION["v"]
        + (["l1qT", "routerT", "b1T"] if not L else []) + T[0]
        + ATTENTION["xT"] + T[1]
        + ROUTING["w"] * R + T[2]
        + LINEAR["u"] * L + ROUTING["lg"] * R + T[3]
        + ["lT"] * R + LINEAR["kT"] * L + ROUTING["z"] * R + ["PV0"] + T[4]
        + LINEAR["p"] * L + T[5]
        + ["OT0"] + ["g", "ctx"] * L + T[6]
        + ["m2"] * L + ROUTING["c"] * R + ["m3"] * L
    )


TAIL_UNITS = (ATTENTION["T"][7] + ROUTING["o"] + ["PV1", "OT1"] + ROUTING["w"] + ROUTING["lg"]
              + ["lT"] + LINEAR["u"] + ROUTING["z"] + LINEAR["kT"] + LINEAR["p"]
              + ["g"] + ROUTING["c"] + ["ctx", "m2", "m3"])
END_UNITS = ROUTING["o"] + ROUTING["w"] + ROUTING["lg"] + ["lT"] + ROUTING["z"] + ROUTING["c"]
TAIL_AT = dict(o1=0, OT=0, w=1, lg=2, lT=3, u=3, z=4, kT=4, p=5, g=6, c=6, ctx=7, m2=8, m3=9)
END_AT = dict(o=10, w=12, lg=13, lT=14, z=14, c=15)
LINEAR_CHAIN, ROUTING_CHAIN = 5, 17


class Place:

    def __init__(self, banks, before):
        self.banks, self.before = banks, before

    def bank(self, unit):
        return self.banks[unit][0]

    def earlier(self, unit):
        bank, n = self.banks[unit]
        return self.before[bank] + n


def place_of(units, before, banks=4):
    count, found = list(before), {}
    for n, unit in enumerate(units):
        bank = n % banks
        found[unit] = (bank, count[bank] - before[bank])
        count[bank] += 1
    return Place(found, before), count


def conv_attention_moe(nc, x, gn_scale, gn_bias, wq, bq, wk, bk, wv, bv, wp, bp,
                       w_qkv, w_out, b_out, router, w1, b1, w2, b2, out):
    SETUP, before = place_of(SETUP_UNITS, [0] * 4)
    FIRST, before = place_of(attention_units(0, 0), before)
    SECOND, before = place_of(attention_units(1, 0), before)
    LOOP, after_one = place_of(attention_units(1, 1), before)
    loops = [n - k for n, k in zip(after_one, before)]

    def loop_place(b):
        return Place(LOOP.banks, [n + (b - 2) * k for n, k in zip(before, loops)])

    TAIL, tail_end = place_of(TAIL_UNITS, [n + (B - 2) * k for n, k in zip(before, loops)], 2)
    END, _ = place_of(END_UNITS, tail_end, 2)

    def y_place(m):
        return Place({"y0": (2, 0), "y1": (3, 0)}, [tail_end[k] + m for k in range(4)])

    scratch_z = nc.dram_tensor("scratch_z", (B * HALVES, C, BANK), FP32).ap()
    scratch_c = nc.dram_tensor("scratch_c", (B * HALVES, 2 * E, BANK), FP32).ap()
    x_v = x.rearrange("b c h w -> b c (h w)")
    out_v = out.rearrange("b c h w -> b c (h w)")

    ctx = ExitStack()
    with ctx:
        def sb(name, shape, dt=FP32):
            return ctx.enter_context(nc.sbuf_tensor(name, shape, dt))

        def sem(name):
            return ctx.enter_context(nc.semaphore(name))

        ident = sb("ident", [P, P])
        group_mean = sb("group_mean", [C, C])
        head_mask = sb("head_mask", [C, C])
        minus_half = sb("minus_half", [P, TILES])
        falling = sb("falling", [P, E])
        wout_s = sb("wout_s", [C, C])
        wqkv_s = sb("wqkv_s", [C, 3 * C])
        l1qT = sb("l1qT", [C, C])
        wq_hi, wq_lo, wk_hi, wk_lo, wpv_hi, wpv_lo, l1k_hi, l1k_lo, rt_hi, rt_lo = (
            sb(n, [C, C], FP32R) for n in ("wq_hi", "wq_lo", "wk_hi", "wk_lo", "wpv_hi", "wpv_lo",
                                           "l1k_hi", "l1k_lo", "rt_hi", "rt_lo"))
        bout_row = sb("bout_row", [P, C])
        cols = sb("cols", [C, 8])
        bq_c, bk_c, bv_c, bp_c, gs_c, gb_c, bias_o = (cols[:, i:i + 1] for i in range(7))
        b1_c = sb("b1_c", [C, E])
        b2_s = sb("b2_s", [2 * E, C])
        b2_hi, b2_lo = sb("b2_hi", [2 * E, C], FP32R), sb("b2_lo", [2 * E, C], FP32R)
        pick = sb("pick", [2 * E, E, P], FP32R)
        w1_hi, w1_lo, w2_hi, w2_lo = (sb(n, [C, E * C], FP32R) for n in
                                      ("w1_hi", "w1_lo", "w2_hi", "w2_lo"))
        h_f = sb("h_f", [C, T])
        h_hi, h_lo = sb("h_hi", [C, T], FP32R), sb("h_lo", [C, T], FP32R)
        xb = sb("xb", [C, T])
        q_hi, q_lo, k_hi, k_lo = (sb(n, [C, T], FP32R) for n in ("q_hi", "q_lo", "k_hi", "k_lo"))
        v_hi, v_lo = sb("v_hi", [P, TILES * C], FP32R), sb("v_lo", [P, TILES * C], FP32R)
        prob = sb("prob", [P, 2, T])
        pT_hi = sb("pT_hi", [P, TILES, BANK], FP32R)
        pT_lo = sb("pT_lo", [P, TILES, BANK], FP32R)
        o_s = sb("o_s", [C, BANK])
        xT = sb("xT", [P, TILES, C])
        t1 = sb("t1", [P, TILES, C])
        t2 = sb("t2", [P, TILES, C])
        u = sb("u", [P, TILES, C])
        uT_hi, uT_lo = sb("uT_hi", [C, T], FP32R), sb("uT_lo", [C, T], FP32R)
        p1 = sb("p1", [C, T])
        p1T = sb("p1T", [P, TILES, C])
        w_n = sb("w_n", [P, TILES, C])
        gT_s, ctx_s, m2T_s = (sb(n, [C, C]) for n in ("gT_s", "ctx_s", "m2T_s"))
        m3_hi, m3_lo = sb("m3_hi", [C, C], FP32R), sb("m3_lo", [C, C], FP32R)
        wT_hi, wT_lo = sb("wT_hi", [C, B * T], FP32R), sb("wT_lo", [C, B * T], FP32R)
        gst = sb("gst", [C, B, HALVES, 6])
        gmv = sb("gmv", [C, B, 2])
        gsum = sb("gsum", [C, 4, B])
        gmul, gadd = sb("gmul", [C, B]), sb("gadd", [C, B])
        affine = sb("affine", [C, 2])
        mx = sb("mx", [P, 2, TILES])
        psum_row = sb("psum_row", [P, 2, TILES])
        lst = sb("lst", [P, TILES, 6])
        lmv = [sb(f"lmv{n}", [P, TILES, 2]) for n in range(2)]
        rstd = [sb(f"rstd{n}", [P, 3, TILES]) for n in range(2)]
        kst = sb("kst", [C, 8])
        lg = sb("lg", [P, TILES, E])
        rt = sb("rt", [P, 6, TILES, E])
        rr = sb("rr", [P, 8, TILES])
        comb = sb("comb", [P, TILES, 2 * E])
        gel, hs, out_s, z_in = (sb(n, [C, T]) for n in ("gel", "hs", "out_s", "z_in"))
        cb_in = sb("cb_in", [2 * E, HALVES, BANK], FP32R)
        wq_raw, wk_raw, wq_sc = (p1T[:, i, :] for i in range(3))
        rows8 = p1T[0:E, 3:5, :]
        wv_s, wp_s, wvT = gT_s, ctx_s, m2T_s
        w1_raw, w2_raw = t1[:, :, :].rearrange("p a b -> p (a b)"), u[:, :, :].rearrange("p a b -> p (a b)")
        pick_raw = w_n[0:2 * E, :, :].rearrange("p a b -> p (a b)")
        lgT = p1[0:E, :]
        hs_hi = [m[:, n * BANK:(n + 1) * BANK] for m in (h_hi, q_hi) for n in range(2)]
        hs_lo = [m[:, n * BANK:(n + 1) * BANK] for m in (h_lo, q_lo) for n in range(2)]
        x_of = [xb, gel, hs, out_s]
        zT_early, cT_early = out_s[:, :], z_in[0:2 * E, :]
        zT_late, cT_late = xb[:, :], h_f[0:2 * E, :]

        scores = ctx.enter_context(nc.psum_tensor("scores", [P, 4, BANK], FP32))
        ring = ctx.enter_context(nc.psum_tensor("ring", [P, 4, BANK], FP32))

        filled = [sem(f"filled{k}") for k in range(4)]
        drained = [sem(f"drained{k}") for k in range(4)]
        ld_x = [sem(f"ld_x{b}") for b in range(B)]
        ld_w = {n: sem(f"ld_{n}") for n in ("wq", "wk", "wv", "wp", "cols", "qkv", "wout", "bout",
                                            "rows8", "b2", "w1", "w2")}
        const_made = sem("const_made")
        mask_made = sem("mask_made")
        experts_split = sem("experts_split")
        setup_made = sem("setup_made")
        pool_chain = sem("pool_chain")
        dve_chain = sem("dve_chain")
        gn_mv = sem("gn_mv")
        gn_rstd = sem("gn_rstd")
        gn_made = sem("gn_made")
        h_made, xb_made = sem("h_made"), sem("xb_made")
        h_hi_made, h_lo_made = sem("h_hi_made"), sem("h_lo_made")
        affine_made, share_hi = sem("affine_made"), sem("share_hi")
        x_again = sem("x_again")
        passed_dve, passed_pe, passed_pool, passed_sp = (
            sem(f"passed_{e}") for e in ("dve", "pe", "pool", "sp"))
        xb_read = sem("xb_read")
        s_made, s_max, s_exp = sem("s_made"), sem("s_max"), sem("s_exp")
        qk_hi_made, v_hi_made, p_hi_made = sem("qk_hi_made"), sem("v_hi_made"), sem("p_hi_made")
        m3_lo_made = sem("m3_lo_made")
        u_hi_made, m3_hi_made, w_hi_made = sem("u_hi_made"), sem("m3_hi_made"), sem("w_hi_made")
        r_made = sem("r_made")
        linear_chain, routing_chain = sem("linear_chain"), sem("routing_chain")
        ln_stats = [sem(f"ln_stats{n}") for n in range(2)]
        ln_small = [sem(f"ln_small{n}") for n in range(2)]
        u_made, w_made, z_made, t1b_made = sem("u_made"), sem("w_made"), sem("z_made"), sem("t1b_made")
        k_max, r_exp, c_made = sem("k_max"), sem("r_exp"), sem("c_made")
        z_stored, c_stored = sem("z_stored"), sem("c_stored")
        z_loaded = [sem(f"z_loaded{h}") for h in range(HALVES)]
        c_loaded = [sem(f"c_loaded{h}") for h in range(HALVES)]
        e_h, e_gelu, e_mul, e_hi, e_lo, e_y = (sem(n) for n in
                                               ("e_h", "e_gelu", "e_mul", "e_hi", "e_lo", "e_y"))
        stored = [sem(f"stored{h}") for h in range(HALVES)]

        row_max, row_sum = mx[:, 0, :], psum_row
        bqs_c = cols[:, 7:8]
        block = ctx.enter_context(nc.Block())
        passed = {}

        def gathered(*steps):
            found = {}
            for at, step in steps:
                found.setdefault(at, []).append(step)
            return found

        def first_batch(m):
            return isinstance(m, int) and m == 0

        def as_tiles(m):
            return m.rearrange("p (j t) -> p j t", j=QUAD)

        def tile_group(m, n, i):
            return m[:, n * QUAD:(n + 1) * QUAD, (i % QUAD) * P:(i % QUAD + 1) * P]

        def ps(place, unit):
            return ring[:, place.bank(unit), :]

        def wait_filled(eng, place, unit):
            eng.wait_ge(filled[place.bank(unit)], place.earlier(unit) + 1)

        def wait_drained(eng, place, unit):
            eng.wait_ge(drained[place.bank(unit)], place.earlier(unit) + 1)

        def apart(eng):
            eng.sem_inc(passed[eng], 1)

        def tile(m, j):
            return m[:, j * P:(j + 1) * P]

        def half(m, n):
            return m[:, n * BANK:(n + 1) * BANK]

        @block.sync
        def _(sp):
            passed[sp] = passed_sp
            sp.dma_start(xb[:, :], x_v[0]).then_inc(ld_x[0], 16)
            sp.dma_start(wp_s[:, :], wp).then_inc(ld_w["wp"], 16)
            sp.dma_start(rows8[:, 0, :], router).then_inc(ld_w["rows8"], 16)
            sp.dma_start(rows8[:, 1, :], b1).then_inc(ld_w["rows8"], 16)
            for n in range(2):
                sp.dma_start(b2_s[n * E:(n + 1) * E, :], b2).then_inc(ld_w["b2"], 16)
            for b in range(1, B):
                sp.dma_start(x_of[b][:, :], x_v[b]).then_inc(ld_x[b], 16)
            sp.dma_start(w1_raw.rearrange("p (e f) -> p e f", e=E),
                         w1.rearrange("e c f -> c e f")).then_inc(ld_w["w1"], 16)
            sp.dma_start(w2_raw.rearrange("p (e f) -> p e f", e=E),
                         w2.rearrange("e c f -> c e f")).then_inc(ld_w["w2"], 16)

            def store_routed(place, lc, zT, cT):
                for unit in ROUTING["z"]:
                    wait_drained(sp, place, unit)
                    apart(sp)
                sp.dma_start(scratch_z[bass.ds(lc * HALVES, HALVES)].rearrange("h c t -> c h t"),
                             zT.rearrange("c (h t) -> c h t", h=HALVES)).then_inc(z_stored, 16)
                for unit in ROUTING["c"]:
                    wait_drained(sp, place, unit)
                    apart(sp)
                sp.dma_start(scratch_c[bass.ds(lc * HALVES, HALVES)].rearrange("h c t -> c h t"),
                             cT.rearrange("c (h t) -> c h t", h=HALVES)).then_inc(c_stored, 16)

            def load_x(b):
                sp.wait_ge(xb_read, b)
                apart(sp)
                sp.dma_start(xb[:, :], x_v[b]).then_inc(x_again, 16)

            def load_routed(m, h):
                sp.wait_ge(z_stored, 16 * (m + 2))
                apart(sp)
                sp.wait_ge(c_stored, 16 * (m + 2))
                apart(sp)
                sp.dma_start(half(z_in, h), scratch_z[m * HALVES + h]).then_inc(z_loaded[h], 16)
                sp.dma_start(cb_in[:, h, :].bitcast(FP32), scratch_c[m * HALVES + h]).then_inc(c_loaded[h], 16)

            sp.sem_inc(z_stored, 16)
            sp.sem_inc(c_stored, 16)
            load_x(1)
            load_x(2)
            with sp.Fori(2, B - 1) as b:
                load_x(b + 1)
                store_routed(loop_place(b), b - 2, zT_early, cT_early)
            store_routed(loop_place(B - 1), B - 3, zT_early, cT_early)
            sp.wait_ge(c_stored, 16 * (B - 1))
            for h in range(HALVES):
                load_routed(0, h)

            def result(m, h, more):
                wait_drained(sp, y_place(m), f"y{h}")
                apart(sp)
                sp.dma_start(out_v[m, :, h * BANK:(h + 1) * BANK], half(out_s, h)).then_inc(stored[h], 16)
                if more:
                    load_routed(m + 1, h)

            sp.wait_ge(xb_read, B)
            store_routed(TAIL, B - 2, zT_late, cT_late)
            result(0, 0, True)
            store_routed(END, B - 1, zT_late, cT_late)
            result(0, 1, True)
            with sp.Fori(1, B - 1) as m:
                for h in range(HALVES):
                    result(m, h, True)
            for h in range(HALVES):
                result(B - 1, h, False)
            for h in range(HALVES):
                sp.wait_ge(stored[h], 16 * B)

        @block.gpsimd
        def _(pool):
            passed[pool] = passed_pool
            made = [0]

            def after(ins):
                made[0] += 1
                ins.then_inc(pool_chain, 1)
                pool.wait_ge(pool_chain, made[0])

            bout_b = bout_row[:, :].unsqueeze(1).to_broadcast([P, TILES, C])
            pool.dma_start(wqkv_s[:, :], w_qkv).then_inc(ld_w["qkv"], 16)
            pool.dma_start(wout_s[:, :], w_out).then_inc(ld_w["wout"], 16)
            pool.dma_start(bout_row[:, :], b_out.rearrange("(a c) -> a c", a=1).to_broadcast([P, C])
                           ).then_inc(ld_w["bout"], 16)
            pool.memset(group_mean[:, :], 1.0 / GROUP)
            pool.memset(minus_half[:, :], -0.5)
            after(pool.memset(ident[:, :], 0.0))
            after(pool.affine_select(out=ident[:, :], in_=ident[:, :], compare_op=ALU.not_equal, fill=1.0,
                                     base=0, pattern=[[-1, P]], channel_multiplier=1))
            g_v = group_mean[:, :].rearrange("p (g c) -> p g c", c=GROUP)
            after(pool.affine_select(out=g_v, in_=g_v, compare_op=ALU.is_ge, fill=0.0, base=0,
                                     pattern=[[-GROUP, C // GROUP], [0, GROUP]], channel_multiplier=1))
            pool.affine_select(out=g_v, in_=g_v, compare_op=ALU.is_ge, fill=0.0, base=GROUP - 1,
                               pattern=[[GROUP, C // GROUP], [0, GROUP]],
                               channel_multiplier=-1).then_inc(const_made, 1)

            def group_rstd(place, b0, nb):
                wait_drained(pool, place, "gn_var")
                after(pool.tensor_scalar(gsum[:, 3, b0:b0 + nb], gsum[:, 2, b0:b0 + nb],
                                         1.0, GN_EPS, ALU.mult, ALU.add))
                pool.tensor_tensor(gsum[:, 3, b0:b0 + nb], gsum[:, 3, b0:b0 + nb],
                                   minus_half[:, 0:nb], ALU.pow).then_inc(gn_rstd, 1)

            def norm_x(b):
                pool.tensor_copy(affine[:, 0:1], gmul[:, bass.ds(b, 1)])
                pool.tensor_copy(affine[:, 1:2], gadd[:, bass.ds(b, 1)]).then_inc(affine_made, 1)
                pool.wait_ge(affine_made, b + 1)
                apart(pool)
                pool.tensor_scalar(h_f[:, :], xb[:, :], affine[:, 0:1], affine[:, 1:2],
                                   ALU.mult, ALU.add).then_inc(h_made, 1)

            def low_h(b):
                for n in range(HALVES):
                    pool.wait_ge(h_hi_made, b * HALVES + n + 1)
                    pool.tensor_tensor(half(h_lo, n), half(h_f, n), half(h_hi, n).bitcast(FP32), ALU.subtract
                                       ).then_inc(h_lo_made, 1)

            def add_bias(b):
                pool.tensor_scalar(xb[:, :], xb[:, :], 1.0, bias_o, ALU.mult, ALU.add).then_inc(xb_made, 1)

            def layer_norm(n, lb, src, dst, ready):
                eps, std, neg = (rstd[n][:, i, :] for i in range(3))
                pool.wait_ge(ln_stats[n], lb + 1)
                apart(pool)
                pool.tensor_scalar(neg, lmv[n][:, :, 0], -1.0, 0.0, ALU.mult, ALU.add)
                pool.tensor_scalar(eps, lmv[n][:, :, 1], 1.0, LN_EPS, ALU.mult, ALU.add
                                   ).then_inc(ln_small[n], 1)
                pool.wait_ge(ln_small[n], lb * 2 + 1)
                pool.tensor_tensor(std, eps, minus_half[:, :], ALU.pow).then_inc(ln_small[n], 1)
                pool.wait_ge(ln_small[n], lb * 2 + 2)
                apart(pool)
                for j in range(TILES):
                    last = pool.tensor_scalar(dst[:, j, :], src[:, j, :], neg[:, j:j + 1], std[:, j:j + 1],
                                              ALU.add, ALU.mult)
                last.then_inc(ready, 1)

            def second_norm(lc):
                layer_norm(1, lc, t2, w_n, w_made)
                pool.wait_ge(w_made, lc + 1)
                pool.tensor_tensor(t2[:, :, :], t2[:, :, :], w_n[:, :, :], ALU.add).then_inc(z_made, 1)

            def first_norm(place, lb, routed):
                layer_norm(0, lb, t1, u, u_made)
                if routed is not None:
                    wait_filled(pool, routed, "z1")
                pool.tensor_tensor(t2[:, :, :], t1[:, :, :], bout_b, ALU.add).then_inc(t1b_made, 1)

            group_rstd(SETUP, 0, 1)
            pool.wait_ge(gn_made, 1)
            norm_x(0)
            low_h(0)
            after(pool.memset(head_mask[:, :], float(HEAD) ** -0.5))
            m_v = head_mask[:, :].rearrange("p (g c) -> p g c", c=HEAD)
            after(pool.affine_select(out=m_v, in_=m_v, compare_op=ALU.is_ge, fill=0.0, base=0,
                                     pattern=[[-HEAD, HEADS], [0, HEAD]], channel_multiplier=1))
            after(pool.affine_select(out=m_v, in_=m_v, compare_op=ALU.is_ge, fill=0.0, base=HEAD - 1,
                                     pattern=[[HEAD, HEADS], [0, HEAD]], channel_multiplier=-1))
            for e in range(E):
                pool.memset(falling[:, e:e + 1], float(E - e))
            p_v = pick_raw.rearrange("p (e t) -> p e t", e=E)
            after(pool.memset(pick_raw, 0.0))
            for base in (0, -E):
                after(pool.affine_select(out=p_v, in_=p_v, compare_op=ALU.not_equal, fill=1.0, base=base,
                                         pattern=[[-1, E], [0, P]], channel_multiplier=1))
            pool.tensor_copy(pick[:, :, :], p_v).then_inc(mask_made, 1)
            wait_drained(pool, SETUP, "bias_o")
            add_bias(0)
            group_rstd(FIRST, 1, B - 1)
            pool.wait_ge(gn_made, 2)
            for n, (name, raw, hi, lo) in enumerate((("w1", w1_raw, w1_hi, w1_lo),
                                                    ("w2", w2_raw, w2_hi, w2_lo),
                                                    ("b2", b2_s[:, :], b2_hi, b2_lo))):
                pool.wait_ge(ld_w[name], 32 if name == "b2" else 16)
                after(pool.tensor_copy(hi[:, :], raw))
                pool.tensor_tensor(lo[:, :], raw, hi[:, :].bitcast(FP32), ALU.subtract
                                   ).then_inc(experts_split, 1)
            pool.wait_ge(ld_w["bout"], 16)

            def batch(place, b, la, lc):
                pool.wait_ge(x_again, b * 16)
                apart(pool)
                norm_x(b)
                low_h(b)
                if lc is not None:
                    second_norm(lc)
                add_bias(b)
                first_norm(place, la, place if lc is not None else None)

            batch(SECOND, 1, 0, None)
            with pool.Fori(2, B) as b:
                batch(loop_place(b), b, b - 1, b - 2)
            second_norm(B - 2)
            first_norm(TAIL, B - 1, TAIL)
            second_norm(B - 1)

        @block.scalar
        def _(act):
            act.dma_start(wq_raw, wq).then_inc(ld_w["wq"], 16)
            for i, v in enumerate((bq, bk, bv, bp, gn_scale, gn_bias)):
                act.dma_start(cols[:, i:i + 1], v.rearrange("(c a) -> c a", a=1)).then_inc(ld_w["cols"], 16)
            act.dma_start(wk_raw, wk).then_inc(ld_w["wk"], 16)
            act.dma_start(wv_s[:, :], wv).then_inc(ld_w["wv"], 16)

            def split_h(b):
                act.wait_ge(h_made, b + 1)
                for n in range(HALVES):
                    act.activation(half(h_hi, n), half(h_f, n), ACT.Copy).then_inc(h_hi_made, 1)

            def project_qk(place):
                for unit, hi, bias, n in (("q0", q_hi, bqs_c, 0), ("q1", q_hi, bqs_c, 1),
                                          ("k0", k_hi, bk_c, 0), ("k1", k_hi, bk_c, 1)):
                    wait_filled(act, place, unit)
                    act.activation(half(hi, n), ps(place, unit), ACT.Identity, bias=bias).then_inc(qk_hi_made, 1)

            def project_v(place):
                for n in range(HALVES):
                    wait_filled(act, place, f"v{n}")
                    act.activation(half(v_hi, n), ps(place, f"v{n}"), ACT.Copy).then_inc(v_hi_made, 1)

            def softmax(b, i):
                act.wait_ge(s_max, b * TILES + i + 1)
                act.activation(prob[:, i % 2, :], scores[:, 2 * (i % 2):2 * (i % 2) + 2, :].rearrange("p a t -> p (a t)"),
                               ACT.Exp, bias=row_max[:, i:i + 1], accum_out=row_sum[:, 0, i:i + 1]).then_inc(s_exp, 1)

            def turn_probs(place, i):
                for n, unit in enumerate((f"T{i}a", f"T{i}b")):
                    wait_filled(act, place, unit)
                    act.activation(tile_group(pT_hi, n, i), as_tiles(ps(place, unit)), ACT.Copy).then_inc(p_hi_made, 1)

            def take_o(place, g):
                wait_filled(act, place, f"PV{g}")
                act.activation(o_s[:, :], ps(place, f"PV{g}"), ACT.Copy).then_inc(drained[place.bank(f"PV{g}")], 1)

            def turn_x(place):
                for n in range(HALVES):
                    unit = f"xT{n}"
                    wait_filled(act, place, unit)
                    act.activation(xT[:, n * QUAD:(n + 1) * QUAD, :], as_tiles(ps(place, unit)), ACT.Copy
                                   ).then_inc(drained[place.bank(unit)], 1)

            def turn_normed(place, kind, hi, made):
                for n in range(HALVES):
                    wait_filled(act, place, f"{kind}{n}")
                    act.activation(hi[n], ps(place, f"{kind}{n}"), ACT.Copy).then_inc(made, 1)

            def key_softmax(place, lb):
                act.wait_ge(k_max, lb + 1)
                for n in range(HALVES):
                    act.activation(half(p1, n), ps(place, f"kT{n}"), ACT.Exp, bias=kst[:, 2:3],
                                   accum_out=kst[:, 4 + n:5 + n]).then_inc(drained[place.bank(f"kT{n}")], 1)

            def turn_keys(place):
                for n in range(HALVES):
                    unit = f"p{n}"
                    wait_filled(act, place, unit)
                    act.activation(p1T[:, n * QUAD:(n + 1) * QUAD, :], as_tiles(ps(place, unit)), ACT.Copy
                                   ).then_inc(drained[place.bank(unit)], 1)

            def take_m3(place):
                wait_filled(act, place, "m3")
                act.activation(m3_hi[:, :], tile(ps(place, "m3"), 0), ACT.Copy).then_inc(m3_hi_made, 1)

            def take_logits(place):
                for n in range(HALVES):
                    unit = f"lg{n}"
                    wait_filled(act, place, unit)
                    act.activation(half(lgT, n), ps(place, unit)[0:E, :], ACT.Copy
                                   ).then_inc(drained[place.bank(unit)], 1)

            def route_exp(place, lb):
                wait_drained(act, place, "lT")
                act.activation(rt[:, 1, :, :], rt[:, 0, :, :], ACT.Exp).then_inc(r_exp, 1)

            def turn_z(place, lc, zT):
                act.wait_ge(z_stored, lc * 16 + 16)
                for n in range(HALVES):
                    unit = f"z{n}"
                    wait_filled(act, place, unit)
                    act.activation(half(zT, n), ps(place, unit), ACT.Copy).then_inc(drained[place.bank(unit)], 1)

            def turn_comb(place, lc, cT):
                act.wait_ge(c_stored, lc * 16 + 16)
                for n in range(HALVES):
                    unit = f"c{n}"
                    wait_filled(act, place, unit)
                    act.activation(half(cT, n), ps(place, unit)[0:2 * E, :], ACT.Copy
                                   ).then_inc(drained[place.bank(unit)], 1)

            def w_halves(lb):
                return [wT_hi[:, bass.ds(lb * T + n * BANK, BANK)] for n in range(HALVES)]

            uT_halves = [half(uT_hi, n) for n in range(HALVES)]

            def batch(place, b, la, lc):
                split_h(b)
                if la is not None:
                    turn_probs(place, 7)
                project_qk(place)
                softmax(b, 0)
                if la is not None:
                    take_o(place, 1)
                softmax(b, 1)
                project_v(place)
                turn_probs(place, 0)
                softmax(b, 2)
                if la is not None:
                    wait_drained(act, place, "OT1")
                turn_x(place)
                act.sem_inc(xb_read, 1)
                turn_probs(place, 1)
                softmax(b, 3)
                if lc is not None:
                    turn_normed(place, "w", w_halves(lc), w_hi_made)
                turn_probs(place, 2)
                softmax(b, 4)
                if la is not None:
                    turn_normed(place, "u", uT_halves, u_hi_made)
                if lc is not None:
                    take_logits(place)
                turn_probs(place, 3)
                softmax(b, 5)
                if lc is not None:
                    route_exp(place, lc)
                if la is not None:
                    key_softmax(place, la)
                if lc is not None:
                    turn_z(place, lc, zT_early)
                take_o(place, 0)
                turn_probs(place, 4)
                softmax(b, 6)
                if la is not None:
                    turn_keys(place)
                turn_probs(place, 5)
                softmax(b, 7)
                turn_probs(place, 6)
                if lc is not None:
                    turn_comb(place, lc, cT_early)
                if la is not None:
                    take_m3(place)

            batch(FIRST, 0, None, None)
            batch(SECOND, 1, 0, None)
            with act.Fori(2, B) as b:
                batch(loop_place(b), b, b - 1, b - 2)

            def gelu(m, s):
                act.wait_ge(e_h, m * (2 * E) + s + 1)
                if not (first_batch(m) and s < 2):
                    act.wait_ge(e_mul, m * (2 * E) + s - 1)
                act.activation(half(gel, s % 2), scores[:, s % 2, :], ACT.Gelu, bias=b1_c[:, s % E:s % E + 1]
                               ).then_inc(e_gelu, 1)

            def high(m, s):
                act.wait_ge(e_mul, m * (2 * E) + s + 1)
                if not (first_batch(m) and s < 4):
                    act.wait_ge(e_y, m * (2 * E) + s - 3)
                act.activation(hs_hi[s % 4], half(hs, s % 2), ACT.Copy).then_inc(e_hi, 1)

            def experts(m, between):
                gelu(m, 0)
                for s in range(2 * E):
                    if s + 1 < 2 * E:
                        gelu(m, s + 1)
                    high(m, s)
                    for step in between.get(s, ()):
                        step()

            la, lc = B - 1, B - 2
            turn_probs(TAIL, 7)
            experts(0, gathered(
                (TAIL_AT["o1"], lambda: take_o(TAIL, 1)),
                (TAIL_AT["w"], lambda: turn_normed(TAIL, "w", w_halves(lc), w_hi_made)),
                (TAIL_AT["lg"], lambda: take_logits(TAIL)),
                (TAIL_AT["u"], lambda: turn_normed(TAIL, "u", uT_halves, u_hi_made)),
                (TAIL_AT["z"], lambda: route_exp(TAIL, lc)),
                (TAIL_AT["z"], lambda: turn_z(TAIL, lc, zT_late)),
                (TAIL_AT["kT"], lambda: key_softmax(TAIL, la)),
                (TAIL_AT["p"], lambda: turn_keys(TAIL)),
                (TAIL_AT["c"], lambda: turn_comb(TAIL, lc, cT_late)),
                (TAIL_AT["m3"], lambda: take_m3(TAIL)),
                (END_AT["w"], lambda: turn_normed(END, "w", w_halves(la), w_hi_made)),
                (END_AT["lg"], lambda: take_logits(END)),
                (END_AT["z"], lambda: route_exp(END, la)),
                (END_AT["z"], lambda: turn_z(END, la, zT_late)),
                (END_AT["c"], lambda: turn_comb(END, la, cT_late)),
            ))
            with act.Fori(1, B) as m:
                experts(m, {})

        @block.vector
        def _(dve):
            passed[dve] = passed_dve
            made = [0]

            def after(ins):
                made[0] += 1
                ins.then_inc(dve_chain, 1)
                dve.wait_ge(dve_chain, made[0])

            linked = {}

            def link(chain, lb, ins):
                n, per_batch = linked.get(chain, 0) + 1, dict(linear=LINEAR_CHAIN, routing=ROUTING_CHAIN)[chain]
                linked[chain] = n % per_batch
                signal = dict(linear=linear_chain, routing=routing_chain)[chain]
                ins.then_inc(signal, 1)
                dve.wait_ge(signal, lb * per_batch + n)

            def group_stats(b0, nb):
                for b in range(b0, b0 + nb):
                    dve.wait_ge(ld_x[b], 16)
                    for n in range(HALVES):
                        last = dve.bn_stats(gst[:, b, n, :], half(x_of[b], n))
                after(last)
                for b in range(b0, b0 + nb):
                    last = dve.bn_aggr(gmv[:, b, :], gst[:, b, :, :])
                last.then_inc(gn_mv, 1)

            def group_deviation(place, b0, nb):
                mean, dev = gsum[:, 0, b0:b0 + nb], gsum[:, 1, b0:b0 + nb]
                wait_filled(dve, place, "gn_mean")
                dve.tensor_copy(mean, ps(place, "gn_mean")[:, 0:nb]).then_inc(drained[place.bank("gn_mean")], 1)
                wait_drained(dve, place, "gn_mean")
                after(dve.tensor_tensor(dev, gmv[:, b0:b0 + nb, 0], mean, ALU.subtract))
                after(dve.tensor_tensor(dev, dev, dev, ALU.mult))
                dve.tensor_tensor(dev, dev, gmv[:, b0:b0 + nb, 1], ALU.add).then_inc(gn_mv, 1)
                wait_filled(dve, place, "gn_var")
                dve.tensor_copy(gsum[:, 2, b0:b0 + nb], ps(place, "gn_var")[:, 0:nb]
                                ).then_inc(drained[place.bank("gn_var")], 1)

            def group_affine(n, b0, nb):
                dve.wait_ge(gn_rstd, n)
                after(dve.tensor_scalar(gmul[:, b0:b0 + nb], gsum[:, 3, b0:b0 + nb], gs_c, None, ALU.mult))
                after(dve.tensor_tensor(gadd[:, b0:b0 + nb], gsum[:, 0, b0:b0 + nb], gmul[:, b0:b0 + nb], ALU.mult))
                dve.tensor_scalar(gadd[:, b0:b0 + nb], gadd[:, b0:b0 + nb], -1.0, gb_c, ALU.mult, ALU.add
                                  ).then_inc(gn_made, 1)

            def split(raw, hi, lo):
                after(dve.tensor_copy(hi, raw))
                dve.tensor_tensor(lo, raw, hi.bitcast(FP32), ALU.subtract).then_inc(setup_made, 1)

            dve.memset(rt_hi[:, :].bitcast(FP32), 0.0)
            dve.memset(rt_lo[:, :].bitcast(FP32), 0.0)
            group_stats(0, 1)
            dve.wait_ge(ld_w["wq"], 16)
            after(dve.tensor_scalar(wq_sc, wq_raw, SCALE, None, ALU.mult))
            split(wq_sc, wq_hi[:, :], wq_lo[:, :])
            group_deviation(SETUP, 0, 1)
            dve.wait_ge(ld_w["wk"], 16)
            split(wk_raw, wk_hi[:, :], wk_lo[:, :])
            dve.wait_ge(ld_w["cols"], 96)
            dve.tensor_scalar(bqs_c, bq_c, SCALE, None, ALU.mult).then_inc(setup_made, 1)
            group_affine(1, 0, 1)
            wait_filled(dve, SETUP, "wvT")
            dve.tensor_copy(wvT[:, :], tile(ps(SETUP, "wvT"), 0)).then_inc(drained[SETUP.bank("wvT")], 1)
            wait_filled(dve, SETUP, "wpv")
            after(dve.tensor_copy(wpv_hi[:, :], tile(ps(SETUP, "wpv"), 0)))
            dve.tensor_tensor(wpv_lo[:, :], tile(ps(SETUP, "wpv"), 0), wpv_hi[:, :].bitcast(FP32), ALU.subtract
                              ).then_inc(drained[SETUP.bank("wpv")], 1)
            wait_filled(dve, SETUP, "bias_o")
            dve.tensor_tensor(bias_o, ps(SETUP, "bias_o")[:, 0:1], bp_c, ALU.add
                              ).then_inc(drained[SETUP.bank("bias_o")], 1)

            def setup_rest():
                wait_filled(dve, FIRST, "l1qT")
                dve.tensor_copy(l1qT[:, :], tile(ps(FIRST, "l1qT"), 0)).then_inc(drained[FIRST.bank("l1qT")], 1)
                wait_filled(dve, FIRST, "routerT")
                after(dve.tensor_copy(rt_hi[:, 0:E], ps(FIRST, "routerT")[:, 0:E]))
                dve.tensor_tensor(rt_lo[:, 0:E], ps(FIRST, "routerT")[:, 0:E], rt_hi[:, 0:E].bitcast(FP32),
                                  ALU.subtract).then_inc(drained[FIRST.bank("routerT")], 1)
                wait_filled(dve, FIRST, "b1T")
                dve.tensor_copy(b1_c[:, :], ps(FIRST, "b1T")[:, 0:E]).then_inc(drained[FIRST.bank("b1T")], 1)
                dve.wait_ge(ld_w["qkv"], 16)
                split(wqkv_s[:, C:2 * C], l1k_hi[:, :], l1k_lo[:, :])

            def low(place, unit, hi, lo, made, count):
                dve.wait_ge(made, count)
                dve.tensor_tensor(lo, ps(place, unit)[:, 0:lo.shape[-1]], hi.bitcast(FP32), ALU.subtract
                                  ).then_inc(drained[place.bank(unit)], 1)

            def project_qk(place, b):
                for n, (unit, hi, lo, bias) in enumerate((("q0", q_hi, q_lo, bqs_c), ("q1", q_hi, q_lo, bqs_c),
                                                          ("k0", k_hi, k_lo, bk_c), ("k1", k_hi, k_lo, bk_c))):
                    dve.wait_ge(qk_hi_made, b * 4 + n + 1)
                    dve.scalar_tensor_tensor(out=half(lo, n % 2), in0=ps(place, unit), scalar=bias,
                                             in1=half(hi, n % 2).bitcast(FP32), op0=ALU.add, op1=ALU.subtract
                                             ).then_inc(drained[place.bank(unit)], 1)

            def project_v(place, b):
                for n in range(HALVES):
                    low(place, f"v{n}", half(v_hi, n), half(v_lo, n), v_hi_made, b * HALVES + n + 1)

            def row_maximum(b, i):
                dve.wait_ge(s_made, b * TILES + i + 1)
                dve.tensor_reduce(row_max[:, i:i + 1], scores[:, 2 * (i % 2):2 * (i % 2) + 2, :].rearrange("p a t -> p (a t)"),
                                  AX.X, ALU.max, negate=True).then_inc(s_max, 1)

            def turn_probs(place, b, i):
                for n, unit in enumerate((f"T{i}a", f"T{i}b")):
                    dve.wait_ge(p_hi_made, b * (2 * TILES) + 2 * i + n + 1)
                    dve.tensor_tensor(tile_group(pT_lo, n, i), as_tiles(ps(place, unit)),
                                      tile_group(pT_hi, n, i).bitcast(FP32), ALU.subtract
                                      ).then_inc(drained[place.bank(unit)], 1)

            def residual(place, b, g):
                dve.wait_ge(s_exp, b * TILES + (g + 1) * QUAD)
                dve.reciprocal(row_sum[:, 1, g * QUAD:(g + 1) * QUAD], row_sum[:, 0, g * QUAD:(g + 1) * QUAD]
                               ).then_inc(r_made, 1)
                dve.wait_ge(r_made, b * 2 + g + 1)
                if g == 0:
                    wait_drained(dve, place, "xT0")
                    wait_drained(dve, place, "xT1")
                wait_filled(dve, place, f"OT{g}")
                for j in range(QUAD):
                    i = g * QUAD + j
                    last = dve.scalar_tensor_tensor(out=t1[:, i, :], in0=tile(ps(place, f"OT{g}"), j),
                                                    scalar=row_sum[:, 1, i:i + 1], in1=xT[:, i, :],
                                                    op0=ALU.mult, op1=ALU.add)
                last.then_inc(drained[place.bank(f"OT{g}")], 1)

            def norm_stats(n, lb, src):
                for j in range(TILES):
                    last = dve.bn_stats(lst[:, j, :], src[:, j, :])
                link("linear", lb, last)
                apart(dve)
                for j in range(TILES):
                    last = dve.bn_aggr(lmv[n][:, j, :], lst[:, j, :])
                last.then_inc(ln_stats[n], 1)

            def norm1_stats(place, lb):
                wait_drained(dve, place, "OT1")
                norm_stats(0, lb, t1)

            def turn_normed(place, kind, hi, lo, made, lb):
                for n in range(HALVES):
                    low(place, f"{kind}{n}", hi[n], lo[n], made, lb * HALVES + n + 1)

            def key_maximum(place, lb):
                for n in range(HALVES):
                    wait_filled(dve, place, f"kT{n}")
                    last = dve.tensor_reduce(kst[:, n:n + 1], ps(place, f"kT{n}"), AX.X, ALU.max, negate=True)
                link("linear", lb, last)
                dve.tensor_tensor(kst[:, 2:3], kst[:, 0:1], kst[:, 1:2], ALU.min).then_inc(k_max, 1)

            def key_sums(place, lb):
                wait_drained(dve, place, "kT0")
                wait_drained(dve, place, "kT1")
                link("linear", lb, dve.tensor_tensor(kst[:, 6:7], kst[:, 4:5], kst[:, 5:6], ALU.add))
                link("linear", lb, dve.reciprocal(kst[:, 7:8], kst[:, 6:7]))

            def take(place, unit, dst):
                wait_filled(dve, place, unit)
                dve.tensor_copy(dst, tile(ps(place, unit), 0)).then_inc(drained[place.bank(unit)], 1)

            def take_ctx(place):
                wait_filled(dve, place, "ctx")
                dve.scalar_tensor_tensor(out=ctx_s[:, :], in0=tile(ps(place, "ctx"), 0), scalar=kst[:, 7:8],
                                         in1=head_mask[:, :], op0=ALU.mult, op1=ALU.mult
                                         ).then_inc(drained[place.bank("ctx")], 1)

            def take_m3(place, lb):
                dve.wait_ge(m3_hi_made, lb + 1)
                dve.tensor_tensor(m3_lo[:, :], tile(ps(place, "m3"), 0), m3_hi[:, :].bitcast(FP32), ALU.subtract
                                  ).then_inc(drained[place.bank("m3")], 1)
                wait_drained(dve, place, "m3")
                dve.sem_inc(m3_lo_made, 1)

            def take_out(place, lb):
                dve.wait_ge(t1b_made, lb + 1)
                for n in range(HALVES):
                    unit = f"o{n}"
                    wait_filled(dve, place, unit)
                    dst = t2[:, n * QUAD:(n + 1) * QUAD, :]
                    dve.tensor_tensor(dst, as_tiles(ps(place, unit)), dst, ALU.add).then_inc(drained[place.bank(unit)], 1)

            def norm2_stats(place, lb):
                wait_drained(dve, place, "o0")
                wait_drained(dve, place, "o1")
                norm_stats(1, lb, t2)

            def over(v):
                return v.unsqueeze(2).to_broadcast([P, TILES, E])

            falling_b = falling[:, :].unsqueeze(1).to_broadcast([P, TILES, E])

            def route(place, lc):
                less, ex, one, left, two = (rt[:, i, :, :] for i in range(5))
                top, total, k1, second, k2, both = (rr[:, i, :] for i in range(6))
                tt, red, stt = dve.tensor_tensor, dve.tensor_reduce, dve.scalar_tensor_tensor

                def part_a():
                    wait_filled(dve, place, "lT")
                    logits = ps(place, "lT")[:, 0:TILES * E].rearrange("p (j e) -> p j e", e=E)
                    link("routing", lc, red(top, logits, AX.X, ALU.max, negate=True))
                    tt(less, logits, over(top), ALU.add).then_inc(drained[place.bank("lT")], 1)
                    wait_drained(dve, place, "lT")
                    link("routing", lc, dve.tensor_scalar(one, less, 0.0, None, ALU.is_equal))
                    link("routing", lc, tt(one, one, falling_b, ALU.mult))
                    link("routing", lc, red(k1, one, AX.X, ALU.max))
                    link("routing", lc, tt(one, one, over(k1), ALU.is_equal))
                    link("routing", lc, stt(out=left, in0=one, scalar=-3e38, in1=less, op0=ALU.mult, op1=ALU.add))

                def part_b():
                    link("routing", lc, red(second, left, AX.X, ALU.max))
                    link("routing", lc, tt(two, left, over(second), ALU.is_equal))
                    link("routing", lc, tt(two, two, falling_b, ALU.mult))
                    link("routing", lc, red(k2, two, AX.X, ALU.max))
                    link("routing", lc, tt(two, two, over(k2), ALU.is_equal))
                    dve.wait_ge(r_exp, lc + 1)
                    red(total, ex, AX.X, ALU.add)
                    link("routing", lc, tt(one, one, two, ALU.add))

                def part_c():
                    link("routing", lc, tt(one, one, ex, ALU.mult))
                    link("routing", lc, red(both, one, AX.X, ALU.add))
                    link("routing", lc, stt(out=both, in0=total, scalar=1e-12, in1=both, op0=ALU.mult, op1=ALU.max))
                    link("routing", lc, dve.reciprocal(both, both))
                    link("routing", lc, tt(one, one, over(both), ALU.mult))
                    dve.tensor_copy(comb[:, :, 0:E].bitcast(FP32R), one).then_inc(share_hi, 1)
                    dve.wait_ge(share_hi, lc + 1)
                    tt(comb[:, :, E:2 * E], one, comb[:, :, 0:E], ALU.subtract).then_inc(c_made, 1)

                return part_a, part_b, part_c

            def w_halves(w, lb):
                return [w[:, bass.ds(lb * T + n * BANK, BANK)] for n in range(HALVES)]

            uT_halves = [[half(m, n) for n in range(HALVES)] for m in (uT_hi, uT_lo)]

            def batch(place, b, la, lc):
                if la is not None:
                    turn_probs(place, la, 7)
                if lc is not None:
                    route_a, route_b, route_c = route(place, lc)
                    take_out(place, lc)
                project_qk(place, b)
                row_maximum(b, 0)
                if la is None:
                    group_stats(1, B - 1)
                    group_deviation(place, 1, B - 1)
                if lc is not None:
                    norm2_stats(place, lc)
                row_maximum(b, 1)
                if la is not None:
                    residual(place, la, 1)
                    norm1_stats(place, la)
                project_v(place, b)
                if la is None:
                    setup_rest()
                turn_probs(place, b, 0)
                row_maximum(b, 2)
                if la is None:
                    group_affine(2, 1, B - 1)
                turn_probs(place, b, 1)
                row_maximum(b, 3)
                if lc is not None:
                    turn_normed(place, "w", w_halves(wT_hi, lc), w_halves(wT_lo, lc), w_hi_made, lc)
                turn_probs(place, b, 2)
                row_maximum(b, 4)
                if la is not None:
                    turn_normed(place, "u", uT_halves[0], uT_halves[1], u_hi_made, la)
                turn_probs(place, b, 3)
                row_maximum(b, 5)
                if lc is not None:
                    route_a()
                if la is not None:
                    key_maximum(place, la)
                if lc is not None:
                    route_b()
                    route_c()
                if la is not None:
                    key_sums(place, la)
                turn_probs(place, b, 4)
                row_maximum(b, 6)
                turn_probs(place, b, 5)
                row_maximum(b, 7)
                if la is not None:
                    dve.wait_ge(t1b_made, la + 1)
                else:
                    dve.wait_ge(experts_split, 3)
                residual(place, b, 0)
                if la is not None:
                    take(place, "g", gT_s[:, :])
                    take_ctx(place)
                turn_probs(place, b, 6)
                if la is not None:
                    take(place, "m2", m2T_s[:, :])
                    take_m3(place, la)

            batch(FIRST, 0, None, None)
            batch(SECOND, 1, 0, None)
            with dve.Fori(2, B) as b:
                batch(loop_place(b), b, b - 1, b - 2)

            def weigh(m, s):
                dve.wait_ge(e_gelu, m * (2 * E) + s + 1)
                if not (first_batch(m) and s < 2):
                    dve.wait_ge(e_hi, m * (2 * E) + s - 1)
                    dve.wait_ge(e_lo, m * (2 * E) + s - 1)
                dve.tensor_tensor(half(hs, s % 2), half(gel, s % 2), scores[:, 2 + s % 2, :], ALU.mult
                                  ).then_inc(e_mul, 1)

            def lower(m, s):
                dve.wait_ge(e_hi, m * (2 * E) + s + 1)
                if not (first_batch(m) and s < 4):
                    dve.wait_ge(e_y, m * (2 * E) + s - 3)
                dve.tensor_tensor(hs_lo[s % 4], half(hs, s % 2), hs_hi[s % 4].bitcast(FP32),
                                  ALU.subtract).then_inc(e_lo, 1)

            def result(m, h):
                place = y_place(m)
                dve.wait_ge(e_y, m * (2 * E) + (h + 1) * E)
                dve.wait_ge(z_loaded[h], m * 16 + 16)
                if not first_batch(m):
                    dve.wait_ge(stored[h], m * 16)
                dve.tensor_tensor(half(out_s, h), ps(place, f"y{h}"), half(z_in, h), ALU.add
                                  ).then_inc(drained[place.bank(f"y{h}")], 1)

            def experts(m, between):
                weigh(m, 0)
                for s in range(2 * E):
                    if s + 1 < 2 * E:
                        weigh(m, s + 1)
                    lower(m, s)
                    if s == 2 and not first_batch(m):
                        result(m - 1, 1)
                    if s == E + 2:
                        result(m, 0)
                    for step in between.get(s, ()):
                        step()

            la, lc = B - 1, B - 2
            turn_probs(TAIL, la, 7)
            routes, last_routes = route(TAIL, lc), route(END, la)
            take_out(TAIL, lc)
            norm2_stats(TAIL, lc)
            experts(0, gathered(
                (TAIL_AT["OT"], lambda: residual(TAIL, la, 1)),
                (TAIL_AT["OT"], lambda: norm1_stats(TAIL, la)),
                (TAIL_AT["w"], lambda: turn_normed(TAIL, "w", w_halves(wT_hi, lc), w_halves(wT_lo, lc), w_hi_made, lc)),
                (TAIL_AT["lT"], routes[0]),
                (TAIL_AT["u"], lambda: turn_normed(TAIL, "u", uT_halves[0], uT_halves[1], u_hi_made, la)),
                (TAIL_AT["kT"], lambda: key_maximum(TAIL, la)),
                (TAIL_AT["kT"], routes[1]),
                (TAIL_AT["p"], routes[2]),
                (TAIL_AT["p"], lambda: key_sums(TAIL, la)),
                (TAIL_AT["g"], lambda: take(TAIL, "g", gT_s[:, :])),
                (TAIL_AT["ctx"], lambda: take_ctx(TAIL)),
                (TAIL_AT["m2"], lambda: take(TAIL, "m2", m2T_s[:, :])),
                (TAIL_AT["m3"], lambda: take_m3(TAIL, la)),
                (END_AT["o"], lambda: take_out(END, la)),
                (END_AT["o"], lambda: norm2_stats(END, la)),
                (END_AT["w"], lambda: turn_normed(END, "w", w_halves(wT_hi, la), w_halves(wT_lo, la), w_hi_made, la)),
                (END_AT["lT"], last_routes[0]),
                (END_AT["lT"], last_routes[1]),
                (END_AT["lT"], last_routes[2]),
            ))
            with dve.Fori(1, B) as m:
                experts(m, {})
            result(B - 1, 1)

        @block.tensor
        def _(pe):
            passed[pe] = passed_pe
            def open_unit(place, unit):
                if not (isinstance(place.earlier(unit), int) and place.earlier(unit) == 0):
                    pe.wait_ge(drained[place.bank(unit)], place.earlier(unit))
                return ps(place, unit)

            def fill(place, unit, ins):
                ins.then_inc(filled[place.bank(unit)], 1)

            def product3(dst, left, right, start=True, stop=True):
                (lh, ll), (rh, rl) = left, right
                pe.matmul(dst, lh, rh, start=start, stop=False)
                pe.matmul(dst, lh, rl, start=False, stop=False)
                return pe.matmul(dst, ll, rh, start=False, stop=stop)

            def whole(place, unit, left, right):
                fill(place, unit, product3(open_unit(place, unit), left, right))

            def small(place, unit, n, left, right):
                dst = open_unit(place, unit)
                fill(place, unit, pe.matmul(dst[:, 0:n], left, right, start=True, stop=True))

            def turn(place, unit, tiles, rows=P, step=P):
                dst = open_unit(place, unit)
                for j, t in enumerate(tiles):
                    last = pe.transpose(dst[0:t.shape[-1], j * step:j * step + rows], t, ident[0:rows, 0:rows])
                fill(place, unit, last)

            def group_average(place, n, b0, nb):
                pe.wait_ge(gn_mv, n + 1)
                small(place, "gn_mean", nb, group_mean[:, :], gmv[:, b0:b0 + nb, 0])
                pe.wait_ge(gn_mv, n + 2)
                small(place, "gn_var", nb, group_mean[:, :], gsum[:, 1, b0:b0 + nb])

            pe.wait_ge(const_made, 1)
            group_average(SETUP, 0, 0, 1)
            pe.wait_ge(ld_w["wv"], 16)
            turn(SETUP, "wvT", [wv_s[:, :]])
            wait_drained(pe, SETUP, "wvT")
            pe.wait_ge(ld_w["wp"], 16)
            small(SETUP, "wpv", C, wvT[:, :], wp_s[:, :])
            pe.wait_ge(ld_w["cols"], 96)
            small(SETUP, "bias_o", 1, wp_s[:, :], bv_c)
            pe.wait_ge(setup_made, 3)

            def project_qk(place, b):
                for n, (unit, w) in enumerate((("q0", (wq_hi, wq_lo)), ("q1", (wq_hi, wq_lo)),
                                               ("k0", (wk_hi, wk_lo)), ("k1", (wk_hi, wk_lo)))):
                    pe.wait_ge(h_lo_made, b * HALVES + n % 2 + 1)
                    whole(place, unit, [m[:, :] for m in w], (half(h_hi, n % 2), half(h_lo, n % 2)))

            def project_v(place):
                for n in range(HALVES):
                    dst = open_unit(place, f"v{n}")
                    for j in range(QUAD):
                        i = n * QUAD + j
                        last = product3(tile(dst, j), (tile(h_hi, i), tile(h_lo, i)), (wpv_hi[:, :], wpv_lo[:, :]))
                    fill(place, f"v{n}", last)

            def score(b, i):
                if not (isinstance(b, int) and b == 0 and i < 2):
                    pe.wait_ge(s_exp, b * TILES + i - 1)
                for n in range(HALVES):
                    last = product3(scores[:, 2 * (i % 2) + n, :], (tile(q_hi, i), tile(q_lo, i)),
                                    (half(k_hi, n), half(k_lo, n)))
                last.then_inc(s_made, 1)

            def turn_probs(place, b, i):
                pe.wait_ge(s_exp, b * TILES + i + 1)
                for n in range(HALVES):
                    turn(place, f"T{i}" + "ab"[n], [tile(prob[:, i % 2, :], n * QUAD + j) for j in range(QUAD)])

            def attend(place, g, k0, k1):
                unit = f"PV{g}"
                if k0 == 0:
                    open_unit(place, unit)
                    wait_drained(pe, place, f"T{(g + 1) * QUAD - 1}a")
                    wait_drained(pe, place, f"T{(g + 1) * QUAD - 1}b")
                for k in range(k0, k1):
                    last = product3(ps(place, unit), (tile(v_hi, k), tile(v_lo, k)),
                                    (pT_hi[:, k, :], pT_lo[:, k, :]), start=k == 0, stop=k == TILES - 1)
                if k1 == TILES:
                    fill(place, unit, last)

            def turn_o(place, g):
                wait_drained(pe, place, f"PV{g}")
                turn(place, f"OT{g}", [tile(o_s, j) for j in range(QUAD)])

            def turn_x(place, b):
                pe.wait_ge(xb_made, b + 1)
                for n in range(HALVES):
                    turn(place, f"xT{n}", [tile(xb, n * QUAD + j) for j in range(QUAD)])

            def tiles_of(src, n):
                return [src[:, n * QUAD + j, :] for j in range(QUAD)]

            def turn_u(place, lb):
                pe.wait_ge(u_made, lb + 1)
                for n in range(HALVES):
                    turn(place, f"u{n}", tiles_of(u, n))

            def keys(place):
                for n in range(HALVES):
                    wait_drained(pe, place, f"u{n}")
                    whole(place, f"kT{n}", (l1k_hi[:, :], l1k_lo[:, :]), (half(uT_hi, n), half(uT_lo, n)))

            def turn_keys(place):
                for n in range(HALVES):
                    wait_drained(pe, place, f"kT{n}")
                    turn(place, f"p{n}", [tile(p1, n * QUAD + j) for j in range(QUAD)])

            def gather_keys(place):
                wait_drained(pe, place, "p0")
                wait_drained(pe, place, "p1")
                dst = open_unit(place, "g")
                for j in range(TILES):
                    last = pe.matmul(dst[:, 0:C], u[:, j, :], p1T[:, j, :], start=j == 0, stop=j == TILES - 1)
                fill(place, "g", last)

            def context(place):
                wait_drained(pe, place, "g")
                small(place, "ctx", C, gT_s[:, :], wqkv_s[:, 2 * C:3 * C])

            def merge2(place):
                wait_drained(pe, place, "ctx")
                small(place, "m2", C, ctx_s[:, :], l1qT[:, :])

            def merge3(place):
                wait_drained(pe, place, "m2")
                small(place, "m3", C, m2T_s[:, :], wout_s[:, :])

            def linear_out(place, lb):
                pe.wait_ge(m3_lo_made, lb + 1)
                for n in range(HALVES):
                    dst = open_unit(place, f"o{n}")
                    for j in range(QUAD):
                        i = n * QUAD + j
                        last = product3(tile(dst, j), (tile(uT_hi, i), tile(uT_lo, i)), (m3_hi[:, :], m3_lo[:, :]))
                    fill(place, f"o{n}", last)

            def turn_w(place, lb):
                pe.wait_ge(w_made, lb + 1)
                for n in range(HALVES):
                    turn(place, f"w{n}", tiles_of(w_n, n))

            def w_of(lb, n):
                return [m[:, bass.ds(lb * T + n * BANK, BANK)] for m in (wT_hi, wT_lo)]

            def logits(place, lb):
                for n in range(HALVES):
                    wait_drained(pe, place, f"w{n}")
                    whole(place, f"lg{n}", (rt_hi[:, :], rt_lo[:, :]), w_of(lb, n))

            def turn_logits(place):
                wait_drained(pe, place, "lg0")
                wait_drained(pe, place, "lg1")
                dst = open_unit(place, "lT")
                apart(pe)
                for j in range(TILES):
                    last = pe.transpose(dst[:, j * E:(j + 1) * E], tile(lgT, j), ident[0:E, 0:E])
                fill(place, "lT", last)

            def turn_z(place, lb):
                pe.wait_ge(z_made, lb + 1)
                for n in range(HALVES):
                    turn(place, f"z{n}", tiles_of(t2, n))

            def turn_comb(place, lb):
                pe.wait_ge(c_made, lb + 1)
                for n in range(HALVES):
                    turn(place, f"c{n}", tiles_of(comb, n))

            def batch(place, b, la, lc):
                if la is not None:
                    turn_probs(place, la, 7)
                if lc is not None:
                    linear_out(place, lc)
                project_qk(place, b)
                if la is not None:
                    attend(place, 1, 0, QUAD)
                for unit in ATTENTION["qk"]:
                    wait_drained(pe, place, unit)
                score(b, 0)
                if la is None:
                    group_average(place, 2, 1, B - 1)
                else:
                    attend(place, 1, QUAD, TILES)
                score(b, 1)
                if la is not None:
                    turn_o(place, 1)
                project_v(place)
                if la is None:
                    pe.wait_ge(ld_w["qkv"], 16)
                    turn(place, "l1qT", [wqkv_s[:, 0:C]])
                    pe.wait_ge(ld_w["rows8"], 32)
                    turn(place, "routerT", [rows8[:, 0, :]], rows=E)
                    turn(place, "b1T", [rows8[:, 1, :]], rows=E)
                turn_probs(place, b, 0)
                score(b, 2)
                turn_x(place, b)
                turn_probs(place, b, 1)
                score(b, 3)
                if lc is not None:
                    turn_w(place, lc)
                turn_probs(place, b, 2)
                score(b, 4)
                if la is not None:
                    turn_u(place, la)
                if lc is not None:
                    logits(place, lc)
                turn_probs(place, b, 3)
                score(b, 5)
                if lc is not None:
                    turn_logits(place)
                if la is not None:
                    keys(place)
                if lc is not None:
                    turn_z(place, lc)
                for n in range(HALVES):
                    wait_drained(pe, place, f"v{n}")
                attend(place, 0, 0, TILES)
                turn_probs(place, b, 4)
                score(b, 6)
                if la is not None:
                    turn_keys(place)
                turn_probs(place, b, 5)
                score(b, 7)
                turn_o(place, 0)
                if la is not None:
                    gather_keys(place)
                    context(place)
                turn_probs(place, b, 6)
                if la is not None:
                    merge2(place)
                if lc is not None:
                    turn_comb(place, lc)
                if la is not None:
                    merge3(place)

            batch(FIRST, 0, None, None)
            batch(SECOND, 1, 0, None)
            with pe.Fori(2, B) as b:
                batch(loop_place(b), b, b - 1, b - 2)

            def hidden(m, s):
                h, e = s // E, s % E
                if first_batch(m) and s < 2:
                    pe.wait_ge(s_exp, B * TILES)
                else:
                    pe.wait_ge(e_gelu, m * (2 * E) + s - 1)
                    pe.wait_ge(e_mul, m * (2 * E) + s - 1)
                product3(scores[:, s % 2, :], (tile(w1_hi, e), tile(w1_lo, e)), w_of(m, h))
                pe.wait_ge(c_loaded[h], m * 16 + 16)
                pe.matmul(scores[:, 2 + s % 2, :], pick[:, e, :], cb_in[:, h, :], start=True, stop=True
                          ).then_inc(e_h, 1)

            def outward(m, s):
                h, e = s // E, s % E
                place = y_place(m)
                dst = ps(place, f"y{h}")
                if e == 0:
                    open_unit(place, f"y{h}")
                    pe.matmul(dst, b2_hi[:, :], cb_in[:, h, :], start=True, stop=False)
                    pe.matmul(dst, b2_lo[:, :], cb_in[:, h, :], start=False, stop=False)
                pe.wait_ge(e_lo, m * (2 * E) + s + 1)
                last = product3(dst, (tile(w2_hi, e), tile(w2_lo, e)), (hs_hi[s % 4], hs_lo[s % 4]),
                                start=False, stop=e == E - 1)
                last.then_inc(e_y, 1)

            def experts(m, last, between):
                for s in range(2 * E):
                    if s + 2 < 2 * E:
                        hidden(m, s + 2)
                    elif not last:
                        hidden(m + 1, s + 2 - 2 * E)
                    if s > 0:
                        outward(m, s - 1)
                    elif not first_batch(m):
                        outward(m - 1, 2 * E - 1)
                    for step in between.get(s, ()):
                        step()

            la, lc = B - 1, B - 2
            turn_probs(TAIL, la, 7)
            linear_out(TAIL, lc)
            pe.wait_ge(experts_split, 3)
            pe.wait_ge(mask_made, 1)
            hidden(0, 0)
            hidden(0, 1)
            attend(TAIL, 1, 0, TILES)
            experts(0, False, gathered(
                (TAIL_AT["OT"], lambda: turn_o(TAIL, 1)),
                (TAIL_AT["w"], lambda: turn_w(TAIL, lc)),
                (TAIL_AT["lg"], lambda: logits(TAIL, lc)),
                (TAIL_AT["lT"], lambda: turn_logits(TAIL)),
                (TAIL_AT["u"], lambda: turn_u(TAIL, la)),
                (TAIL_AT["z"], lambda: turn_z(TAIL, lc)),
                (TAIL_AT["kT"], lambda: keys(TAIL)),
                (TAIL_AT["p"], lambda: turn_keys(TAIL)),
                (TAIL_AT["g"], lambda: gather_keys(TAIL)),
                (TAIL_AT["c"], lambda: turn_comb(TAIL, lc)),
                (TAIL_AT["ctx"], lambda: context(TAIL)),
                (TAIL_AT["m2"], lambda: merge2(TAIL)),
                (TAIL_AT["m3"], lambda: merge3(TAIL)),
                (END_AT["o"], lambda: linear_out(END, la)),
                (END_AT["w"], lambda: turn_w(END, la)),
                (END_AT["lg"], lambda: logits(END, la)),
                (END_AT["lT"], lambda: turn_logits(END)),
                (END_AT["z"], lambda: turn_z(END, la)),
                (END_AT["c"], lambda: turn_comb(END, la)),
            ))
            with pe.Fori(1, B - 1) as m:
                experts(m, False, {})
            experts(B - 1, True, {})
            outward(B - 1, 2 * E - 1)


_INS = ['x', 'L0_conv_gn_scale', 'L0_conv_gn_bias', 'L0_conv_Wq', 'L0_conv_bq', 'L0_conv_Wk', 'L0_conv_bk',
        'L0_conv_Wv', 'L0_conv_bv', 'L0_conv_Wp', 'L0_conv_bp', 'L1_attn_W_qkv', 'L1_attn_W_out',
        'L1_attn_b_out', 'L1_ffn_router_w', 'L1_ffn_w1', 'L1_ffn_b1', 'L1_ffn_w2', 'L1_ffn_b2']


def kernel(**inputs):
    import numpy as _np
    import concourse.bacc as _bacc
    from concourse import mybir as _mybir
    from concourse.bass_utils import run_bass_kernel_spmd as _run

    nc = _bacc.Bacc("TRN2", target_bir_lowering=False, num_devices=1)
    arrays, args = {}, []
    for name in _INS:
        a = _np.ascontiguousarray(inputs[name])
        arrays[f"in_{name}_dram"] = a
        args.append(nc.dram_tensor(f"in_{name}_dram", a.shape, _mybir.dt.from_np(a.dtype), kind="ExternalInput").ap())
    o = nc.dram_tensor("out_0_dram", (4, 128, 32, 32), _mybir.dt.float32, kind="ExternalOutput").ap()
    conv_attention_moe(nc, *args, o)
    r = _run(nc, [arrays], core_ids=[0])
    return r.results[0]["out_0_dram"]
```

```python
from contextlib import ExitStack

import concourse.bass as bass
from concourse import mybir

FP32 = mybir.dt.float32
FP32R = mybir.dt.float32r
ALU = mybir.AluOpType
ACT = mybir.ActivationFunctionType
AX = mybir.AxisListType

B, C, T = 4, 128, 1024
GROUP = C // 32
HEADS, HEAD = 4, 32
E = 8
P = 128
BANK = 512
TILES = T // P
QUAD = BANK // P
HALVES = T // BANK
SCALE = float(C) ** -0.5
GN_EPS, LN_EPS = 1e-6, 1e-5

SETUP_UNITS = ["gn_mean", "gn_var", "wvT", "wpv", "bias_o"]
ATTENTION = dict(
    qk=["q0", "k0", "k1", "q1"], v=["v0", "v1"], xT=["xT0", "xT1"],
    T=[[f"T{i}a", f"T{i}b"] for i in range(TILES)],
)
LINEAR = dict(u=["u0", "u1"], kT=["kT0", "kT1"], p=["p0", "p1"])
ROUTING = dict(o=["o0", "o1"], w=["w0", "w1"], lg=["lg0", "lg1"], z=["z0", "z1"], c=["c0", "c1"])


def attention_units(linear, routing):
    T, L, R = ATTENTION["T"], linear, routing
    return (
        T[6] * L + ["ctx"] * R + ["q0"] + T[7] * L + ["m2"] * R + ["k0", "k1"] + ["m3"] * R + ["q1"]
        + ["PV1"] * L + ROUTING["o"] * R + ["OT1"] * L + ATTENTION["v"]
        + ["gn_mean", "l1qT", "routerT", "b1T", "gn_var"] * (not L) + T[0]
        + T[1] + ATTENTION["xT"]
        + ROUTING["w"] * R + T[2]
        + ROUTING["lg"] * R + T[3] + LINEAR["u"] * L
        + ["lT"] * R + ROUTING["z"] * R + LINEAR["kT"] * L + ["PV0"] + T[4]
        + LINEAR["p"] * L + ROUTING["c"] * R + T[5]
        + ["g"] * L + ["OT0"]
    )


TAIL_UNITS = (ATTENTION["T"][6] + ["ctx"] + ATTENTION["T"][7] + ["m2", "m3", "PV1"] + ROUTING["o"]
              + ["OT1"] + ROUTING["w"] + ROUTING["lg"] + LINEAR["u"] + ["lT"] + ROUTING["z"]
              + LINEAR["kT"] + LINEAR["p"] + ["g"] + ROUTING["c"])
END_UNITS = (["ctx", "m2", "m3"] + ROUTING["o"] + ROUTING["w"] + ROUTING["lg"] + ["lT"]
             + ROUTING["z"] + ROUTING["c"])
TAIL_AT = dict(m3=0, PV=1, o=2, OT=5, w=6, lg=8, u=10, lT=11, z=12, kT=12, exp=12, p=13, g=14, c=15)
END_AT = dict(ctx=16, m2=17, m3=18, o=20, w=25, lg=27, lT=27, z=28, exp=27, c=31)
LINEAR_CHAIN, ROUTING_CHAIN = 5, 17


class Place:

    def __init__(self, banks, before):
        self.banks, self.before = banks, before

    def bank(self, unit):
        return self.banks[unit][0]

    def earlier(self, unit):
        bank, n = self.banks[unit]
        return self.before[bank] + n


def place_of(units, before, first=0, wide=None):
    count, found, turn = list(before), {}, first
    for n, unit in enumerate(units):
        if wide is not None and n >= wide:
            turn %= 2
        shared = unit == "OT1" and wide is None
        bank = found["PV1"][0] if shared else turn % 4
        found[unit] = (bank, count[bank] - before[bank])
        count[bank] += 1
        turn += not shared
    return Place(found, before), count, turn


def conv_attention_moe(nc, x, gn_scale, gn_bias, wq, bq, wk, bk, wv, bv, wp, bp,
                       w_qkv, w_out, b_out, router, w1, b1, w2, b2, out):
    SETUP, before, turn = place_of(SETUP_UNITS, [0] * 4)
    FIRST, before, turn = place_of(attention_units(0, 0), before, turn)
    SECOND, before, turn = place_of(attention_units(1, 0), before, turn)
    LOOP, after_one, after_turn = place_of(attention_units(1, 1), before, turn)
    assert after_turn % 4 == turn % 4
    loops = [n - k for n, k in zip(after_one, before)]

    def loop_place(b):
        return Place(LOOP.banks, [n + (b - 2) * k for n, k in zip(before, loops)])

    TAIL, tail_end, turn = place_of(TAIL_UNITS, [n + (B - 2) * k for n, k in zip(before, loops)],
                                    turn, TAIL_UNITS.index("OT1"))
    END, _, _ = place_of(END_UNITS, tail_end, turn, 0)

    def y_place(m):
        return Place({"y0": (2, 0), "y1": (3, 0)}, [tail_end[k] + m for k in range(4)])

    scratch_z = nc.dram_tensor("scratch_z", (B * HALVES, C, BANK), FP32).ap()
    scratch_c = nc.dram_tensor("scratch_c", (B * HALVES, 2 * E, BANK), FP32).ap()
    x_v = x.rearrange("b c h w -> b c (h w)")
    out_v = out.rearrange("b c h w -> b c (h w)")

    ctx = ExitStack()
    with ctx:
        def sb(name, shape, dt=FP32):
            return ctx.enter_context(nc.sbuf_tensor(name, shape, dt))

        def sem(name):
            return ctx.enter_context(nc.semaphore(name))

        ident = sb("ident", [P, P])
        group_mean = sb("group_mean", [C, C])
        head_mask = sb("head_mask", [C, C])
        minus_half = sb("minus_half", [P, TILES])
        falling = sb("falling", [P, E])
        wout_s = sb("wout_s", [C, C])
        wqkv_s = sb("wqkv_s", [C, 3 * C])
        l1qT = sb("l1qT", [C, C])
        wq_hi, wq_lo, wk_hi, wk_lo, wpv_hi, wpv_lo, l1k_hi, l1k_lo, rt_hi, rt_lo = (
            sb(n, [C, C], FP32R) for n in ("wq_hi", "wq_lo", "wk_hi", "wk_lo", "wpv_hi", "wpv_lo",
                                           "l1k_hi", "l1k_lo", "rt_hi", "rt_lo"))
        bout_row = sb("bout_row", [P, C])
        cols = sb("cols", [C, 8])
        bq_c, bk_c, bv_c, bp_c, gs_c, gb_c, bias_o = (cols[:, i:i + 1] for i in range(7))
        b1_c = sb("b1_c", [C, E])
        b2_s = sb("b2_s", [2 * E, C])
        b2_hi, b2_lo = sb("b2_hi", [2 * E, C], FP32R), sb("b2_lo", [2 * E, C], FP32R)
        pick = sb("pick", [2 * E, E, P], FP32R)
        w1_hi, w1_lo, w2_hi, w2_lo = (sb(n, [C, E * C], FP32R) for n in
                                      ("w1_hi", "w1_lo", "w2_hi", "w2_lo"))
        h_f = sb("h_f", [C, T])
        h_hi, h_lo = sb("h_hi", [C, T], FP32R), sb("h_lo", [C, T], FP32R)
        xb = sb("xb", [C, T])
        q_hi, q_lo, k_hi, k_lo = (sb(n, [C, T], FP32R) for n in ("q_hi", "q_lo", "k_hi", "k_lo"))
        v_hi, v_lo = sb("v_hi", [P, TILES * C], FP32R), sb("v_lo", [P, TILES * C], FP32R)
        prob = sb("prob", [P, 2, T])
        pT_hi = sb("pT_hi", [P, TILES, BANK], FP32R)
        pT_lo = sb("pT_lo", [P, TILES, BANK], FP32R)
        o_s = sb("o_s", [C, BANK])
        xT = sb("xT", [P, TILES, C])
        t1 = sb("t1", [P, TILES, C])
        t2 = sb("t2", [P, TILES, C])
        u = sb("u", [P, TILES, C])
        uT_hi, uT_lo = sb("uT_hi", [C, T], FP32R), sb("uT_lo", [C, T], FP32R)
        p1 = sb("p1", [C, T])
        p1T = sb("p1T", [P, TILES, C])
        w_n = sb("w_n", [P, TILES, C])
        gT_s, ctx_s, m2T_s = (sb(n, [C, C]) for n in ("gT_s", "ctx_s", "m2T_s"))
        m3_hi, m3_lo = sb("m3_hi", [C, C], FP32R), sb("m3_lo", [C, C], FP32R)
        wT_hi, wT_lo = sb("wT_hi", [C, B * T], FP32R), sb("wT_lo", [C, B * T], FP32R)
        gst = sb("gst", [C, B, HALVES, 6])
        gmv = sb("gmv", [C, B, 2])
        gsum = sb("gsum", [C, 4, B])
        gmul, gadd = sb("gmul", [C, B]), sb("gadd", [C, B])
        affine = sb("affine", [C, 2])
        row_max = sb("row_max", [P, TILES])
        row_sum = sb("row_sum", [P, 2, TILES])
        lst = sb("lst", [P, TILES, 6])
        lmv = [sb(f"lmv{n}", [P, TILES, 2]) for n in range(2)]
        rstd = [sb(f"rstd{n}", [P, 3, TILES]) for n in range(2)]
        kst = sb("kst", [C, 8])
        rt = sb("rt", [P, 5, TILES, E])
        rr = sb("rr", [P, 6, TILES])
        comb = sb("comb", [P, TILES, 2 * E])
        gel, hs, out_s, z_in = (sb(n, [C, T]) for n in ("gel", "hs", "out_s", "z_in"))
        cb_in = sb("cb_in", [2 * E, HALVES, BANK], FP32R)
        wq_raw, wk_raw, wq_sc = (p1T[:, i, :] for i in range(3))
        rows8 = p1T[0:E, 3:5, :]
        wv_s, wp_s, wvT = gT_s, ctx_s, m2T_s
        w1_raw, w2_raw = t1[:, :, :].rearrange("p a b -> p (a b)"), u[:, :, :].rearrange("p a b -> p (a b)")
        pick_raw = w_n[0:2 * E, :, :].rearrange("p a b -> p (a b)")
        lgT = p1[0:E, :]
        hs_hi = [m[:, n * BANK:(n + 1) * BANK] for m in (h_hi, q_hi) for n in range(2)]
        hs_lo = [m[:, n * BANK:(n + 1) * BANK] for m in (h_lo, q_lo) for n in range(2)]
        x_of = [xb, gel, hs, out_s]
        zT_early, cT_early = out_s[:, :], z_in[0:2 * E, :]
        zT_late, cT_late = xb[:, :], h_f[0:2 * E, :]

        scores = ctx.enter_context(nc.psum_tensor("scores", [P, 4, BANK], FP32))
        ring = ctx.enter_context(nc.psum_tensor("ring", [P, 4, BANK], FP32))

        filled = [sem(f"filled{k}") for k in range(4)]
        drained = [sem(f"drained{k}") for k in range(4)]
        ld_x = [sem(f"ld_x{b}") for b in range(B)]
        ld_x0b = sem("ld_x0b")
        ld_w = {n: sem(f"ld_{n}") for n in ("wq", "wk", "wv", "wp", "gn", "cols", "qkv", "wout", "bout",
                                            "rows8", "b2", "w1", "w2")}
        const_made = sem("const_made")
        mask_made = sem("mask_made")
        experts_split = sem("experts_split")
        setup_made = sem("setup_made")
        pool_chain = sem("pool_chain")
        dve_chain = sem("dve_chain")
        gn_mv = sem("gn_mv")
        gn_rstd = sem("gn_rstd")
        gn_made = sem("gn_made")
        g_made = sem("g_made")
        h_made, xb_made = sem("h_made"), sem("xb_made")
        h_hi_made, h_lo_made = sem("h_hi_made"), sem("h_lo_made")
        affine_made, share_hi = sem("affine_made"), sem("share_hi")
        x_again = sem("x_again")
        passed_dve, passed_pe, passed_pool, passed_sp = (
            sem(f"passed_{e}") for e in ("dve", "pe", "pool", "sp"))
        xb_read = sem("xb_read")
        s_made, s_max, s_exp = sem("s_made"), sem("s_max"), sem("s_exp")
        qk_hi_made, v_hi_made, p_hi_made = sem("qk_hi_made"), sem("v_hi_made"), sem("p_hi_made")
        u_hi_made, m3_hi_made, w_hi_made = sem("u_hi_made"), sem("m3_hi_made"), sem("w_hi_made")
        r_made = sem("r_made")
        linear_chain, routing_chain = sem("linear_chain"), sem("routing_chain")
        ln_stats = [sem(f"ln_stats{n}") for n in range(2)]
        ln_small = [sem(f"ln_small{n}") for n in range(2)]
        u_made, w_made, z_made, t1b_made = sem("u_made"), sem("w_made"), sem("z_made"), sem("t1b_made")
        k_max, r_exp, c_made = sem("k_max"), sem("r_exp"), sem("c_made")
        z_stored, c_stored = sem("z_stored"), sem("c_stored")
        z_loaded = [sem(f"z_loaded{h}") for h in range(HALVES)]
        c_loaded = [sem(f"c_loaded{h}") for h in range(HALVES)]
        e_h, e_gelu, e_mul, e_hi, e_lo, e_y = (sem(n) for n in
                                               ("e_h", "e_gelu", "e_mul", "e_hi", "e_lo", "e_y"))
        stored = [sem(f"stored{h}") for h in range(HALVES)]

        bqs_c = cols[:, 7:8]
        block = ctx.enter_context(nc.Block())
        passed = {}

        def gathered(*steps):
            found = {}
            for at, step in steps:
                found.setdefault(at, []).append(step)
            return found

        def between_steps(steps, m, s):
            for step in steps.get(m * 2 * E + s, ()) if steps else ():
                step()

        def first_batch(m):
            return isinstance(m, int) and m == 0

        def as_tiles(m):
            return m.rearrange("p (j t) -> p j t", j=QUAD)

        def tile_group(m, n, i):
            return m[:, n * QUAD:(n + 1) * QUAD, (i % QUAD) * P:(i % QUAD + 1) * P]

        def ps(place, unit):
            return ring[:, place.bank(unit), :]

        def wait_filled(eng, place, unit):
            eng.wait_ge(filled[place.bank(unit)], place.earlier(unit) + 1)

        def wait_drained(eng, place, unit):
            eng.wait_ge(drained[place.bank(unit)], place.earlier(unit) + 1)

        def apart(eng):
            eng.sem_inc(passed[eng], 1)

        def tile(m, j):
            return m[:, j * P:(j + 1) * P]

        def half(m, n):
            return m[:, n * BANK:(n + 1) * BANK]

        @block.sync
        def _(sp):
            passed[sp] = passed_sp
            sp.dma_start(half(xb, 0), x_v[0, :, 0:BANK]).then_inc(ld_x[0], 16)
            for i, v in ((4, gn_scale), (5, gn_bias)):
                sp.dma_start(cols[:, i:i + 1], v.rearrange("(c a) -> c a", a=1)).then_inc(ld_w["gn"], 16)
            sp.dma_start(wk_raw, wk).then_inc(ld_w["wk"], 16)
            sp.dma_start(wv_s[:, :], wv).then_inc(ld_w["wv"], 16)
            sp.dma_start(wp_s[:, :], wp).then_inc(ld_w["wp"], 16)
            sp.dma_start(wqkv_s[:, :], w_qkv).then_inc(ld_w["qkv"], 16)
            for b in range(1, B):
                sp.dma_start(x_of[b][:, :], x_v[b]).then_inc(ld_x[b], 16)
            sp.dma_start(rows8[:, 0, :], router).then_inc(ld_w["rows8"], 16)
            sp.dma_start(rows8[:, 1, :], b1).then_inc(ld_w["rows8"], 16)
            for n in range(2):
                sp.dma_start(b2_s[n * E:(n + 1) * E, :], b2).then_inc(ld_w["b2"], 16)
            sp.dma_start(w1_raw.rearrange("p (e f) -> p e f", e=E),
                         w1.rearrange("e c f -> c e f")).then_inc(ld_w["w1"], 16)
            sp.dma_start(w2_raw.rearrange("p (e f) -> p e f", e=E),
                         w2.rearrange("e c f -> c e f")).then_inc(ld_w["w2"], 16)
            sp.dma_start(wout_s[:, :], w_out).then_inc(ld_w["wout"], 16)
            sp.dma_start(bout_row[:, :], b_out.rearrange("(a c) -> a c", a=1).to_broadcast([P, C])
                         ).then_inc(ld_w["bout"], 16)

            def store_residual(place, lc, zT):
                for unit in ROUTING["z"]:
                    wait_drained(sp, place, unit)
                    apart(sp)
                sp.dma_start(scratch_z[bass.ds(lc * HALVES, HALVES)].rearrange("h c t -> c h t"),
                             zT.rearrange("c (h t) -> c h t", h=HALVES)).then_inc(z_stored, 16)

            def store_shares(place, lc, cT):
                for unit in ROUTING["c"]:
                    wait_drained(sp, place, unit)
                    apart(sp)
                sp.dma_start(scratch_c[bass.ds(lc * HALVES, HALVES)].rearrange("h c t -> c h t"),
                             cT.rearrange("c (h t) -> c h t", h=HALVES)).then_inc(c_stored, 16)

            def load_x(b):
                sp.wait_ge(xb_read, b)
                apart(sp)
                sp.dma_start(xb[:, :], x_v[b]).then_inc(x_again, 16)

            def load_routed(m, h):
                sp.wait_ge(z_stored, 16 * (m + 2))
                apart(sp)
                sp.wait_ge(c_stored, 16 * (m + 2))
                apart(sp)
                sp.dma_start(half(z_in, h), scratch_z[m * HALVES + h]).then_inc(z_loaded[h], 16)
                sp.dma_start(cb_in[:, h, :].bitcast(FP32), scratch_c[m * HALVES + h]).then_inc(c_loaded[h], 16)

            sp.sem_inc(z_stored, 16)
            sp.sem_inc(c_stored, 16)
            load_x(1)
            load_x(2)
            with sp.Fori(2, B - 1) as b:
                load_x(b + 1)
                store_residual(loop_place(b), b - 2, zT_early)
                store_shares(loop_place(b), b - 2, cT_early)
            store_residual(loop_place(B - 1), B - 3, zT_early)
            store_shares(loop_place(B - 1), B - 3, cT_early)
            sp.wait_ge(c_stored, 16 * (B - 1))
            for h in range(HALVES):
                load_routed(0, h)

            def result(m, h, more):
                wait_drained(sp, y_place(m), f"y{h}")
                apart(sp)
                sp.dma_start(out_v[m, :, h * BANK:(h + 1) * BANK], half(out_s, h)).then_inc(stored[h], 16)
                if more:
                    load_routed(m + 1, h)

            sp.wait_ge(xb_read, B)
            store_residual(TAIL, B - 2, zT_late)
            result(0, 0, True)
            store_shares(TAIL, B - 2, cT_late)
            result(0, 1, True)
            store_residual(END, B - 1, zT_late)
            result(1, 0, True)
            store_shares(END, B - 1, cT_late)
            result(1, 1, True)
            with sp.Fori(2, B - 1) as m:
                for h in range(HALVES):
                    result(m, h, True)
            for h in range(HALVES):
                result(B - 1, h, False)
            for h in range(HALVES):
                sp.wait_ge(stored[h], 16 * B)

        @block.gpsimd
        def _(pool):
            passed[pool] = passed_pool
            made = [0]

            def after(ins):
                made[0] += 1
                ins.then_inc(pool_chain, 1)
                pool.wait_ge(pool_chain, made[0])

            bout_b = bout_row[:, :].unsqueeze(1).to_broadcast([P, TILES, C])
            pool.memset(group_mean[:, :], 1.0 / GROUP)
            pool.memset(minus_half[:, :], -0.5)
            after(pool.memset(ident[:, :], 0.0))
            after(pool.affine_select(out=ident[:, :], in_=ident[:, :], compare_op=ALU.not_equal, fill=1.0,
                                     base=0, pattern=[[-1, P]], channel_multiplier=1))
            g_v = group_mean[:, :].rearrange("p (g c) -> p g c", c=GROUP)
            after(pool.affine_select(out=g_v, in_=g_v, compare_op=ALU.is_ge, fill=0.0, base=0,
                                     pattern=[[-GROUP, C // GROUP], [0, GROUP]], channel_multiplier=1))
            pool.affine_select(out=g_v, in_=g_v, compare_op=ALU.is_ge, fill=0.0, base=GROUP - 1,
                               pattern=[[GROUP, C // GROUP], [0, GROUP]],
                               channel_multiplier=-1).then_inc(const_made, 1)

            def group_rstd(place, b0, nb):
                wait_drained(pool, place, "gn_var")
                after(pool.tensor_scalar(gsum[:, 3, b0:b0 + nb], gsum[:, 2, b0:b0 + nb],
                                         1.0, GN_EPS, ALU.mult, ALU.add))
                pool.tensor_tensor(gsum[:, 3, b0:b0 + nb], gsum[:, 3, b0:b0 + nb],
                                   minus_half[:, 0:nb], ALU.pow).then_inc(gn_rstd, 1)

            def affine_of(b):
                pool.tensor_copy(affine[:, 0:1], gmul[:, bass.ds(b, 1)])
                pool.tensor_copy(affine[:, 1:2], gadd[:, bass.ds(b, 1)]).then_inc(affine_made, 1)
                pool.wait_ge(affine_made, b + 1)
                apart(pool)

            def norm_x(b):
                affine_of(b)
                pool.tensor_scalar(h_f[:, :], xb[:, :], affine[:, 0:1], affine[:, 1:2], ALU.mult, ALU.add)
                pool.tensor_scalar(h_hi[:, :], xb[:, :], affine[:, 0:1], affine[:, 1:2],
                                   ALU.mult, ALU.add).then_inc(h_made, 1)
                pool.wait_ge(h_made, b + 1)
                apart(pool)
                for n in range(HALVES):
                    pool.tensor_tensor(half(h_lo, n), half(h_f, n), half(h_hi, n).bitcast(FP32), ALU.subtract
                                       ).then_inc(h_lo_made, 1)

            def add_bias(b):
                pool.tensor_scalar(xb[:, :], xb[:, :], 1.0, bias_o, ALU.mult, ALU.add).then_inc(xb_made, 1)

            def layer_norm(n, lb, src, dst, ready):
                eps, std, neg = (rstd[n][:, i, :] for i in range(3))
                pool.wait_ge(ln_stats[n], lb + 1)
                apart(pool)
                pool.tensor_scalar(eps, lmv[n][:, :, 1], 1.0, LN_EPS, ALU.mult, ALU.add
                                   ).then_inc(ln_small[n], 1)
                pool.tensor_scalar(neg, lmv[n][:, :, 0], -1.0, 0.0, ALU.mult, ALU.add)
                pool.wait_ge(ln_small[n], lb * 2 + 1)
                pool.tensor_tensor(std, eps, minus_half[:, :], ALU.pow).then_inc(ln_small[n], 1)
                pool.wait_ge(ln_small[n], lb * 2 + 2)
                apart(pool)
                for j in range(TILES):
                    last = pool.tensor_scalar(dst[:, j, :], src[:, j, :], neg[:, j:j + 1], std[:, j:j + 1],
                                              ALU.add, ALU.mult)
                    if j % QUAD == QUAD - 1:
                        last.then_inc(ready, 1)

            def second_norm(lc):
                layer_norm(1, lc, t2, w_n, w_made)

            def normed_residual(lc):
                pool.wait_ge(w_made, lc * HALVES + HALVES)
                pool.tensor_tensor(t2[:, :, :], t2[:, :, :], w_n[:, :, :], ALU.add).then_inc(z_made, 1)

            def first_norm(lb):
                layer_norm(0, lb, t1, u, u_made)

            def add_bout(lb, routed):
                if routed is not None:
                    wait_filled(pool, routed, "z1")
                pool.tensor_tensor(t2[:, :, :], t1[:, :, :], bout_b, ALU.add).then_inc(t1b_made, 1)

            group_rstd(SETUP, 0, 1)
            pool.wait_ge(gn_made, 1)
            pool.sem_inc(h_made, 1)
            pool.sem_inc(affine_made, 1)
            after(pool.memset(head_mask[:, :], float(HEAD) ** -0.5))
            m_v = head_mask[:, :].rearrange("p (g c) -> p g c", c=HEAD)
            after(pool.affine_select(out=m_v, in_=m_v, compare_op=ALU.is_ge, fill=0.0, base=0,
                                     pattern=[[-HEAD, HEADS], [0, HEAD]], channel_multiplier=1))
            after(pool.affine_select(out=m_v, in_=m_v, compare_op=ALU.is_ge, fill=0.0, base=HEAD - 1,
                                     pattern=[[HEAD, HEADS], [0, HEAD]], channel_multiplier=-1))
            for e in range(E):
                pool.memset(falling[:, e:e + 1], float(E - e))
            p_v = pick_raw.rearrange("p (e t) -> p e t", e=E)
            after(pool.memset(pick_raw, 0.0))
            for base in (0, -E):
                after(pool.affine_select(out=p_v, in_=p_v, compare_op=ALU.not_equal, fill=1.0, base=base,
                                         pattern=[[-1, E], [0, P]], channel_multiplier=1))
            pool.tensor_scalar(pick[:, :, :], p_v, 1.0, 0.0, ALU.mult, ALU.add).then_inc(mask_made, 1)
            wait_drained(pool, SETUP, "bias_o")
            add_bias(0)
            for n, (name, raw, hi, lo) in enumerate((("w1", w1_raw, w1_hi, w1_lo),
                                                    ("w2", w2_raw, w2_hi, w2_lo),
                                                    ("b2", b2_s[:, :], b2_hi, b2_lo))):
                pool.wait_ge(ld_w[name], 32 if name == "b2" else 16)
                after(pool.tensor_scalar(hi[:, :], raw, 1.0, 0.0, ALU.mult, ALU.add))
                pool.tensor_tensor(lo[:, :], raw, hi[:, :].bitcast(FP32), ALU.subtract
                                   ).then_inc(experts_split, 1)
                if name == "w1":
                    group_rstd(FIRST, 1, B - 1)
            pool.wait_ge(gn_made, 2)
            pool.wait_ge(ld_w["bout"], 16)

            def batch(place, b, la, lc):
                pool.wait_ge(x_again, b * 16)
                apart(pool)
                norm_x(b)
                add_bias(b)
                if lc is not None:
                    second_norm(lc)
                    normed_residual(lc)
                first_norm(la)
                add_bout(la, place if lc is not None else None)

            batch(SECOND, 1, 0, None)
            with pool.Fori(2, B) as b:
                batch(loop_place(b), b, b - 1, b - 2)
            second_norm(B - 2)
            normed_residual(B - 2)
            first_norm(B - 1)
            add_bout(B - 1, TAIL)
            second_norm(B - 1)
            normed_residual(B - 1)

        @block.scalar
        def _(act):
            act.dma_start(half(xb, 1), x_v[0, :, BANK:T]).then_inc(ld_x0b, 16)
            act.dma_start(wq_raw, wq).then_inc(ld_w["wq"], 16)
            for i, v in enumerate((bq, bk, bv, bp)):
                act.dma_start(cols[:, i:i + 1], v.rearrange("(c a) -> c a", a=1)).then_inc(ld_w["cols"], 16)

            def split_first():
                act.wait_ge(gn_made, 1)
                for n in range(HALVES):
                    act.activation(half(h_hi, n), half(xb, n), ACT.Identity, bias=gadd[:, 0:1],
                                   scale=gmul[:, 0:1]).then_inc(h_hi_made, 1)

            def project(place, unit, hi, bias):
                wait_filled(act, place, unit)
                act.activation(half(hi, int(unit[1])), ps(place, unit), ACT.Identity, bias=bias
                               ).then_inc(qk_hi_made, 1)

            def project_v(place):
                for n in range(HALVES):
                    wait_filled(act, place, f"v{n}")
                    act.activation(half(v_hi, n), ps(place, f"v{n}"), ACT.Copy).then_inc(v_hi_made, 1)

            def softmax(b, i):
                act.wait_ge(s_max, b * TILES + i + 1)
                act.activation(prob[:, i % 2, :], scores[:, 2 * (i % 2):2 * (i % 2) + 2, :].rearrange("p a t -> p (a t)"),
                               ACT.Exp, bias=row_max[:, i:i + 1], accum_out=row_sum[:, 0, i:i + 1]).then_inc(s_exp, 1)

            def turn_probs(place, i):
                for n, unit in enumerate((f"T{i}a", f"T{i}b")):
                    wait_filled(act, place, unit)
                    act.activation(tile_group(pT_hi, n, i), as_tiles(ps(place, unit)), ACT.Copy).then_inc(p_hi_made, 1)

            def take_o(place, g):
                wait_filled(act, place, f"PV{g}")
                act.activation(o_s[:, :], ps(place, f"PV{g}"), ACT.Copy).then_inc(drained[place.bank(f"PV{g}")], 1)

            def turn_x(place):
                for n in range(HALVES):
                    unit = f"xT{n}"
                    wait_filled(act, place, unit)
                    act.activation(xT[:, n * QUAD:(n + 1) * QUAD, :], as_tiles(ps(place, unit)), ACT.Copy
                                   ).then_inc(drained[place.bank(unit)], 1)

            def turn_normed(place, kind, hi, made):
                for n in range(HALVES):
                    wait_filled(act, place, f"{kind}{n}")
                    act.activation(hi[n], ps(place, f"{kind}{n}"), ACT.Copy).then_inc(made, 1)

            def key_softmax(place, lb):
                act.wait_ge(k_max, lb + 1)
                for n in range(HALVES):
                    act.activation(half(p1, n), ps(place, f"kT{n}"), ACT.Exp, bias=kst[:, 2:3],
                                   accum_out=kst[:, 4 + n:5 + n]).then_inc(drained[place.bank(f"kT{n}")], 1)

            def turn_keys(place):
                for n in range(HALVES):
                    unit = f"p{n}"
                    wait_filled(act, place, unit)
                    act.activation(p1T[:, n * QUAD:(n + 1) * QUAD, :], as_tiles(ps(place, unit)), ACT.Copy
                                   ).then_inc(drained[place.bank(unit)], 1)

            def take_m3(place):
                wait_filled(act, place, "m3")
                act.activation(m3_hi[:, :], tile(ps(place, "m3"), 0), ACT.Copy).then_inc(m3_hi_made, 1)

            def take_logits(place):
                for n in range(HALVES):
                    unit = f"lg{n}"
                    wait_filled(act, place, unit)
                    act.activation(half(lgT, n), ps(place, unit)[0:E, :], ACT.Copy
                                   ).then_inc(drained[place.bank(unit)], 1)

            def route_exp(place, lb):
                wait_drained(act, place, "lT")
                act.activation(rt[:, 1, :, :], rt[:, 0, :, :], ACT.Exp).then_inc(r_exp, 1)

            def turn_z(place, lc, zT):
                act.wait_ge(z_stored, lc * 16 + 16)
                for n in range(HALVES):
                    unit = f"z{n}"
                    wait_filled(act, place, unit)
                    act.activation(half(zT, n), ps(place, unit), ACT.Copy).then_inc(drained[place.bank(unit)], 1)

            def w_halves(lb):
                return [wT_hi[:, bass.ds(lb * T + n * BANK, BANK)] for n in range(HALVES)]

            uT_halves = [half(uT_hi, n) for n in range(HALVES)]

            def batch(place, b, la, lc):
                if la is not None:
                    turn_probs(place, 6)
                else:
                    split_first()
                project(place, "q0", q_hi, bqs_c)
                if la is not None:
                    turn_probs(place, 7)
                project(place, "k0", k_hi, bk_c)
                project(place, "k1", k_hi, bk_c)
                if lc is not None:
                    take_m3(place)
                project(place, "q1", q_hi, bqs_c)
                if la is not None:
                    take_o(place, 1)
                softmax(b, 0)
                if la is not None:
                    softmax(b, 1)
                project_v(place)
                if la is None:
                    softmax(b, 1)
                turn_probs(place, 0)
                turn_probs(place, 1)
                softmax(b, 2)
                if la is not None:
                    wait_drained(act, place, "OT1")
                turn_x(place)
                act.sem_inc(xb_read, 1)
                if la is None:
                    for i in range(2, QUAD):
                        turn_probs(place, i)
                        softmax(b, i + 1)
                else:
                    if lc is not None:
                        turn_normed(place, "w", w_halves(lc), w_hi_made)
                    softmax(b, 3)
                    turn_probs(place, 2)
                    if lc is not None:
                        take_logits(place)
                    turn_probs(place, 3)
                    turn_normed(place, "u", uT_halves, u_hi_made)
                    softmax(b, 4)
                if lc is not None:
                    turn_z(place, lc, zT_early)
                softmax(b, 5)
                if lc is not None:
                    route_exp(place, lc)
                if la is not None:
                    key_softmax(place, la)
                take_o(place, 0)
                turn_probs(place, 4)
                if la is not None:
                    turn_keys(place)
                softmax(b, 6)
                turn_probs(place, 5)
                softmax(b, 7)

            batch(FIRST, 0, None, None)
            batch(SECOND, 1, 0, None)
            with act.Fori(2, B) as b:
                batch(loop_place(b), b, b - 1, b - 2)

            def gelu(m, s):
                act.wait_ge(e_h, m * (2 * E) + s + 1)
                if not (first_batch(m) and s < 2):
                    act.wait_ge(e_mul, m * (2 * E) + s - 1)
                act.activation(half(gel, s % 2), scores[:, s % 2, :], ACT.Gelu, bias=b1_c[:, s % E:s % E + 1]
                               ).then_inc(e_gelu, 1)

            def high(m, s):
                act.wait_ge(e_mul, m * (2 * E) + s + 1)
                if not (first_batch(m) and s < 4):
                    act.wait_ge(e_y, m * (2 * E) + s - 3)
                act.activation(hs_hi[s % 4], half(hs, s % 2), ACT.Copy).then_inc(e_hi, 1)

            def experts(m, between):
                for s in range(2 * E):
                    gelu(m, s)
                    if s > 0:
                        high(m, s - 1)
                    elif not first_batch(m):
                        high(m - 1, 2 * E - 1)
                    between_steps(between, m, s)

            la, lc = B - 1, B - 2
            turn_probs(TAIL, 6)
            turn_probs(TAIL, 7)
            linear_and_routing = gathered(
                (TAIL_AT["m3"], lambda: take_m3(TAIL)),
                (TAIL_AT["PV"] + 3, lambda: take_o(TAIL, 1)),
                (TAIL_AT["w"], lambda: turn_normed(TAIL, "w", w_halves(lc), w_hi_made)),
                (TAIL_AT["lg"], lambda: take_logits(TAIL)),
                (TAIL_AT["u"], lambda: turn_normed(TAIL, "u", uT_halves, u_hi_made)),
                (TAIL_AT["z"], lambda: turn_z(TAIL, lc, zT_late)),
                (TAIL_AT["exp"], lambda: route_exp(TAIL, lc)),
                (TAIL_AT["exp"], lambda: key_softmax(TAIL, la)),
                (TAIL_AT["p"], lambda: turn_keys(TAIL)),
                (END_AT["m3"], lambda: take_m3(END)),
                (END_AT["w"], lambda: turn_normed(END, "w", w_halves(la), w_hi_made)),
                (END_AT["lg"], lambda: take_logits(END)),
                (END_AT["z"], lambda: turn_z(END, la, zT_late)),
                (END_AT["exp"], lambda: route_exp(END, la)),
            )
            experts(0, linear_and_routing)
            experts(1, linear_and_routing)
            with act.Fori(2, B) as m:
                experts(m, {})
            high(B - 1, 2 * E - 1)

        @block.vector
        def _(dve):
            passed[dve] = passed_dve
            made = [0]

            def after(ins):
                made[0] += 1
                ins.then_inc(dve_chain, 1)
                dve.wait_ge(dve_chain, made[0])

            linked = {}

            def link(chain, lb, ins):
                n, per_batch = linked.get(chain, 0) + 1, dict(linear=LINEAR_CHAIN, routing=ROUTING_CHAIN)[chain]
                linked[chain] = n % per_batch
                signal = dict(linear=linear_chain, routing=routing_chain)[chain]
                ins.then_inc(signal, 1)
                dve.wait_ge(signal, lb * per_batch + n)

            def group_stats(b):
                for n in range(HALVES):
                    dve.wait_ge(ld_x0b if (b, n) == (0, 1) else ld_x[b], 16)
                    last = dve.bn_stats(gst[:, b, n, :], half(x_of[b], n))
                after(last)

            def channel_means(b0, nb):
                for b in range(b0, b0 + nb):
                    last = dve.bn_aggr(gmv[:, b, :], gst[:, b, :, :])
                last.then_inc(gn_mv, 1)

            def group_deviation(place, b0, nb):
                mean, dev = gsum[:, 0, b0:b0 + nb], gsum[:, 1, b0:b0 + nb]
                wait_filled(dve, place, "gn_mean")
                dve.tensor_copy(mean, ps(place, "gn_mean")[:, 0:nb]).then_inc(drained[place.bank("gn_mean")], 1)
                wait_drained(dve, place, "gn_mean")
                after(dve.tensor_tensor(dev, gmv[:, b0:b0 + nb, 0], mean, ALU.subtract))
                after(dve.tensor_tensor(dev, dev, dev, ALU.mult))
                dve.tensor_tensor(dev, dev, gmv[:, b0:b0 + nb, 1], ALU.add).then_inc(gn_mv, 1)

            def group_variance(place, b0, nb):
                wait_filled(dve, place, "gn_var")
                dve.tensor_copy(gsum[:, 2, b0:b0 + nb], ps(place, "gn_var")[:, 0:nb]
                                ).then_inc(drained[place.bank("gn_var")], 1)

            def group_affine(n, b0, nb):
                dve.wait_ge(gn_rstd, n)
                after(dve.tensor_scalar(gmul[:, b0:b0 + nb], gsum[:, 3, b0:b0 + nb], gs_c, None, ALU.mult))
                after(dve.tensor_tensor(gadd[:, b0:b0 + nb], gsum[:, 0, b0:b0 + nb], gmul[:, b0:b0 + nb], ALU.mult))
                dve.tensor_scalar(gadd[:, b0:b0 + nb], gadd[:, b0:b0 + nb], -1.0, gb_c, ALU.mult, ALU.add
                                  ).then_inc(gn_made, 1)

            def split(raw, hi, lo):
                after(dve.tensor_copy(hi, raw))
                dve.tensor_tensor(lo, raw, hi.bitcast(FP32), ALU.subtract).then_inc(setup_made, 1)

            def first_norm():
                dve.wait_ge(gn_made, 1)
                for n in range(HALVES):
                    last = dve.tensor_scalar(half(h_f, n), half(xb, n), gmul[:, 0:1], gadd[:, 0:1],
                                             ALU.mult, ALU.add)
                after(last)

            def low_first():
                for n in range(HALVES):
                    dve.wait_ge(h_hi_made, n + 1)
                    dve.tensor_tensor(half(h_lo, n), half(h_f, n), half(h_hi, n).bitcast(FP32), ALU.subtract
                                      ).then_inc(h_lo_made, 1)

            dve.memset(rt_hi[:, :].bitcast(FP32), 0.0)
            dve.memset(rt_lo[:, :].bitcast(FP32), 0.0)
            group_stats(0)
            channel_means(0, 1)
            dve.wait_ge(ld_w["wq"], 16)
            after(dve.tensor_scalar(wq_sc, wq_raw, SCALE, None, ALU.mult))
            split(wq_sc, wq_hi[:, :], wq_lo[:, :])
            group_deviation(SETUP, 0, 1)
            group_variance(SETUP, 0, 1)
            dve.wait_ge(ld_w["wk"], 16)
            split(wk_raw, wk_hi[:, :], wk_lo[:, :])
            dve.wait_ge(ld_w["gn"], 32)
            group_affine(1, 0, 1)
            first_norm()
            dve.wait_ge(ld_w["cols"], 64)
            dve.tensor_scalar(bqs_c, bq_c, SCALE, None, ALU.mult).then_inc(setup_made, 1)
            wait_filled(dve, SETUP, "wvT")
            dve.tensor_copy(wvT[:, :], tile(ps(SETUP, "wvT"), 0)).then_inc(drained[SETUP.bank("wvT")], 1)
            low_first()
            wait_filled(dve, SETUP, "wpv")
            after(dve.tensor_copy(wpv_hi[:, :], tile(ps(SETUP, "wpv"), 0)))
            dve.tensor_tensor(wpv_lo[:, :], tile(ps(SETUP, "wpv"), 0), wpv_hi[:, :].bitcast(FP32), ALU.subtract
                              ).then_inc(drained[SETUP.bank("wpv")], 1)
            wait_filled(dve, SETUP, "bias_o")
            dve.tensor_tensor(bias_o, ps(SETUP, "bias_o")[:, 0:1], bp_c, ALU.add
                              ).then_inc(drained[SETUP.bank("bias_o")], 1)

            def setup_rest():
                wait_filled(dve, FIRST, "l1qT")
                dve.tensor_copy(l1qT[:, :], tile(ps(FIRST, "l1qT"), 0)).then_inc(drained[FIRST.bank("l1qT")], 1)
                wait_filled(dve, FIRST, "routerT")
                after(dve.tensor_copy(rt_hi[:, 0:E], ps(FIRST, "routerT")[:, 0:E]))
                dve.tensor_tensor(rt_lo[:, 0:E], ps(FIRST, "routerT")[:, 0:E], rt_hi[:, 0:E].bitcast(FP32),
                                  ALU.subtract).then_inc(drained[FIRST.bank("routerT")], 1)
                wait_filled(dve, FIRST, "b1T")
                dve.tensor_copy(b1_c[:, :], ps(FIRST, "b1T")[:, 0:E]).then_inc(drained[FIRST.bank("b1T")], 1)
                dve.wait_ge(ld_w["qkv"], 16)
                split(wqkv_s[:, C:2 * C], l1k_hi[:, :], l1k_lo[:, :])

            def low(place, unit, hi, lo, made, count):
                dve.wait_ge(made, count)
                dve.tensor_tensor(lo, ps(place, unit)[:, 0:lo.shape[-1]], hi.bitcast(FP32), ALU.subtract
                                  ).then_inc(drained[place.bank(unit)], 1)

            def project(place, b, unit, hi, lo, bias):
                n = int(unit[1])
                dve.wait_ge(qk_hi_made, b * 4 + ATTENTION["qk"].index(unit) + 1)
                dve.scalar_tensor_tensor(out=half(lo, n), in0=ps(place, unit), scalar=bias,
                                         in1=half(hi, n).bitcast(FP32), op0=ALU.add, op1=ALU.subtract
                                         ).then_inc(drained[place.bank(unit)], 1)

            def project_v(place, b):
                for n in range(HALVES):
                    low(place, f"v{n}", half(v_hi, n), half(v_lo, n), v_hi_made, b * HALVES + n + 1)

            def row_maximum(b, i):
                dve.wait_ge(s_made, b * TILES + i + 1)
                dve.tensor_reduce(row_max[:, i:i + 1], scores[:, 2 * (i % 2):2 * (i % 2) + 2, :].rearrange("p a t -> p (a t)"),
                                  AX.X, ALU.max, negate=True).then_inc(s_max, 1)

            def turn_probs(place, b, i):
                for n, unit in enumerate((f"T{i}a", f"T{i}b")):
                    dve.wait_ge(p_hi_made, b * (2 * TILES) + 2 * i + n + 1)
                    dve.tensor_tensor(tile_group(pT_lo, n, i), as_tiles(ps(place, unit)),
                                      tile_group(pT_hi, n, i).bitcast(FP32), ALU.subtract
                                      ).then_inc(drained[place.bank(unit)], 1)

            def invert_sums(b, g):
                dve.wait_ge(s_exp, b * TILES + (g + 1) * QUAD)
                dve.reciprocal(row_sum[:, 1, g * QUAD:(g + 1) * QUAD], row_sum[:, 0, g * QUAD:(g + 1) * QUAD]
                               ).then_inc(r_made, 1)

            def residual(place, b, g):
                dve.wait_ge(r_made, b * 2 + g + 1)
                if g == 0:
                    wait_drained(dve, place, "xT0")
                    wait_drained(dve, place, "xT1")
                wait_filled(dve, place, f"OT{g}")
                for j in range(QUAD):
                    i = g * QUAD + j
                    last = dve.scalar_tensor_tensor(out=t1[:, i, :], in0=tile(ps(place, f"OT{g}"), j),
                                                    scalar=row_sum[:, 1, i:i + 1], in1=xT[:, i, :],
                                                    op0=ALU.mult, op1=ALU.add)
                last.then_inc(drained[place.bank(f"OT{g}")], 1)

            def norm_stats(n, lb, src):
                for j in range(TILES):
                    last = dve.bn_stats(lst[:, j, :], src[:, j, :])
                link("linear", lb, last)
                apart(dve)
                for j in range(TILES):
                    last = dve.bn_aggr(lmv[n][:, j, :], lst[:, j, :])
                last.then_inc(ln_stats[n], 1)

            def norm1_stats(place, lb):
                wait_drained(dve, place, "OT1")
                norm_stats(0, lb, t1)

            def turn_normed(place, kind, hi, lo, made, lb):
                for n in range(HALVES):
                    low(place, f"{kind}{n}", hi[n], lo[n], made, lb * HALVES + n + 1)

            def key_maximum(place, lb):
                for n in range(HALVES):
                    wait_filled(dve, place, f"kT{n}")
                    last = dve.tensor_reduce(kst[:, n:n + 1], ps(place, f"kT{n}"), AX.X, ALU.max, negate=True)
                link("linear", lb, last)
                dve.tensor_tensor(kst[:, 2:3], kst[:, 0:1], kst[:, 1:2], ALU.min).then_inc(k_max, 1)

            def key_sums(place, lb):
                wait_drained(dve, place, "kT0")
                wait_drained(dve, place, "kT1")
                link("linear", lb, dve.tensor_tensor(kst[:, 6:7], kst[:, 4:5], kst[:, 5:6], ALU.add))
                link("linear", lb, dve.reciprocal(kst[:, 7:8], kst[:, 6:7]))

            def take(place, unit, dst):
                wait_filled(dve, place, unit)
                dve.tensor_copy(dst, tile(ps(place, unit), 0)).then_inc(drained[place.bank(unit)], 1)

            def take_g(place):
                take(place, "g", gT_s[:, :])
                wait_drained(dve, place, "g")
                dve.sem_inc(g_made, 1)

            def take_ctx(place):
                wait_filled(dve, place, "ctx")
                dve.scalar_tensor_tensor(out=ctx_s[:, :], in0=tile(ps(place, "ctx"), 0), scalar=kst[:, 7:8],
                                         in1=head_mask[:, :], op0=ALU.mult, op1=ALU.mult
                                         ).then_inc(drained[place.bank("ctx")], 1)

            def take_m3(place, lb):
                low(place, "m3", m3_hi[:, :], m3_lo[:, :], m3_hi_made, lb + 1)

            def take_out(place, lb):
                dve.wait_ge(t1b_made, lb + 1)
                for n in range(HALVES):
                    unit = f"o{n}"
                    wait_filled(dve, place, unit)
                    dst = t2[:, n * QUAD:(n + 1) * QUAD, :]
                    dve.tensor_tensor(dst, as_tiles(ps(place, unit)), dst, ALU.add).then_inc(drained[place.bank(unit)], 1)

            def norm2_stats(place, lb):
                wait_drained(dve, place, "o0")
                wait_drained(dve, place, "o1")
                norm_stats(1, lb, t2)

            def turn_comb(place, lc, cT):
                dve.wait_ge(c_stored, lc * 16 + 16)
                for n in range(HALVES):
                    unit = f"c{n}"
                    wait_filled(dve, place, unit)
                    dve.tensor_copy(half(cT, n), ps(place, unit)[0:2 * E, :]).then_inc(drained[place.bank(unit)], 1)

            def over(v):
                return v.unsqueeze(2).to_broadcast([P, TILES, E])

            falling_b = falling[:, :].unsqueeze(1).to_broadcast([P, TILES, E])

            def route(place, lc):
                less, ex, one, left, two = (rt[:, i, :, :] for i in range(5))
                top, total, k1, second, k2, both = (rr[:, i, :] for i in range(6))
                tt, red, stt = dve.tensor_tensor, dve.tensor_reduce, dve.scalar_tensor_tensor

                def less_top():
                    wait_filled(dve, place, "lT")
                    logits = ps(place, "lT")[:, 0:TILES * E].rearrange("p (j e) -> p j e", e=E)
                    link("routing", lc, red(top, logits, AX.X, ALU.max, negate=True))
                    tt(less, logits, over(top), ALU.add).then_inc(drained[place.bank("lT")], 1)

                def part_a():
                    wait_drained(dve, place, "lT")
                    link("routing", lc, dve.tensor_scalar(one, less, 0.0, None, ALU.is_equal))
                    link("routing", lc, tt(one, one, falling_b, ALU.mult))
                    link("routing", lc, red(k1, one, AX.X, ALU.max))
                    link("routing", lc, tt(one, one, over(k1), ALU.is_equal))
                    link("routing", lc, stt(out=left, in0=one, scalar=-3e38, in1=less, op0=ALU.mult, op1=ALU.add))

                def part_b():
                    link("routing", lc, red(second, left, AX.X, ALU.max))
                    link("routing", lc, tt(two, left, over(second), ALU.is_equal))
                    link("routing", lc, tt(two, two, falling_b, ALU.mult))
                    link("routing", lc, red(k2, two, AX.X, ALU.max))
                    link("routing", lc, tt(two, two, over(k2), ALU.is_equal))
                    dve.wait_ge(r_exp, lc + 1)
                    red(total, ex, AX.X, ALU.add)
                    link("routing", lc, tt(one, one, two, ALU.add))

                def part_c():
                    link("routing", lc, tt(one, one, ex, ALU.mult))
                    link("routing", lc, red(both, one, AX.X, ALU.add))
                    link("routing", lc, stt(out=both, in0=total, scalar=1e-12, in1=both, op0=ALU.mult, op1=ALU.max))
                    link("routing", lc, dve.reciprocal(both, both))
                    link("routing", lc, tt(one, one, over(both), ALU.mult))
                    dve.tensor_copy(comb[:, :, 0:E].bitcast(FP32R), one).then_inc(share_hi, 1)
                    dve.wait_ge(share_hi, lc + 1)
                    tt(comb[:, :, E:2 * E], one, comb[:, :, 0:E], ALU.subtract).then_inc(c_made, 1)

                return less_top, part_a, part_b, part_c

            def w_halves(w, lb):
                return [w[:, bass.ds(lb * T + n * BANK, BANK)] for n in range(HALVES)]

            uT_halves = [[half(m, n) for n in range(HALVES)] for m in (uT_hi, uT_lo)]

            def batch(place, b, la, lc):
                if lc is not None:
                    route_less, route_a, route_b, route_c = route(place, lc)
                    take_ctx(place)
                if la is not None:
                    turn_probs(place, la, 6)
                else:
                    for n in range(1, B - 1):
                        group_stats(n)
                project(place, b, "q0", q_hi, q_lo, bqs_c)
                if la is not None:
                    turn_probs(place, la, 7)
                if lc is not None:
                    take(place, "m2", m2T_s[:, :])
                project(place, b, "k0", k_hi, k_lo, bk_c)
                project(place, b, "k1", k_hi, k_lo, bk_c)
                if lc is not None:
                    take_m3(place, lc)
                project(place, b, "q1", q_hi, q_lo, bqs_c)
                if la is None:
                    group_stats(B - 1)
                    channel_means(1, B - 1)
                if la is not None:
                    invert_sums(la, 1)
                if lc is not None:
                    take_out(place, lc)
                    norm2_stats(place, lc)
                row_maximum(b, 0)
                if la is None:
                    project_v(place, b)
                    group_deviation(place, 1, B - 1)
                row_maximum(b, 1)
                if la is not None:
                    residual(place, la, 1)
                if la is not None:
                    project_v(place, b)
                else:
                    setup_rest()
                    group_variance(place, 1, B - 1)
                turn_probs(place, b, 0)
                row_maximum(b, 2)
                if la is None:
                    group_affine(2, 1, B - 1)
                if la is not None:
                    norm1_stats(place, la)
                turn_probs(place, b, 1)
                row_maximum(b, 3)
                if lc is not None:
                    turn_normed(place, "w", w_halves(wT_hi, lc), w_halves(wT_lo, lc), w_hi_made, lc)
                turn_probs(place, b, 2)
                row_maximum(b, 4)
                turn_probs(place, b, 3)
                if la is not None:
                    turn_normed(place, "u", uT_halves[0], uT_halves[1], u_hi_made, la)
                if lc is not None:
                    route_less()
                row_maximum(b, 5)
                invert_sums(b, 0)
                if lc is not None:
                    route_a()
                if la is not None:
                    key_maximum(place, la)
                if lc is not None:
                    route_b()
                    route_c()
                if la is not None:
                    key_sums(place, la)
                turn_probs(place, b, 4)
                row_maximum(b, 6)
                if lc is not None:
                    turn_comb(place, lc, cT_early)
                turn_probs(place, b, 5)
                row_maximum(b, 7)
                if la is not None:
                    take_g(place)
                if la is not None:
                    dve.wait_ge(t1b_made, la + 1)
                else:
                    dve.wait_ge(experts_split, 3)
                residual(place, b, 0)

            batch(FIRST, 0, None, None)
            batch(SECOND, 1, 0, None)
            with dve.Fori(2, B) as b:
                batch(loop_place(b), b, b - 1, b - 2)

            def weigh(m, s):
                dve.wait_ge(e_gelu, m * (2 * E) + s + 1)
                if not (first_batch(m) and s < 2):
                    dve.wait_ge(e_hi, m * (2 * E) + s - 1)
                    dve.wait_ge(e_lo, m * (2 * E) + s - 1)
                dve.tensor_tensor(half(hs, s % 2), half(gel, s % 2), scores[:, 2 + s % 2, :], ALU.mult
                                  ).then_inc(e_mul, 1)

            def lower(m, s):
                dve.wait_ge(e_hi, m * (2 * E) + s + 1)
                if not (first_batch(m) and s < 4):
                    dve.wait_ge(e_y, m * (2 * E) + s - 3)
                dve.tensor_tensor(hs_lo[s % 4], half(hs, s % 2), hs_hi[s % 4].bitcast(FP32),
                                  ALU.subtract).then_inc(e_lo, 1)

            def result(m, h):
                place = y_place(m)
                dve.wait_ge(e_y, m * (2 * E) + (h + 1) * E)
                dve.wait_ge(z_loaded[h], m * 16 + 16)
                if not first_batch(m):
                    dve.wait_ge(stored[h], m * 16)
                dve.tensor_tensor(half(out_s, h), ps(place, f"y{h}"), half(z_in, h), ALU.add
                                  ).then_inc(drained[place.bank(f"y{h}")], 1)

            def experts(m, between):
                for s in range(2 * E):
                    weigh(m, s)
                    if s > 0:
                        lower(m, s - 1)
                    elif not first_batch(m):
                        lower(m - 1, 2 * E - 1)
                    if s == 3 and not first_batch(m):
                        result(m - 1, 1)
                    if s == E + 3:
                        result(m, 0)
                    between_steps(between, m, s)

            la, lc = B - 1, B - 2
            take_ctx(TAIL)
            turn_probs(TAIL, la, 6)
            take(TAIL, "m2", m2T_s[:, :])
            turn_probs(TAIL, la, 7)
            routes, last_routes = route(TAIL, lc), route(END, la)
            linear_and_routing = gathered(
                (TAIL_AT["m3"], lambda: take_m3(TAIL, lc)),
                (TAIL_AT["o"], lambda: take_out(TAIL, lc)),
                (TAIL_AT["o"], lambda: norm2_stats(TAIL, lc)),
                (TAIL_AT["o"] + 2, lambda: invert_sums(la, 1)),
                (TAIL_AT["OT"], lambda: residual(TAIL, la, 1)),
                (TAIL_AT["OT"], lambda: norm1_stats(TAIL, la)),
                (TAIL_AT["w"], lambda: turn_normed(TAIL, "w", w_halves(wT_hi, lc), w_halves(wT_lo, lc), w_hi_made, lc)),
                (TAIL_AT["u"], lambda: turn_normed(TAIL, "u", uT_halves[0], uT_halves[1], u_hi_made, la)),
                (TAIL_AT["lT"], routes[0]),
                (TAIL_AT["lT"], routes[1]),
                (TAIL_AT["kT"], lambda: key_maximum(TAIL, la)),
                (TAIL_AT["exp"] + 1, routes[2]),
                (TAIL_AT["exp"] + 1, lambda: key_sums(TAIL, la)),
                (TAIL_AT["exp"] + 2, routes[3]),
                (TAIL_AT["g"], lambda: take_g(TAIL)),
                (TAIL_AT["c"], lambda: turn_comb(TAIL, lc, cT_late)),
                (END_AT["ctx"], lambda: take_ctx(END)),
                (END_AT["m2"], lambda: take(END, "m2", m2T_s[:, :])),
                (END_AT["m3"], lambda: take_m3(END, la)),
                (END_AT["o"], lambda: take_out(END, la)),
                (END_AT["o"], lambda: norm2_stats(END, la)),
                (END_AT["w"], lambda: turn_normed(END, "w", w_halves(wT_hi, la), w_halves(wT_lo, la), w_hi_made, la)),
                (END_AT["lT"], last_routes[0]),
                (END_AT["lT"], last_routes[1]),
                (END_AT["exp"] + 1, last_routes[2]),
                (END_AT["exp"] + 2, last_routes[3]),
                (END_AT["c"], lambda: turn_comb(END, la, cT_late)),
            )
            experts(0, linear_and_routing)
            experts(1, linear_and_routing)
            with dve.Fori(2, B) as m:
                experts(m, {})
            lower(B - 1, 2 * E - 1)
            result(B - 1, 1)

        @block.tensor
        def _(pe):
            passed[pe] = passed_pe

            def open_unit(place, unit):
                if not (isinstance(place.earlier(unit), int) and place.earlier(unit) == 0):
                    pe.wait_ge(drained[place.bank(unit)], place.earlier(unit))
                return ps(place, unit)

            def fill(place, unit, ins):
                ins.then_inc(filled[place.bank(unit)], 1)

            def product3(dst, left, right, start=True, stop=True):
                (lh, ll), (rh, rl) = left, right
                pe.matmul(dst, lh, rh, start=start, stop=False)
                pe.matmul(dst, lh, rl, start=False, stop=False)
                return pe.matmul(dst, ll, rh, start=False, stop=stop)

            def whole(place, unit, left, right):
                fill(place, unit, product3(open_unit(place, unit), left, right))

            def small(place, unit, n, left, right):
                dst = open_unit(place, unit)
                fill(place, unit, pe.matmul(dst[:, 0:n], left, right, start=True, stop=True))

            def turn(place, unit, tiles, rows=P, step=P):
                dst = open_unit(place, unit)
                for j, t in enumerate(tiles):
                    last = pe.transpose(dst[0:t.shape[-1], j * step:j * step + rows], t, ident[0:rows, 0:rows])
                fill(place, unit, last)

            def group_means(place, n, b0, nb):
                pe.wait_ge(gn_mv, n + 1)
                small(place, "gn_mean", nb, group_mean[:, :], gmv[:, b0:b0 + nb, 0])

            def group_variances(place, n, b0, nb):
                pe.wait_ge(gn_mv, n + 2)
                small(place, "gn_var", nb, group_mean[:, :], gsum[:, 1, b0:b0 + nb])

            def keep_busy(products):
                for _ in range(products):
                    pe.matmul(scores[:, 3, 0:C], group_mean[:, :], ident[:, :], start=True, stop=True)

            pe.wait_ge(const_made, 1)
            group_means(SETUP, 0, 0, 1)
            keep_busy(1)
            group_variances(SETUP, 0, 0, 1)
            keep_busy(6)
            pe.wait_ge(ld_w["wv"], 16)
            turn(SETUP, "wvT", [wv_s[:, :]])
            keep_busy(2)
            wait_drained(pe, SETUP, "wvT")
            pe.wait_ge(ld_w["wp"], 16)
            small(SETUP, "wpv", C, wvT[:, :], wp_s[:, :])
            pe.wait_ge(ld_w["cols"], 64)
            small(SETUP, "bias_o", 1, wp_s[:, :], bv_c)
            keep_busy(6)
            pe.wait_ge(setup_made, 3)

            def project(place, b, unit, hi, lo):
                n = int(unit[1])
                pe.wait_ge(h_lo_made, b * HALVES + n + 1)
                whole(place, unit, (hi[:, :], lo[:, :]), (half(h_hi, n), half(h_lo, n)))

            def project_v(place):
                for n in range(HALVES):
                    dst = open_unit(place, f"v{n}")
                    for j in range(QUAD):
                        i = n * QUAD + j
                        last = product3(tile(dst, j), (tile(h_hi, i), tile(h_lo, i)), (wpv_hi[:, :], wpv_lo[:, :]))
                    fill(place, f"v{n}", last)

            def score(b, i):
                if not (isinstance(b, int) and b == 0 and i < 2):
                    pe.wait_ge(s_exp, b * TILES + i - 1)
                for n in range(HALVES):
                    last = product3(scores[:, 2 * (i % 2) + n, :], (tile(q_hi, i), tile(q_lo, i)),
                                    (half(k_hi, n), half(k_lo, n)))
                last.then_inc(s_made, 1)

            def turn_probs(place, b, i):
                pe.wait_ge(s_exp, b * TILES + i + 1)
                for n in range(HALVES):
                    turn(place, f"T{i}" + "ab"[n], [tile(prob[:, i % 2, :], n * QUAD + j) for j in range(QUAD)])

            def attend(place, g, k0, k1):
                unit = f"PV{g}"
                if k0 == 0:
                    open_unit(place, unit)
                    last_of = {place.bank(t): t for t in ATTENTION["v"] * (g == 0)
                               + ATTENTION["T"][(g + 1) * QUAD - 1]}
                    for bank, t in last_of.items():
                        if bank != place.bank(unit):
                            wait_drained(pe, place, t)
                for k in range(k0, k1):
                    last = product3(ps(place, unit), (tile(v_hi, k), tile(v_lo, k)),
                                    (pT_hi[:, k, :], pT_lo[:, k, :]), start=k == 0, stop=k == TILES - 1)
                if k1 == TILES:
                    fill(place, unit, last)

            def turn_o(place, g):
                wait_drained(pe, place, f"PV{g}")
                turn(place, f"OT{g}", [tile(o_s, j) for j in range(QUAD)])

            def turn_x(place, b):
                pe.wait_ge(xb_made, b + 1)
                for n in range(HALVES):
                    turn(place, f"xT{n}", [tile(xb, n * QUAD + j) for j in range(QUAD)])

            def tiles_of(src, n):
                return [src[:, n * QUAD + j, :] for j in range(QUAD)]

            def turn_u(place, lb):
                for n in range(HALVES):
                    pe.wait_ge(u_made, lb * HALVES + n + 1)
                    turn(place, f"u{n}", tiles_of(u, n))

            def keys(place):
                for n in range(HALVES):
                    wait_drained(pe, place, f"u{n}")
                    whole(place, f"kT{n}", (l1k_hi[:, :], l1k_lo[:, :]), (half(uT_hi, n), half(uT_lo, n)))

            def turn_keys(place):
                for n in range(HALVES):
                    wait_drained(pe, place, f"kT{n}")
                    turn(place, f"p{n}", [tile(p1, n * QUAD + j) for j in range(QUAD)])

            def gather_keys(place):
                wait_drained(pe, place, "p0")
                wait_drained(pe, place, "p1")
                dst = open_unit(place, "g")
                for j in range(TILES):
                    last = pe.matmul(dst[:, 0:C], u[:, j, :], p1T[:, j, :], start=j == 0, stop=j == TILES - 1)
                fill(place, "g", last)

            def context(place, lb):
                pe.wait_ge(g_made, lb + 1)
                small(place, "ctx", C, gT_s[:, :], wqkv_s[:, 2 * C:3 * C])

            def merge2(place):
                wait_drained(pe, place, "ctx")
                small(place, "m2", C, ctx_s[:, :], l1qT[:, :])

            def merge3(place):
                wait_drained(pe, place, "m2")
                small(place, "m3", C, m2T_s[:, :], wout_s[:, :])

            def linear_out(place):
                wait_drained(pe, place, "m3")
                for n in range(HALVES):
                    dst = open_unit(place, f"o{n}")
                    for j in range(QUAD):
                        i = n * QUAD + j
                        last = product3(tile(dst, j), (tile(uT_hi, i), tile(uT_lo, i)), (m3_hi[:, :], m3_lo[:, :]))
                    fill(place, f"o{n}", last)

            def turn_w(place, lb):
                for n in range(HALVES):
                    pe.wait_ge(w_made, lb * HALVES + n + 1)
                    turn(place, f"w{n}", tiles_of(w_n, n))

            def w_of(lb, n):
                return [m[:, bass.ds(lb * T + n * BANK, BANK)] for m in (wT_hi, wT_lo)]

            def logits(place, lb):
                for n in range(HALVES):
                    wait_drained(pe, place, f"w{n}")
                    whole(place, f"lg{n}", (rt_hi[:, :], rt_lo[:, :]), w_of(lb, n))

            def turn_logits(place):
                wait_drained(pe, place, "lg0")
                wait_drained(pe, place, "lg1")
                dst = open_unit(place, "lT")
                apart(pe)
                for j in range(TILES):
                    last = pe.transpose(dst[:, j * E:(j + 1) * E], tile(lgT, j), ident[0:E, 0:E])
                fill(place, "lT", last)

            def turn_z(place, lb):
                pe.wait_ge(z_made, lb + 1)
                for n in range(HALVES):
                    turn(place, f"z{n}", tiles_of(t2, n))

            def turn_comb(place, lb):
                pe.wait_ge(c_made, lb + 1)
                for n in range(HALVES):
                    turn(place, f"c{n}", tiles_of(comb, n))

            def batch(place, b, la, lc):
                if la is not None:
                    turn_probs(place, la, 6)
                if lc is not None:
                    context(place, lc)
                project(place, b, "q0", wq_hi, wq_lo)
                if la is not None:
                    turn_probs(place, la, 7)
                if lc is not None:
                    merge2(place)
                project(place, b, "k0", wk_hi, wk_lo)
                project(place, b, "k1", wk_hi, wk_lo)
                if lc is not None:
                    merge3(place)
                project(place, b, "q1", wq_hi, wq_lo)
                if la is not None:
                    attend(place, 1, 0, QUAD // 2)
                if lc is not None:
                    linear_out(place)
                if la is not None:
                    attend(place, 1, QUAD // 2, QUAD)
                for unit in ("q0", "k0", "k1"):
                    wait_drained(pe, place, unit)
                score(b, 0)
                if la is None:
                    project_v(place)
                    group_means(place, 2, 1, B - 1)
                    score(b, 1)
                else:
                    attend(place, 1, QUAD, TILES)
                    score(b, 1)
                    turn_o(place, 1)
                    project_v(place)
                if la is None:
                    pe.wait_ge(ld_w["qkv"], 16)
                    turn(place, "l1qT", [wqkv_s[:, 0:C]])
                    pe.wait_ge(ld_w["rows8"], 32)
                    turn(place, "routerT", [rows8[:, 0, :]], rows=E)
                    turn(place, "b1T", [rows8[:, 1, :]], rows=E)
                    group_variances(place, 2, 1, B - 1)
                turn_probs(place, b, 0)
                score(b, 2)
                turn_probs(place, b, 1)
                turn_x(place, b)
                score(b, 3)
                if lc is not None:
                    turn_w(place, lc)
                turn_probs(place, b, 2)
                wait_drained(pe, place, "q1")
                score(b, 4)
                if lc is not None:
                    logits(place, lc)
                turn_probs(place, b, 3)
                score(b, 5)
                if la is not None:
                    turn_u(place, la)
                if lc is not None:
                    turn_logits(place)
                if lc is not None:
                    turn_z(place, lc)
                if la is not None:
                    keys(place)
                attend(place, 0, 0, TILES)
                turn_probs(place, b, 4)
                score(b, 6)
                if la is not None:
                    turn_keys(place)
                if lc is not None:
                    turn_comb(place, lc)
                turn_probs(place, b, 5)
                score(b, 7)
                if la is not None:
                    gather_keys(place)
                turn_o(place, 0)

            batch(FIRST, 0, None, None)
            batch(SECOND, 1, 0, None)
            with pe.Fori(2, B) as b:
                batch(loop_place(b), b, b - 1, b - 2)

            def hidden(m, s):
                h, e = s // E, s % E
                if first_batch(m) and s < 2:
                    pe.wait_ge(s_exp, B * TILES)
                else:
                    pe.wait_ge(e_gelu, m * (2 * E) + s - 1)
                    pe.wait_ge(e_mul, m * (2 * E) + s - 1)
                product3(scores[:, s % 2, :], (tile(w1_hi, e), tile(w1_lo, e)), w_of(m, h))
                pe.wait_ge(c_loaded[h], m * 16 + 16)
                pe.matmul(scores[:, 2 + s % 2, :], pick[:, e, :], cb_in[:, h, :], start=True, stop=True
                          ).then_inc(e_h, 1)

            def outward(m, s):
                h, e = s // E, s % E
                place = y_place(m)
                dst = ps(place, f"y{h}")
                if e == 0:
                    open_unit(place, f"y{h}")
                    pe.matmul(dst, b2_hi[:, :], cb_in[:, h, :], start=True, stop=False)
                    pe.matmul(dst, b2_lo[:, :], cb_in[:, h, :], start=False, stop=False)
                pe.wait_ge(e_lo, m * (2 * E) + s + 1)
                last = product3(dst, (tile(w2_hi, e), tile(w2_lo, e)), (hs_hi[s % 4], hs_lo[s % 4]),
                                start=False, stop=e == E - 1)
                last.then_inc(e_y, 1)

            def experts(m, between):
                for s in range(2 * E):
                    hidden(m, s)
                    if s >= 3:
                        outward(m, s - 3)
                    elif not first_batch(m):
                        outward(m - 1, 2 * E + s - 3)
                    between_steps(between, m, s)

            la, lc = B - 1, B - 2
            turn_probs(TAIL, la, 6)
            context(TAIL, lc)
            turn_probs(TAIL, la, 7)
            merge2(TAIL)
            pe.wait_ge(experts_split, 3)
            pe.wait_ge(mask_made, 1)
            linear_and_routing = gathered(
                (TAIL_AT["m3"], lambda: merge3(TAIL)),
                *((TAIL_AT["PV"] + n, lambda n=n: attend(TAIL, 1, 2 * n, 2 * n + 2)) for n in range(4)),
                (TAIL_AT["o"], lambda: linear_out(TAIL)),
                (TAIL_AT["OT"], lambda: turn_o(TAIL, 1)),
                (TAIL_AT["w"], lambda: turn_w(TAIL, lc)),
                (TAIL_AT["lg"], lambda: logits(TAIL, lc)),
                (TAIL_AT["u"], lambda: turn_u(TAIL, la)),
                (TAIL_AT["lT"], lambda: turn_logits(TAIL)),
                (TAIL_AT["z"], lambda: turn_z(TAIL, lc)),
                (TAIL_AT["kT"], lambda: keys(TAIL)),
                (TAIL_AT["p"], lambda: turn_keys(TAIL)),
                (TAIL_AT["g"], lambda: gather_keys(TAIL)),
                (TAIL_AT["c"], lambda: turn_comb(TAIL, lc)),
                (END_AT["ctx"], lambda: context(END, la)),
                (END_AT["m2"], lambda: merge2(END)),
                (END_AT["m3"], lambda: merge3(END)),
                (END_AT["o"], lambda: linear_out(END)),
                (END_AT["w"], lambda: turn_w(END, la)),
                (END_AT["lg"], lambda: logits(END, la)),
                (END_AT["lT"], lambda: turn_logits(END)),
                (END_AT["z"], lambda: turn_z(END, la)),
                (END_AT["c"], lambda: turn_comb(END, la)),
            )
            experts(0, linear_and_routing)
            experts(1, linear_and_routing)
            with pe.Fori(2, B) as m:
                experts(m, {})
            for s in range(2 * E - 3, 2 * E):
                outward(B - 1, s)


_INS = ['x', 'L0_conv_gn_scale', 'L0_conv_gn_bias', 'L0_conv_Wq', 'L0_conv_bq', 'L0_conv_Wk', 'L0_conv_bk',
        'L0_conv_Wv', 'L0_conv_bv', 'L0_conv_Wp', 'L0_conv_bp', 'L1_attn_W_qkv', 'L1_attn_W_out',
        'L1_attn_b_out', 'L1_ffn_router_w', 'L1_ffn_w1', 'L1_ffn_b1', 'L1_ffn_w2', 'L1_ffn_b2']


def kernel(**inputs):
    import numpy as _np
    import concourse.bacc as _bacc
    from concourse import mybir as _mybir
    from concourse.bass_utils import run_bass_kernel_spmd as _run

    nc = _bacc.Bacc("TRN2", target_bir_lowering=False, num_devices=1)
    arrays, args = {}, []
    for name in _INS:
        a = _np.ascontiguousarray(inputs[name])
        arrays[f"in_{name}_dram"] = a
        args.append(nc.dram_tensor(f"in_{name}_dram", a.shape, _mybir.dt.from_np(a.dtype), kind="ExternalInput").ap())
    o = nc.dram_tensor("out_0_dram", (4, 128, 32, 32), _mybir.dt.float32, kind="ExternalOutput").ap()
    conv_attention_moe(nc, *args, o)
    r = _run(nc, [arrays], core_ids=[0])
    return r.results[0]["out_0_dram"]
```
